# Optimizing a Trainium2 kernel written in Bass

```python
import numpy as np
import jax
import jax.numpy as jnp

def _softmax(x, axis=-1):
    return jax.nn.softmax(x, axis=axis)

def _gelu(x):
    return jax.nn.gelu(x, approximate=True)

def _silu(x):
    return jax.nn.silu(x)

def _sigmoid(x):
    return jax.nn.sigmoid(x)

def _layernorm(x, axis=-1, eps=1e-05):
    m = jnp.mean(x, axis=axis, keepdims=True)
    v = jnp.var(x, axis=axis, keepdims=True)
    return (x - m) / jnp.sqrt(v + eps)

def _scatter_add(tgt, idx, src, axis=0):
    return tgt.at[idx].add(src)

def _segment_sum(src, seg, n):
    return jax.ops.segment_sum(src, seg, n)
kernel_name = 'mk_xattn_ffn_d2_seqx_r4_d12f69'

def setup_inputs(seed: int=0):
    np.random.seed(seed)
    _w = jnp.asarray

    def _rec_inputs():
        import jax
        import jax.numpy as jnp
        _rk = jax.random.key(seed)
        x = 0.000341 + 1 * jax.random.normal(jax.random.fold_in(_rk, 1), (8, 256, 512), jnp.float32)
        _lenS = 256 - jax.random.randint(jax.random.fold_in(_rk, 7), (8,), 0, max(1, 256 // 4) + 1, jnp.int32)
        _lenS2 = 256 - jax.random.randint(jax.random.fold_in(_rk, 8), (8,), 0, max(1, 256 // 4) + 1, jnp.int32)
        _ctx_2048P = jax.random.normal(jax.random.fold_in(_rk, 11), (8, 16, 512), jnp.float32)
        _ctx_2048c = jax.random.dirichlet(jax.random.fold_in(_rk, 511), 0.3 * jnp.ones((16,), jnp.float32), (8, 256))
        _ctx_2048t = jnp.einsum('bsk,bkd->bsd', _ctx_2048c, _ctx_2048P)
        _ctx_2048t = _ctx_2048t * jax.lax.rsqrt(jnp.mean(jnp.square(_ctx_2048t)) + 1e-12) * 0.953939
        ctx_2048 = -1.47943e-05 + 1.00017 * (_ctx_2048t + 0.3 * jax.random.normal(jax.random.fold_in(_rk, 611), (8, 256, 512), jnp.float32))
        return (x, ctx_2048)
    x, ctx_2048 = _rec_inputs()

    def _L0_xattn_setup():
        import jax, jax.numpy as jnp
        import numpy as np

        def _wkv(time_decay, time_first, k, v):
            w = -jnp.exp(time_decay)
            u = time_first
            B, T, C = k.shape
            aa = jnp.zeros((B, C), dtype=k.dtype)
            bb = jnp.zeros((B, C), dtype=k.dtype)
            pp = jnp.full((B, C), -1e+38, dtype=k.dtype)

            def step(carry, kv_t):
                aa, bb, pp = carry
                kt, vt = kv_t
                ww = u + kt
                q = jnp.maximum(pp, ww)
                e1 = jnp.exp(pp - q)
                e2 = jnp.exp(ww - q)
                y_t = (e1 * aa + e2 * vt) / (e1 * bb + e2)
                ww2 = pp + w
                q2 = jnp.maximum(ww2, kt)
                e1b = jnp.exp(ww2 - q2)
                e2b = jnp.exp(kt - q2)
                new_carry = (e1b * aa + e2b * vt, e1b * bb + e2b, q2)
                return (new_carry, y_t)
            ks = jnp.transpose(k, (1, 0, 2))
            vs = jnp.transpose(v, (1, 0, 2))
            _, ys = jax.lax.scan(step, (aa, bb, pp), (ks, vs))
            return jnp.transpose(ys, (1, 0, 2))
        key = jax.random.key(seed)
        k1, k2, k3, k4 = jax.random.split(key, 4)
        B, T, C = (8, 256, 512)
        return {'batch_size': B, 'seq_len': T, 'embedding_dim': C, 'time_decay': jax.random.normal(k1, (C,), dtype=jnp.float32), 'time_first': jax.random.normal(k2, (C,), dtype=jnp.float32), 'k': jax.random.normal(k3, (B, T, C), dtype=jnp.float32), 'v': jax.random.normal(k4, (B, T, C), dtype=jnp.float32)}
    _L0_xattn_all = _L0_xattn_setup()
    _L0_xattn_in = {k: v for k, v in _L0_xattn_all.items() if k in ('time_decay', 'time_first')}
    del _L0_xattn_all

    def _L0_ffn_setup():
        import jax, jax.numpy as jnp
        import numpy as np
        B, S, EMB = (4, 512, 512)
        LAT, HID = (128, 256)
        E, K = (16, 8)
        SCALE = 2.5

        def _w(key, shape, fan_in):
            return jax.random.normal(key, shape, jnp.float32) * fan_in ** (-0.5)

        def _sqrelu(x):
            return jnp.square(jax.nn.relu(x))
        key = jax.random.key(seed)
        ks = jax.random.split(key, 11)
        return {'x': jax.random.normal(ks[0], (B, S, EMB), jnp.float32), 'sw1': _w(ks[1], (HID, EMB), EMB), 'swg': _w(ks[2], (HID, EMB), EMB), 'sw2': _w(ks[3], (EMB, HID), HID), 'rw1': _w(ks[4], (E, HID, LAT), LAT), 'rwg': _w(ks[5], (E, HID, LAT), LAT), 'rw2': _w(ks[6], (E, LAT, HID), HID), 'Wg': _w(ks[7], (E, EMB), EMB), 'Wdown': _w(ks[8], (LAT, EMB), EMB), 'Wup': _w(ks[9], (EMB, LAT), LAT), 'biases': jnp.zeros((E,), jnp.float32)}
    _L0_ffn_all = _L0_ffn_setup()
    _L0_ffn_in = {k: v for k, v in _L0_ffn_all.items() if k in ('sw1', 'swg', 'sw2', 'rw1', 'rwg', 'rw2', 'Wg', 'Wdown', 'Wup', 'biases')}
    del _L0_ffn_all

    def _L1_xattn_setup():
        import jax, jax.numpy as jnp
        import numpy as np
        B, S, DIM, HD = (4, 256, 512, 128)
        H = DIM // HD
        GN_EPS = 0.001

        def _decay_masks(n_heads, seq_len):
            gam = 1.0 - 2.0 ** (-5.0 - jnp.arange(n_heads, dtype=jnp.float32))
            idx = jnp.arange(seq_len, dtype=jnp.float32)
            expo = idx[None, :] - idx[:, None]
            D = jnp.where(expo[None, :, :] <= 0, gam[:, None, None] ** expo[None, :, :], 0.0)
            return D / jnp.sqrt(D.sum(axis=-1))[:, None, :]
        key = jax.random.key(seed)
        ks = jax.random.split(key, 8)
        x = jax.random.normal(ks[0], (B, S, DIM), dtype=jnp.float32)
        k = jax.random.normal(ks[1], (B, S, DIM), dtype=jnp.float32)
        v = jax.random.normal(ks[2], (B, S, DIM), dtype=jnp.float32)
        Wh = jax.random.normal(ks[3], (H, HD, HD), dtype=jnp.float32) / np.sqrt(HD)
        wg_w = jax.random.normal(ks[4], (DIM, DIM), dtype=jnp.float32) / np.sqrt(DIM)
        wo_w = jax.random.normal(ks[5], (DIM, DIM), dtype=jnp.float32) / np.sqrt(DIM)
        gn_gamma = jnp.ones((DIM,), dtype=jnp.float32)
        gn_beta = jnp.zeros((DIM,), dtype=jnp.float32)
        return {'x': x, 'k': k, 'v': v, 'Wh': Wh, 'wg_w': wg_w, 'wo_w': wo_w, 'gn_gamma': gn_gamma, 'gn_beta': gn_beta}
    _L1_xattn_all = _L1_xattn_setup()
    _L1_xattn_in = {k: v for k, v in _L1_xattn_all.items() if k in ('Wh', 'wg_w', 'wo_w', 'gn_gamma', 'gn_beta')}
    del _L1_xattn_all

    def _L1_ffn_setup():
        import jax, jax.numpy as jnp
        import numpy as np
        K_TOP = 2
        key = jax.random.key(seed)
        ks = jax.random.split(key, 6)
        s = 0.02
        B, S, H, D = (4, 256, 512, 256)
        E_SH, E_RT = (2, 16)
        return {'x': jax.random.normal(ks[0], (B, S, H), dtype=jnp.float32), 'Wsh_up': jax.random.normal(ks[1], (E_SH, H, D), dtype=jnp.float32) * s, 'Wsh_down': jax.random.normal(ks[2], (E_SH, D, H), dtype=jnp.float32) * s, 'Wrt_up': jax.random.normal(ks[3], (E_RT, H, D), dtype=jnp.float32) * s, 'Wrt_down': jax.random.normal(ks[4], (E_RT, D, H), dtype=jnp.float32) * s, 'W_router': jax.random.normal(ks[5], (H, E_RT), dtype=jnp.float32) * s}
    _L1_ffn_all = _L1_ffn_setup()
    _L1_ffn_in = {k: v for k, v in _L1_ffn_all.items() if k in ('Wsh_up', 'Wsh_down', 'Wrt_up', 'Wrt_down', 'W_router')}
    del _L1_ffn_all
    return {'x': x, 'ctx_2048': ctx_2048, 'L0_xattn_time_decay': _L0_xattn_in['time_decay'], 'L0_xattn_time_first': _L0_xattn_in['time_first'], 'L0_ffn_sw1': _L0_ffn_in['sw1'], 'L0_ffn_swg': _L0_ffn_in['swg'], 'L0_ffn_sw2': _L0_ffn_in['sw2'], 'L0_ffn_rw1': _L0_ffn_in['rw1'], 'L0_ffn_rwg': _L0_ffn_in['rwg'], 'L0_ffn_rw2': _L0_ffn_in['rw2'], 'L0_ffn_Wg': _L0_ffn_in['Wg'], 'L0_ffn_Wdown': _L0_ffn_in['Wdown'], 'L0_ffn_Wup': _L0_ffn_in['Wup'], 'L0_ffn_biases': _L0_ffn_in['biases'], 'L1_xattn_Wh': _L1_xattn_in['Wh'], 'L1_xattn_wg_w': _L1_xattn_in['wg_w'], 'L1_xattn_wo_w': _L1_xattn_in['wo_w'], 'L1_xattn_gn_gamma': _L1_xattn_in['gn_gamma'], 'L1_xattn_gn_beta': _L1_xattn_in['gn_beta'], 'L1_ffn_Wsh_up': _L1_ffn_in['Wsh_up'], 'L1_ffn_Wsh_down': _L1_ffn_in['Wsh_down'], 'L1_ffn_Wrt_up': _L1_ffn_in['Wrt_up'], 'L1_ffn_Wrt_down': _L1_ffn_in['Wrt_down'], 'L1_ffn_W_router': _L1_ffn_in['W_router']}

def reference(x, ctx_2048, L0_xattn_time_decay, L0_xattn_time_first, L0_ffn_sw1, L0_ffn_swg, L0_ffn_sw2, L0_ffn_rw1, L0_ffn_rwg, L0_ffn_rw2, L0_ffn_Wg, L0_ffn_Wdown, L0_ffn_Wup, L0_ffn_biases, L1_xattn_Wh, L1_xattn_wg_w, L1_xattn_wo_w, L1_xattn_gn_gamma, L1_xattn_gn_beta, L1_ffn_Wsh_up, L1_ffn_Wsh_down, L1_ffn_Wrt_up, L1_ffn_Wrt_down, L1_ffn_W_router):
    import jax
    import jax.numpy as jnp

    def _L0_xattn_ref(batch_size, seq_len, embedding_dim, time_decay, time_first, k, v):
        import jax, jax.numpy as jnp
        import numpy as np

        def _wkv(time_decay, time_first, k, v):
            w = -jnp.exp(time_decay)
            u = time_first
            B, T, C = k.shape
            aa = jnp.zeros((B, C), dtype=k.dtype)
            bb = jnp.zeros((B, C), dtype=k.dtype)
            pp = jnp.full((B, C), -1e+38, dtype=k.dtype)

            def step(carry, kv_t):
                aa, bb, pp = carry
                kt, vt = kv_t
                ww = u + kt
                q = jnp.maximum(pp, ww)
                e1 = jnp.exp(pp - q)
                e2 = jnp.exp(ww - q)
                y_t = (e1 * aa + e2 * vt) / (e1 * bb + e2)
                ww2 = pp + w
                q2 = jnp.maximum(ww2, kt)
                e1b = jnp.exp(ww2 - q2)
                e2b = jnp.exp(kt - q2)
                new_carry = (e1b * aa + e2b * vt, e1b * bb + e2b, q2)
                return (new_carry, y_t)
            ks = jnp.transpose(k, (1, 0, 2))
            vs = jnp.transpose(v, (1, 0, 2))
            _, ys = jax.lax.scan(step, (aa, bb, pp), (ks, vs))
            return jnp.transpose(ys, (1, 0, 2))
        assert seq_len <= 256
        return _wkv(time_decay, time_first, k, v)

    def _L0_ffn_ref(x, sw1, swg, sw2, rw1, rwg, rw2, Wg, Wdown, Wup, biases):
        import jax, jax.numpy as jnp
        import numpy as np
        B, S, EMB = (4, 512, 512)
        LAT, HID = (128, 256)
        E, K = (16, 8)
        SCALE = 2.5

        def _w(key, shape, fan_in):
            return jax.random.normal(key, shape, jnp.float32) * fan_in ** (-0.5)

        def _sqrelu(x):
            return jnp.square(jax.nn.relu(x))
        b, s, d = x.shape
        x2 = x.reshape(-1, d)
        shared = x2 @ sw1.T * _sqrelu(x2 @ swg.T) @ sw2.T
        xl = x2 @ Wdown.T
        probas = jax.nn.sigmoid(x2 @ Wg.T)
        _, idx = jax.lax.top_k(probas + biases, K)
        p = jnp.take_along_axis(probas, idx, axis=-1)
        p = p / p.sum(-1, keepdims=True) * SCALE
        T = x2.shape[0]
        w_dense = jnp.zeros((T, E), x2.dtype).at[jnp.arange(T)[:, None], idx].add(p)
        acc = jnp.zeros_like(xl)
        for e in range(E):
            ye = xl @ rw1[e].T * _sqrelu(xl @ rwg[e].T) @ rw2[e].T
            acc = acc + w_dense[:, e:e + 1] * ye
        out = shared + acc @ Wup.T
        return out.reshape(b, s, d)

    def _L1_xattn_ref(x, k, v, Wh, wg_w, wo_w, gn_gamma, gn_beta):
        import jax, jax.numpy as jnp
        import numpy as np
        B, S, DIM, HD = (4, 256, 512, 128)
        H = DIM // HD
        GN_EPS = 0.001

        def _decay_masks(n_heads, seq_len):
            gam = 1.0 - 2.0 ** (-5.0 - jnp.arange(n_heads, dtype=jnp.float32))
            idx = jnp.arange(seq_len, dtype=jnp.float32)
            expo = idx[None, :] - idx[:, None]
            D = jnp.where(expo[None, :, :] <= 0, gam[:, None, None] ** expo[None, :, :], 0.0)
            return D / jnp.sqrt(D.sum(axis=-1))[:, None, :]
        b, s, dim = x.shape
        h, hd, _ = Wh.shape
        xh = x.reshape(b, s, h, hd)
        kh = k.reshape(b, s, h, hd)
        vh = v.reshape(b, s, h, hd)
        Q = jnp.einsum('bshd,hde->bshe', xh, Wh)
        K = jnp.einsum('bshd,hde->bshe', kh, Wh)
        V = jnp.einsum('bshd,hde->bshe', vh, Wh)
        scores = jnp.einsum('bshe,bthe->bhst', Q, K) / jnp.sqrt(jnp.float32(hd))
        Dn = _decay_masks(h, s)
        masked = scores * Dn[None, :, :, :]
        A = jnp.maximum(jnp.abs(masked.sum(axis=0)), 1.0)
        O = jnp.einsum('hst,bthe->bshe', A, V).reshape(b, s, dim)
        mu = O.mean(axis=-1, keepdims=True)
        var = O.var(axis=-1, keepdims=True)
        Y = (O - mu) / jnp.sqrt(var + GN_EPS) * gn_gamma + gn_beta
        W = jax.nn.relu(x @ wg_w)
        return W * Y @ wo_w

    def _L1_ffn_ref(x, Wsh_up, Wsh_down, Wrt_up, Wrt_down, W_router):
        import jax, jax.numpy as jnp
        import numpy as np
        K_TOP = 2
        B, S, H = x.shape
        E_rt = Wrt_up.shape[0]
        xt = x.reshape(B * S, H)
        sh_mid = jax.nn.gelu(jnp.einsum('th,ehd->ted', xt, Wsh_up), approximate=False)
        shared_out = jnp.einsum('ted,edh->th', sh_mid, Wsh_down)
        probs = jax.nn.softmax(xt @ W_router, axis=-1)
        top_v, top_i = jax.lax.top_k(probs, K_TOP)
        gate = jnp.sum(jax.nn.one_hot(top_i, E_rt, dtype=xt.dtype) * top_v[..., None], axis=1)
        rt_mid = jax.nn.gelu(jnp.einsum('th,ehd->ted', xt, Wrt_up), approximate=False)
        routed_out = jnp.einsum('ted,edh->th', rt_mid * gate[:, :, None], Wrt_down)
        return (shared_out + routed_out).reshape(B, S, H)
    x = x + _L0_xattn_ref(8, 256, 512, L0_xattn_time_decay, L0_xattn_time_first, _layernorm(x, axis=-1), ctx_2048)
    x = x + _L0_ffn_ref(_layernorm(x, axis=-1), L0_ffn_sw1, L0_ffn_swg, L0_ffn_sw2, L0_ffn_rw1, L0_ffn_rwg, L0_ffn_rw2, L0_ffn_Wg, L0_ffn_Wdown, L0_ffn_Wup, L0_ffn_biases)
    x = x + _L1_xattn_ref(_layernorm(x, axis=-1), ctx_2048, ctx_2048, L1_xattn_Wh, L1_xattn_wg_w, L1_xattn_wo_w, L1_xattn_gn_gamma, L1_xattn_gn_beta)
    x = x + _L1_ffn_ref(_layernorm(x, axis=-1), L1_ffn_Wsh_up, L1_ffn_Wsh_down, L1_ffn_Wrt_up, L1_ffn_Wrt_down, L1_ffn_W_router)
    return x

_drawn_inputs = setup_inputs


def setup_inputs(seed=0):
    import zlib

    import numpy as np

    out = dict(_drawn_inputs(seed))
    spreads = {'L0_ffn_biases': (0.0, 0.1),
     'L1_xattn_gn_gamma': (1.0, 0.2),
     'L1_xattn_gn_beta': (0.0, 0.1)}
    factors = {'L1_ffn_Wrt_up': 8.0,
     'L1_ffn_Wrt_down': 8.0,
     'L1_ffn_W_router': 8.0,
     'L1_ffn_Wsh_up': 2.692}
    for name, (base, spread) in spreads.items():
        noise = np.random.default_rng([zlib.crc32(name.encode()), seed]).standard_normal(out[name].shape)
        drawn = base * np.exp(spread * noise) if base else spread * noise
        out[name] = jnp.asarray(drawn.astype(out[name].dtype))
    for name, factor in factors.items():
        out[name] = (out[name] * factor).astype(out[name].dtype)
    return out
```

```python
from contextlib import ExitStack

import concourse.bass as bass
from concourse import mybir

F32 = mybir.dt.float32
F32R = mybir.dt.float32r
BF16 = mybir.dt.bfloat16
I32 = mybir.dt.int32
U32 = mybir.dt.uint32
ALU = mybir.AluOpType
ACT = mybir.ActivationFunctionType
AX_X = mybir.AxisListType.X

P = 128
B, S, D = 8, 256, 512
T = B * S
NT = T // P
GT = 4
GW = GT * P
NG = NT // GT
KD = D // P
LAT, HID, E0 = 128, 256, 16
TOP0 = 8
SCALE0 = 2.5
HJ = HID // P
E1 = 16
SLOTS = 2 * NT + E1 - 1
LN_EPS = 1e-5
NEVER = -1e38


class Ticks:

    def __init__(self, sem, base=0):
        self.sem, self.base, self.n = sem, base, 0

    def tick(self, ins):
        ins.then_inc(self.sem, 1)
        self.n += 1
        return self.base + self.n


def product(pe, out, w, x, first=True, last=True):
    pe.matmul(out, w[0], x[0], start=first, stop=False)
    pe.matmul(out, w[0], x[1], start=False, stop=False)
    return pe.matmul(out, w[1], x[0], start=False, stop=last)


def whole(ap):
    return ap.bitcast(F32)


class Memory:

    def __init__(self, nc, ctx):
        self.nc, self.ctx, self.sems = nc, ctx, []

    def sb(self, name, shape, dtype=F32):
        return self.ctx.enter_context(self.nc.sbuf_tensor(name, shape, dtype))

    def pair(self, name, shape):
        return self.sb(name + "_hi", shape, F32R), self.sb(name + "_lo", shape, F32R)

    def bank(self, name, dtype=F32):
        return self.ctx.enter_context(self.nc.psum_tensor(name, [P, 512], dtype))

    def sem(self, name):
        self.sems.append(self.ctx.enter_context(self.nc.semaphore(name)))
        return self.sems[-1]


def wait_count(eng, sem, count):
    if not isinstance(count, int) or count > 0:
        eng.wait_ge(sem, count)


def wait_alone(eng, sem, count, passed):
    if not isinstance(count, int) or count > 0:
        eng.wait_ge(sem, count)
        if not isinstance(count, int):
            eng.sem_inc(passed, 1)


def starts(n):
    return isinstance(n, int) and n == 0


def skewed(eng, first_part, second_part):
    first_part(0)
    first_part(1)
    second_part(0)
    with eng.Fori(2, NG) as g:
        first_part(g)
        second_part(g - 1)
    second_part(NG - 1)


def mix_stage(nc, kept, io):
    C_DOWN, C_SGATE, C_SUP, C_ROUTE = 0, LAT, LAT + HID, LAT + 2 * HID
    C_ALL = C_ROUTE + P
    LOGIT, LOGIT_T, LATENT, HIDDEN, ROWS, GATE_T = 0, 1, 2, 3, 7, 11
    FILLS = 12
    ACT_READS = [LOGIT, LOGIT_T, LATENT, HIDDEN, HIDDEN + 2, GATE_T]
    DVE_READS = [HIDDEN + 1, HIDDEN + 3, ROWS, ROWS + 1, ROWS + 2, ROWS + 3]
    DVE_MIX, DVE_MOE = 64, 18

    with ExitStack() as ctx:
        mem = Memory(nc, ctx)
        sb, sem = mem.sb, mem.sem
        front = mem.pair("w_front", [P, KD, C_ALL])
        raw = sb("w_raw", [P, 2, C_ROUTE + E0])
        shared_down = mem.pair("w_shared_down", [P, HJ, D])
        bias = sb("gate_bias", [P, E0])
        small = sb("time_decay_and_first", [P, 2, KD])
        exp_decay = sb("exp_decay", [P, KD])
        decay = sb("decay", [P, KD])
        minus_half = sb("minus_half", [P, GT])
        ctx_t = sb("ctx_t", [P, 2, KD, GW])
        stats = sb("stats", [P, GT, 6])
        meanvar = sb("meanvar", [P, GT, 2])
        vareps = sb("vareps", [P, GT])
        rstd = sb("rstd", [P, GT])
        xn = sb("xn", [P, 2, D])
        key = sb("key", [P, KD, GW])
        xnt = mem.pair("xnt", [P, 2, KD, GW])
        top = sb("wkv_top", [P, 2, S + 1])
        num_state = sb("wkv_num_state", [P, 2, S + 1])
        den_state = sb("wkv_den_state", [P, 2, S + 1])
        gap = sb("wkv_gap", [P, GW])
        weight = sb("wkv_weight", [P, 2, 4, GW])
        v_in = sb("wkv_v_in", [P, 2, GW])
        v_now = sb("wkv_v_now", [P, 2, GW])
        den = sb("wkv_den", [P, 2, GW])
        num = sb("wkv_num", [P, 2, GW])
        guess = sb("wkv_guess", [P, 2, GW])
        miss = sb("wkv_miss", [P, GW])
        logit_t = sb("logit_t", [E0, GW])
        minus_exp = sb("exp_minus_logit", [P, GT, E0])
        prob = sb("prob", [P, GT, E0])
        biased = sb("biased", [P, GT, E0])
        cut = sb("cut", [P, GT, E0])
        top8 = sb("top8", [P, GT, TOP0])
        prob_sum = sb("prob_sum", [P, GT])
        gate = sb("gate", [P, GT, E0])
        gate_t = sb("gate_t", [E0, GW])
        relu = sb("shared_relu", [P, GW])
        relu2 = sb("shared_relu2", [P, HJ, GW])
        hid = sb("shared_hid", [P, GW])
        hidp = mem.pair("shared_hidp", [P, HJ, GW])
        turn_bank = [mem.bank(f"turn{i}") for i in range(2)]
        y_bank = [mem.bank(f"y{i}") for i in range(2)]
        out_bank = [mem.bank(f"out{i}") for i in range(4)]

        x_loaded, ctx_loaded = sem("x_loaded"), sem("ctx_loaded")
        small_loaded, w_loaded = sem("small_loaded"), [sem("w_loaded_even"), sem("w_loaded_odd")]
        w_hi_ready, w_lo_ready = sem("w_hi_ready"), sem("w_lo_ready")
        set_dve, set_pool = sem("set_by_dve"), sem("set_by_pool")
        decay_exp = sem("decay_exp")
        meanvar_ready, rstd_ready, vareps_ready = sem("meanvar_ready"), sem("rstd_ready"), sem("vareps_ready")
        normed, turned = sem("normed"), sem("turned")
        key_ready = sem("key_ready")
        expo_ready, weight_ready, v_ready = sem("expo_ready"), sem("weight_ready"), sem("v_ready")
        den_ready, num_ready = sem("den_ready"), sem("num_ready")
        log_ready, guess_ready = sem("log_ready"), sem("guess_ready")
        y_ready, y_turned, y_added = sem("y_ready"), sem("y_turned"), sem("y_added")
        hi_ready, lo_ready = sem("xnt_hi_ready"), sem("xnt_lo_ready")
        filled, read_act, read_dve = sem("filled"), sem("read_by_act"), sem("read_by_dve")
        relu2_ready, hidden_ready = sem("relu2_ready"), sem("hidden_ready")
        gate_ready, gate_stored = sem("gate_ready"), sem("gate_stored")
        dve_mix, dve_moe = sem("dve_mix_steps"), sem("dve_moe_steps")
        block = ctx.enter_context(nc.Block())

        def act_read(g, fill):
            return g * len(ACT_READS) + ACT_READS.index(fill) + 1

        def dve_read(g, fill):
            return g * len(DVE_READS) + DVE_READS.index(fill) + 1

        weight_parts = [(front[0][:, k, 0:C_ROUTE + E0], front[1][:, k, 0:C_ROUTE + E0], C_ROUTE + E0) for k in range(KD)]
        weight_parts += [(shared_down[0][:, j, :], shared_down[1][:, j, :], D) for j in range(HJ)]

        def load_weights(eng, n):
            src = io["w_front"][n * P:(n + 1) * P, :] if n < KD else io["sw2_t"][(n - KD) * P:(n - KD + 1) * P, :]
            eng.dma_start(raw[:, n % 2, 0:weight_parts[n][2]], src).then_inc(w_loaded[n % 2], 16)

        def by_chunk(ap):
            return ap.rearrange("p (c t) -> p c t", c=KD)

        def by_batch(ap):
            return ap.rearrange("p (b t) -> p b t", b=2)

        @block.sync
        def _(sp):
            x_in = io["x"].rearrange("(n p) d -> p n d", p=P)
            ctx_in = io["ctx_t"].rearrange("(c p) t -> p c t", p=P)
            for g in range(NG):
                sp.dma_start(kept.x[:, g * GT:(g + 1) * GT, :], x_in[:, g * GT:(g + 1) * GT, :]
                             ).then_inc(x_loaded, 16)
                if g == 0:
                    sp.wait_ge(x_loaded, 16)
                    for slot in range(2):
                        sp.dma_start(ctx_t[:, slot], ctx_in[:, :, slot * GW:(slot + 1) * GW]
                                     ).then_inc(ctx_loaded, 16)
                        sp.wait_ge(ctx_loaded, 16 * slot + 16)
                sp.wait_ge(x_loaded, 16 * g + 16)
            with sp.Fori(2, NG) as g:
                sp.wait_ge(v_ready, g * KD - KD)
                sp.dma_start(ctx_t[:, g % 2], ctx_in[:, :, bass.ds(g * GW, GW)]).then_inc(ctx_loaded, 16)
                sp.wait_ge(ctx_loaded, g * 16 + 16)
                sp.wait_ge(read_act, (g - 2) * len(ACT_READS) + len(ACT_READS))
                sp.dma_start(kept.gate_dram[:, bass.ds((g - 2) * GW, GW)], gate_t[:, :]).then_inc(gate_stored, 16)
            with sp.Fori(NG - 2, NG) as g:
                sp.wait_ge(read_act, g * len(ACT_READS) + len(ACT_READS))
                sp.dma_start(kept.gate_dram[:, bass.ds(g * GW, GW)], gate_t[:, :]).then_inc(gate_stored, 16)
            sp.wait_ge(gate_stored, 16 * NG)

        @block.gpsimd
        def _(pool):
            pool.memset(kept.ones[:, :], 1.0).then_inc(set_pool, 1)
            pool.memset(minus_half[:, :], -0.5).then_inc(set_pool, 1)
            pool.wait_ge(set_pool, 1)
            pool.affine_select(out=kept.ident[:, :], in_=kept.ones[:, :], pattern=[[-1, P]],
                               compare_op=ALU.is_equal, fill=0.0, base=0,
                               channel_multiplier=1).then_inc(set_pool, 1)
            pool.wait_ge(set_pool, 3)

            def rstds(g, norm):
                n = 2 * g + norm
                wait_alone(pool, meanvar_ready, n * GT + GT, kept.passed)
                pool.tensor_scalar(vareps[:, :], meanvar[:, :, 1], LN_EPS, None, ALU.add).then_inc(vareps_ready, 1)
                pool.wait_ge(vareps_ready, n + 1)
                wait_count(pool, normed, n * GT)
                pool.tensor_tensor(rstd[:, :], vareps[:, :], minus_half[:, :], ALU.pow).then_inc(rstd_ready, 1)

            def mix(g):
                rstds(g, 0)
                pool.wait_ge(ctx_loaded, g * 16 + 16)
                for c in range(KD):
                    k = g * KD + c
                    pool.wait_ge(weight_ready, k + 1)
                    wait_count(pool, num_ready, k - 1)
                    pool.tensor_tensor(v_in[:, c % 2], weight[:, c % 2, 1], ctx_t[:, g % 2, c], ALU.mult)
                    pool.tensor_tensor(v_now[:, c % 2], weight[:, c % 2, 3], ctx_t[:, g % 2, c],
                                       ALU.mult).then_inc(v_ready, 1)
                rstds(g, 1)

            def split_weights():
                for n, (hi, lo, part) in enumerate(weight_parts):
                    pool.wait_ge(w_hi_ready, n + 1)
                    pool.tensor_tensor(lo, raw[:, n % 2, 0:part], whole(hi), ALU.subtract).then_inc(w_lo_ready, 1)

            split_weights()
            mix(0)
            with pool.Fori(1, NG) as g:
                mix(g)

        @block.scalar
        def _(act):
            act.dma_start(small[:, :, :], io["decay_first"]).then_inc(small_loaded, 16)
            act.dma_start(bias[:, :], io["bias"].to_broadcast([P, E0])).then_inc(small_loaded, 16)
            load_weights(act, 0)
            load_weights(act, 1)
            act.preload_act_table_set("natural_log_exp_and_others")
            act.wait_ge(small_loaded, 32)
            act.activation(exp_decay[:, :], small[:, 0, :], ACT.Exp).then_inc(decay_exp, 1)

            def split_weights():
                for n, (hi, _, part) in enumerate(weight_parts):
                    act.wait_ge(w_loaded[n % 2], 16 * (n // 2) + 16)
                    act.activation(hi, raw[:, n % 2, 0:part], ACT.Copy).then_inc(w_hi_ready, 1)
                    if n + 2 < len(weight_parts):
                        act.wait_ge(w_lo_ready, n + 1)
                        load_weights(act, n + 2)

            def mix(g):
                k = g * KD
                for i in range(GT):
                    act.wait_ge(turned, 2 * g * GT + i + 1)
                    act.activation(key[:, :, i * P:(i + 1) * P], by_chunk(turn_bank[i % 2][:, :]),
                                   ACT.Copy).then_inc(key_ready, 1)

                def weights(c):
                    act.wait_ge(expo_ready, k + c + 1)
                    act.activation(weight[:, c % 2], weight[:, c % 2], ACT.Exp).then_inc(weight_ready, 1)

                def guesses(c):
                    act.wait_ge(den_ready, k + c + 1)
                    wait_count(act, y_ready, k + c - 1)
                    act.activation(guess[:, c % 2], den[:, c % 2], ACT.Ln).then_inc(log_ready, 1)
                    act.wait_ge(log_ready, k + c + 1)
                    act.activation(guess[:, c % 2], guess[:, c % 2], ACT.Exp, scale=-1.0).then_inc(guess_ready, 1)

                weights(0)
                weights(1)
                guesses(0)
                weights(2)
                guesses(1)
                weights(3)
                guesses(2)
                guesses(3)
                for i in range(GT):
                    act.wait_ge(turned, 2 * g * GT + GT + i + 1)
                    act.activation(xnt[0][:, g % 2, :, i * P:(i + 1) * P], by_chunk(turn_bank[i % 2][:, :]),
                                   ACT.Copy).then_inc(hi_ready, 1)

            def moe(g):
                f = g * FILLS
                act.wait_ge(filled, f + LOGIT + 1)
                act.activation(logit_t[:, :], out_bank[0][0:E0, :], ACT.Copy).then_inc(read_act, 1)
                act.wait_ge(filled, f + LOGIT_T + 1)
                act.activation(minus_exp[:, :, :].rearrange("p i e -> p (i e)"), out_bank[1][:, 0:GT * E0],
                               ACT.Exp, scale=-1.0).then_inc(read_act, 1)
                act.wait_ge(filled, f + LATENT + 1)
                act.activation(kept.latent[:, bass.ds(g * GW, GW)], out_bank[2][:, :], ACT.Copy).then_inc(read_act, 1)
                for j in range(HJ):
                    act.wait_ge(filled, f + HIDDEN + 2 * j + 1)
                    wait_count(act, relu2_ready, g * HJ + j)
                    act.activation(relu[:, :], out_bank[(HIDDEN + 2 * j) % 4][:, :], ACT.Relu).then_inc(read_act, 1)
                    act.wait_ge(read_act, act_read(g, HIDDEN + 2 * j))
                    act.activation(relu2[:, j], relu[:, :], ACT.Square).then_inc(relu2_ready, 1)
                act.wait_ge(filled, f + GATE_T + 1)
                wait_count(act, gate_stored, g * 16)
                act.activation(gate_t[:, :], out_bank[3][0:E0, :], ACT.Copy).then_inc(read_act, 1)

            split_weights()
            skewed(act, mix, moe)

        @block.vector
        def _(dve):
            dve.memset(top[:, :, 0:1], NEVER)
            dve.memset(num_state[:, :, 0:1], 0.0)
            dve.memset(den_state[:, :, 0:1], 0.0)
            dve.memset(front[0][:, :, C_ROUTE + E0:C_ALL].bitcast(F32), 0.0)
            dve.memset(front[1][:, :, C_ROUTE + E0:C_ALL].bitcast(F32), 0.0).then_inc(set_dve, 1)
            dve.wait_ge(decay_exp, 1)
            dve.tensor_scalar(decay[:, :], exp_decay[:, :], -1.0, None, ALU.mult).then_inc(set_dve, 1)
            dve.wait_ge(set_dve, 2)

            def norm(g, which, step):
                for i in range(GT):
                    last = step.tick(dve.bn_stats(stats[:, i, :], kept.x[:, g * GT + i, :]))
                for i in range(GT):
                    wait_alone(dve, step.sem, last - GT + 1 + i, kept.passed)
                    dve.bn_aggr(meanvar[:, i, :], stats[:, i, :]).then_inc(meanvar_ready, 1)
                dve.wait_ge(rstd_ready, 2 * g + which + 1)
                for i in range(GT):
                    wait_count(dve, turned, (2 * g + which) * GT + i - 1)
                    dve.tensor_scalar(xn[:, i % 2, :], kept.x[:, g * GT + i, :], meanvar[:, i, 0:1],
                                      rstd[:, i:i + 1], ALU.subtract, ALU.mult).then_inc(normed, 1)

            def mix(g):
                step = Ticks(dve_mix, g * DVE_MIX)
                k = g * KD
                wait_alone(dve, x_loaded, g * 16 + 16, kept.passed)
                norm(g, 0, step)
                dve.wait_ge(key_ready, k + KD)

                def exponents(c):
                    slot, keys = c % 2, key[:, c, :]
                    before, after = top[:, :, 0:S], top[:, :, 1:S + 1]
                    for b in range(2):
                        scanned = step.tick(dve.tensor_tensor_scan(
                            top[:, b, 1:S + 1], decay[:, c:c + 1].to_broadcast([P, S]),
                            key[:, c, b * S:(b + 1) * S], NEVER, ALU.add, ALU.max))
                    dve.wait_ge(dve_mix, scanned)
                    wait_count(dve, num_ready, k + c - 1)
                    step.tick(dve.scalar_tensor_tensor(by_batch(weight[:, slot, 0]), before, decay[:, c:c + 1], after,
                                                       ALU.add, ALU.subtract))
                    step.tick(dve.tensor_tensor(by_batch(weight[:, slot, 1]), by_batch(keys), after, ALU.subtract))
                    gapped = step.tick(dve.scalar_tensor_tensor(by_batch(gap[:, :]), by_batch(keys), small[:, 1, c:c + 1],
                                                                before, ALU.add, ALU.subtract))
                    dve.wait_ge(dve_mix, gapped)
                    step.tick(dve.tensor_scalar(weight[:, slot, 2], gap[:, :], -1.0, 0.0, ALU.mult, ALU.min))
                    dve.tensor_scalar(weight[:, slot, 3], gap[:, :], 0.0, None, ALU.min).then_inc(expo_ready, 1)

                def states(c):
                    slot = c % 2
                    keep, old, now = weight[:, slot, 0], weight[:, slot, 2], weight[:, slot, 3]
                    dve.wait_ge(v_ready, k + c + 1)
                    for b in range(2):
                        part = slice(b * S, (b + 1) * S)
                        step.tick(dve.tensor_tensor_scan(den_state[:, b, 1:S + 1], keep[:, part],
                                                         weight[:, slot, 1, part], 0.0, ALU.mult, ALU.add))
                    for b in range(2):
                        part = slice(b * S, (b + 1) * S)
                        scanned = step.tick(dve.tensor_tensor_scan(num_state[:, b, 1:S + 1], keep[:, part],
                                                                   v_in[:, slot, part], 0.0, ALU.mult, ALU.add))
                    dve.wait_ge(dve_mix, scanned - 2)
                    wait_count(dve, log_ready, k + c - 1)
                    a = step.tick(dve.tensor_tensor(by_batch(den[:, slot]), by_batch(old), den_state[:, :, 0:S], ALU.mult))
                    dve.wait_ge(dve_mix, scanned)
                    wait_count(dve, y_turned, k + c - 1)
                    b = step.tick(dve.tensor_tensor(by_batch(num[:, slot]), by_batch(old), num_state[:, :, 0:S], ALU.mult))
                    dve.wait_ge(dve_mix, a)
                    dve.tensor_tensor(den[:, slot], den[:, slot], now, ALU.add).then_inc(den_ready, 1)
                    dve.wait_ge(dve_mix, b)
                    dve.tensor_tensor(num[:, slot], num[:, slot], v_now[:, slot], ALU.add).then_inc(num_ready, 1)

                def quotient(c):
                    slot = c % 2
                    dve.wait_ge(guess_ready, k + c + 1)
                    dve.wait_ge(num_ready, k + c + 1)
                    step.tick(dve.tensor_tensor(miss[:, :], den[:, slot], guess[:, slot], ALU.mult))
                    both = step.tick(dve.tensor_tensor(num[:, slot], num[:, slot], guess[:, slot], ALU.mult))
                    dve.wait_ge(dve_mix, both)
                    dve.scalar_tensor_tensor(num[:, slot], miss[:, :], 2.0, num[:, slot],
                                             ALU.subtract, ALU.mult).then_inc(y_ready, 1)

                def add(c):
                    dve.wait_ge(y_turned, k + c + 1)
                    part = kept.x[:, bass.ds(g * GT, GT), c * P:(c + 1) * P]
                    dve.tensor_tensor(part, part, y_bank[c % 2][:, :].rearrange("p (i d) -> p i d", i=GT),
                                      ALU.subtract).then_inc(y_added, 1)

                exponents(0)
                exponents(1)
                states(0)
                exponents(2)
                states(1)
                quotient(0)
                exponents(3)
                states(2)
                add(0)
                quotient(1)
                states(3)
                add(1)
                quotient(2)
                add(2)
                quotient(3)
                add(3)
                wait_alone(dve, y_added, k + KD, kept.passed)
                norm(g, 1, step)
                for i in range(GT):
                    dve.wait_ge(hi_ready, g * GT + i + 1)
                    part = slice(i * P, (i + 1) * P)
                    dve.tensor_tensor(xnt[1][:, g % 2, :, part], by_chunk(turn_bank[i % 2][:, :]),
                                      whole(xnt[0][:, g % 2, :, part]), ALU.subtract).then_inc(lo_ready, 1)
                assert step.n == DVE_MIX, step.n

            def moe(g):
                step = Ticks(dve_moe, g * DVE_MOE)

                def on(ins):
                    dve.wait_ge(dve_moe, step.tick(ins))

                dve.wait_ge(read_act, act_read(g, LOGIT_T))
                on(dve.tensor_scalar(minus_exp[:, :, :], minus_exp[:, :, :], 1.0, None, ALU.add))
                on(dve.reciprocal(prob[:, :, :], minus_exp[:, :, :]))
                wait_alone(dve, dve_moe, step.tick(dve.tensor_tensor(
                    biased[:, :, :], prob[:, :, :], bias[:, :].unsqueeze(1).to_broadcast([P, GT, E0]), ALU.add)), kept.passed)
                for i in range(GT):
                    last = step.tick(dve.max(top8[:, i], biased[:, i]))
                for i in range(GT):
                    wait_alone(dve, dve_moe, last - GT + 1 + i, kept.passed)
                    chosen = step.tick(dve.match_replace(cut[:, i], top8[:, i], biased[:, i], NEVER))
                dve.wait_ge(dve_moe, chosen)
                on(dve.tensor_tensor(cut[:, :, :], cut[:, :, :], biased[:, :, :], ALU.not_equal))
                on(dve.tensor_tensor(cut[:, :, :], cut[:, :, :], prob[:, :, :], ALU.mult))
                on(dve.tensor_reduce(prob_sum[:, :], cut[:, :, :], AX_X, ALU.add))
                on(dve.reciprocal(prob_sum[:, :], prob_sum[:, :]))
                on(dve.tensor_scalar(prob_sum[:, :], prob_sum[:, :], SCALE0, None, ALU.mult))
                dve.tensor_tensor(gate[:, :, :], cut[:, :, :], prob_sum[:, :].unsqueeze(2).to_broadcast([P, GT, E0]),
                                  ALU.mult).then_inc(gate_ready, 1)
                for j in range(HJ):
                    dve.wait_ge(relu2_ready, g * HJ + j + 1)
                    dve.wait_ge(filled, g * FILLS + HIDDEN + 2 * j + 2)
                    dve.tensor_tensor(hid[:, :], out_bank[(HIDDEN + 2 * j + 1) % 4][:, :], relu2[:, j],
                                      ALU.mult).then_inc(read_dve, 1)
                    dve.wait_ge(read_dve, dve_read(g, HIDDEN + 2 * j + 1))
                    on(dve.tensor_copy(hidp[0][:, j], hid[:, :]))
                    dve.tensor_tensor(hidp[1][:, j], hid[:, :], whole(hidp[0][:, j]), ALU.subtract).then_inc(hidden_ready, 1)
                    dve.wait_ge(hidden_ready, g * HJ + j + 1)
                for i in range(GT):
                    dve.wait_ge(filled, g * FILLS + ROWS + i + 1)
                    dve.tensor_tensor(kept.x[:, g * GT + i, :], kept.x[:, g * GT + i, :],
                                      out_bank[(ROWS + i) % 4][:, :], ALU.add).then_inc(read_dve, 1)
                assert step.n == DVE_MOE, step.n

            skewed(dve, mix, moe)

        @block.tensor
        def _(pe):
            pe.wait_ge(set_pool, 3)

            def mix(g):
                def turn(which):
                    for i in range(GT):
                        n = 2 * g * GT + which * GT + i
                        pe.wait_ge(normed, n + 1)
                        if which == 0 and i < 2:
                            wait_count(pe, lo_ready, g * GT - 1 + i)
                        elif which == 0:
                            pe.wait_ge(key_ready, g * GT + i - 1)
                        elif i < 2:
                            pe.wait_ge(key_ready, g * GT + i + 3)
                        else:
                            pe.wait_ge(lo_ready, g * GT + i - 1)
                        for c in range(KD):
                            done = pe.transpose(turn_bank[i % 2][:, c * P:(c + 1) * P], xn[:, i % 2, c * P:(c + 1) * P],
                                                kept.ident[:, :])
                        done.then_inc(turned, 1)

                turn(0)
                for c in range(KD):
                    pe.wait_ge(y_ready, g * KD + c + 1)
                    wait_count(pe, y_added, g * KD + c - 1)
                    for i in range(GT):
                        done = pe.transpose(y_bank[c % 2][:, i * P:(i + 1) * P], num[:, c % 2, i * P:(i + 1) * P],
                                            kept.ident[:, :])
                    done.then_inc(y_turned, 1)
                turn(1)

            def moe(g):
                slot = g % 2

                def from_norm(bank, col):
                    for k in range(KD):
                        done = product(pe, out_bank[bank][:, :],
                                       [w[:, k, col:col + P] for w in front], [x[:, slot, k, :] for x in xnt],
                                       first=(k == 0), last=(k == KD - 1))
                    done.then_inc(filled, 1)

                pe.wait_ge(w_lo_ready, KD)
                pe.wait_ge(lo_ready, g * GT + GT)
                wait_count(pe, read_dve, g * len(DVE_READS) - 2)
                from_norm(0, C_ROUTE)
                pe.wait_ge(read_act, act_read(g, LOGIT))
                wait_alone(pe, read_dve, g * len(DVE_READS) - 1, kept.passed)
                for i in range(GT):
                    done = pe.transpose(out_bank[1][:, i * E0:(i + 1) * E0], logit_t[:, i * P:(i + 1) * P],
                                        kept.ident[0:E0, 0:E0])
                done.then_inc(filled, 1)
                wait_count(pe, read_dve, g * len(DVE_READS))
                from_norm(2, C_DOWN)
                wait_count(pe, read_act, g * len(ACT_READS))
                from_norm(3, C_SGATE)
                from_norm(0, C_SUP)
                pe.wait_ge(read_act, act_read(g, LOGIT_T))
                from_norm(1, C_SGATE + P)
                pe.wait_ge(read_act, act_read(g, LATENT))
                from_norm(2, C_SUP + P)
                pe.wait_ge(w_lo_ready, KD + HJ)
                pe.wait_ge(hidden_ready, g * HJ + HJ)
                for i in range(GT):
                    if i == 0:
                        pe.wait_ge(read_act, act_read(g, HIDDEN))
                    if i == 1:
                        pe.wait_ge(read_dve, dve_read(g, HIDDEN + 1))
                    if i == 2:
                        pe.wait_ge(read_act, act_read(g, HIDDEN + 2))
                    if i == 3:
                        pe.wait_ge(read_dve, dve_read(g, HIDDEN + 3))
                    for j in range(HJ):
                        done = product(pe, out_bank[(ROWS + i) % 4][:, :],
                                       [h[:, j, i * P:(i + 1) * P] for h in hidp], [w[:, j, :] for w in shared_down],
                                       first=(j == 0), last=(j == HJ - 1))
                    done.then_inc(filled, 1)
                pe.wait_ge(gate_ready, g + 1)
                pe.wait_ge(read_dve, dve_read(g, ROWS))
                for i in range(GT):
                    done = pe.transpose(out_bank[3][0:E0, i * P:(i + 1) * P], gate[:, i, :], kept.ident[:, :])
                done.then_inc(filled, 1)

            skewed(pe, mix, moe)
    return mem.sems


def clear(nc, sems):
    with nc.Block() as block:
        @block.gpsimd
        def _(pool):
            for sem in sems:
                pool.sem_clear(sem)


def latent_moe_stage(nc, kept, io):
    HALVES = NG * HJ
    C_UP, C_GATE, C_DOWN = 0, HID, 2 * HID
    C_ALL = 2 * HID + HJ * LAT
    SPLIT_LAG, DOWN_LAG = 2, 4
    with ExitStack() as ctx:
        mem = Memory(nc, ctx)
        sb, sem = mem.sb, mem.sem
        latp = mem.pair("latent_p", [P, T])
        raw = sb("expert_raw", [P, 2, C_ALL])
        wp = [mem.pair(f"expert_w{i}", [P, C_ALL]) for i in range(2)]
        gates = sb("expert_gates", [P, 2, T])
        zeros = sb("expert_zeros", [P, GW], BF16)
        relu = sb("expert_relu", [P, 2, GW])
        relu2 = sb("expert_relu2", [P, 2, GW])
        prod = sb("expert_prod", [P, 2, GW])
        hid = sb("expert_hid", [P, 4, GW])
        hidp = mem.pair("expert_hidp", [P, 4, GW])
        acc = [mem.bank(f"acc{g}") for g in range(NG)]
        up_bank = [mem.bank(f"up{i}") for i in range(2)]
        gate_bank = [mem.bank(f"gate{i}") for i in range(2)]

        w_loaded = [sem("expert_w_even"), sem("expert_w_odd")]
        gates_loaded = [sem("expert_gates_even"), sem("expert_gates_odd")]
        acc_read = sem("acc_read")
        zeros_set, acc_opened = sem("zeros_set"), sem("acc_opened")
        lat_hi, lat_lo = sem("latent_hi"), sem("latent_lo")
        w_hi, w_lo = sem("expert_w_hi"), sem("expert_w_lo")
        gate_filled, up_filled, down_done = sem("gate_filled"), sem("up_filled"), sem("down_done")
        relu_done, relu2_ready = sem("relu_done"), sem("expert_relu2_ready")
        prod_ready, hid_ready, hid_hi, hid_lo = sem("prod_ready"), sem("hid_ready"), sem("hid_hi"), sem("hid_lo")
        block = ctx.enter_context(nc.Block())

        def load(eng, e, i):
            eng.dma_start(raw[:, i, :], io["experts"][bass.ds(e + i, 1)].rearrange("o p m -> (o p) m")
                          ).then_inc(w_loaded[i], 16)
            eng.dma_start(gates[:, i, :], kept.gate_dram[bass.ds(e + i, 1), :].to_broadcast([P, T])
                          ).then_inc(gates_loaded[i], 16)

        @block.sync
        def _(sp):
            load(sp, 0, 0)
            load(sp, 0, 1)
            with sp.Fori(1, E0 // 2) as pair:
                e = 2 * pair
                for i in range(2):
                    wait_alone(sp, w_lo, e + i - 1, kept.passed)
                    wait_alone(sp, hid_ready, (e + i - 1) * HALVES, kept.passed)
                    load(sp, e, i)

        @block.gpsimd
        def _(pool):
            pool.memset(zeros[:, :], 0.0).then_inc(zeros_set, 1)

            def pair_of_experts(e):
                for m in range(2 * HALVES):
                    n = e * HALVES + m
                    i, g = m // HALVES, m % HALVES // HJ
                    if m % HALVES == 0:
                        pool.wait_ge(gates_loaded[i], e * 8 + 16)
                    pool.wait_ge(prod_ready, n + 1)
                    wait_count(pool, hid_lo, n - 3)
                    pool.tensor_tensor(hid[:, m % 4], prod[:, m % 2], gates[:, i, g * GW:(g + 1) * GW],
                                       ALU.mult).then_inc(hid_ready, 1)

            pair_of_experts(0)
            with pool.Fori(1, E0 // 2) as pair:
                e = 2 * pair
                pair_of_experts(e)

        @block.scalar
        def _(act):
            for g in range(NG):
                part = slice(g * GW, (g + 1) * GW)
                act.activation(latp[0][:, part], kept.latent[:, part], ACT.Copy).then_inc(lat_hi, 1)

            def hi(n, m):
                act.wait_ge(hid_ready, n + 1)
                wait_count(act, down_done, n - 3)
                act.activation(hidp[0][:, m % 4], hid[:, m % 4], ACT.Copy).then_inc(hid_hi, 1)

            def pair_of_experts(e):
                for m in range(2 * HALVES):
                    n = e * HALVES + m
                    act.wait_ge(gate_filled, n + 1)
                    wait_count(act, relu2_ready, n - 1)
                    act.activation(relu[:, m % 2], gate_bank[m % 2][:, :], ACT.Relu).then_inc(relu_done, 1)
                    if m >= SPLIT_LAG or not starts(e):
                        hi(n - SPLIT_LAG, m - SPLIT_LAG)
                    act.wait_ge(relu_done, n + 1)
                    wait_count(act, prod_ready, n - 1)
                    act.activation(relu2[:, m % 2], relu[:, m % 2], ACT.Square).then_inc(relu2_ready, 1)

            pair_of_experts(0)
            with act.Fori(1, E0 // 2) as pair:
                e = 2 * pair
                pair_of_experts(e)
            for m in range(2 * HALVES - SPLIT_LAG, 2 * HALVES):
                hi((E0 - 2) * HALVES + m, m)
            act.wait_ge(down_done, E0 * HALVES)
            for g in range(NG):
                act.activation(kept.latent[:, g * GW:(g + 1) * GW], acc[g][:, :], ACT.Copy).then_inc(acc_read, 1)

        @block.vector
        def _(dve):
            for g in range(NG):
                part = slice(g * GW, (g + 1) * GW)
                dve.wait_ge(lat_hi, g + 1)
                dve.tensor_tensor(latp[1][:, part], kept.latent[:, part], whole(latp[0][:, part]),
                                  ALU.subtract).then_inc(lat_lo, 1)

            def split_weights(e, i):
                dve.wait_ge(w_loaded[i], (e - i) * 8 + 16)
                dve.tensor_copy(wp[i][0][:, :], raw[:, i]).then_inc(w_hi, 1)
                dve.wait_ge(w_hi, e + 1)
                dve.tensor_tensor(wp[i][1][:, :], raw[:, i], whole(wp[i][0][:, :]), ALU.subtract).then_inc(w_lo, 1)

            def lo(n, m):
                dve.wait_ge(hid_hi, n + 1)
                dve.tensor_tensor(hidp[1][:, m % 4], hid[:, m % 4], whole(hidp[0][:, m % 4]),
                                  ALU.subtract).then_inc(hid_lo, 1)

            def pair_of_experts(e, last=False):
                for m in range(2 * HALVES):
                    n = e * HALVES + m
                    dve.wait_ge(relu2_ready, n + 1)
                    dve.wait_ge(up_filled, n + 1)
                    wait_count(dve, hid_ready, n - 1)
                    dve.tensor_tensor(prod[:, m % 2], up_bank[m % 2][:, :], relu2[:, m % 2],
                                      ALU.mult).then_inc(prod_ready, 1)
                    if m >= SPLIT_LAG or not starts(e):
                        lo(n - SPLIT_LAG, m - SPLIT_LAG)
                    if m % HALVES == 6 and not (last and m > HALVES):
                        i = m // HALVES
                        wait_count(dve, down_done, (e + i) * HALVES)
                        split_weights(e + i + 1, (i + 1) % 2)

            split_weights(0, 0)
            pair_of_experts(0)
            with dve.Fori(1, E0 // 2 - 1) as pair:
                e = 2 * pair
                pair_of_experts(e)
            pair_of_experts(E0 - 2, last=True)
            for m in range(2 * HALVES - SPLIT_LAG, 2 * HALVES):
                lo((E0 - 2) * HALVES + m, m)

        @block.tensor
        def _(pe):
            pe.wait_ge(zeros_set, 1)
            for g in range(NG):
                done = pe.matmul(acc[g][:, :], zeros[:, 0:P], zeros[:, :], start=True, stop=True)
            done.then_inc(acc_opened, 1)
            pe.wait_ge(lat_lo, NG)

            def up(n, m):
                i, g, j = m // HALVES, m % HALVES // HJ, m % HJ
                x = [t[:, g * GW:(g + 1) * GW] for t in latp]
                wait_count(pe, prod_ready, n - 1)
                product(pe, gate_bank[m % 2][:, :], [w[:, C_GATE + j * P:C_GATE + (j + 1) * P] for w in wp[i]],
                        x).then_inc(gate_filled, 1)
                product(pe, up_bank[m % 2][:, :], [w[:, C_UP + j * P:C_UP + (j + 1) * P] for w in wp[i]],
                        x).then_inc(up_filled, 1)

            def down(n, m):
                m = m % (2 * HALVES)
                i, g, j = m // HALVES, m % HALVES // HJ, m % HJ
                w = [t[:, C_DOWN + j * LAT:C_DOWN + (j + 1) * LAT] for t in wp[i]]
                pe.wait_ge(hid_lo, n + 1)
                h = [t[:, m % 4] for t in hidp]
                for a, b in ((0, 0), (0, 1), (1, 0)):
                    done = pe.matmul(acc[g][:, :], w[a][:, :], h[b], start=False, stop=False, skip_group_check=True)
                done.then_inc(down_done, 1)

            def pair_of_experts(e):
                for m in range(2 * HALVES):
                    n = e * HALVES + m
                    if m % HALVES == 0:
                        pe.wait_ge(w_lo, e + m // HALVES + 1)
                    up(n, m)
                    if m >= DOWN_LAG or not starts(e):
                        down(n - DOWN_LAG, m - DOWN_LAG)

            pair_of_experts(0)
            with pe.Fori(1, E0 // 2) as pair:
                e = 2 * pair
                pair_of_experts(e)
            for m in range(2 * HALVES - DOWN_LAG, 2 * HALVES):
                down((E0 - 2) * HALVES + m, m)


class Split:

    def __init__(self, mem, name, parts):
        self.parts = parts
        self.raw = mem.sb(name + "_raw", [P, 2, max(p[3] for p in parts)])
        self.loaded = [mem.sem(name + "_loaded_even"), mem.sem(name + "_loaded_odd")]
        self.hi_ready, self.lo_ready = mem.sem(name + "_hi_ready"), mem.sem(name + "_lo_ready")

    def raw_part(self, n):
        _, hi, _, width = self.parts[n]
        flat = self.raw[:, n % 2, 0:width]
        return flat.rearrange("p (k e) -> p k e", k=hi.shape[1]) if len(hi.shape) == 3 else flat

    def load(self, eng, n):
        src, _, _, width = self.parts[n]
        out = self.raw_part(n) if len(src.shape) == 3 and len(self.parts[n][1].shape) == 3 else self.raw[:, n % 2, 0:width]
        eng.dma_start(out, src).then_inc(self.loaded[n % 2], 16)

    def on_scalar(self, act):
        for n in range(min(2, len(self.parts))):
            self.load(act, n)
        for n, (_, hi, _, width) in enumerate(self.parts):
            act.wait_ge(self.loaded[n % 2], 16 * (n // 2) + 16)
            act.activation(hi, self.raw_part(n), ACT.Copy).then_inc(self.hi_ready, 1)
            if n + 2 < len(self.parts):
                act.wait_ge(self.lo_ready, n + 1)
                self.load(act, n + 2)

    def on_pool(self, pool):
        for n, (_, hi, lo, width) in enumerate(self.parts):
            pool.wait_ge(self.hi_ready, n + 1)
            pool.tensor_tensor(lo, self.raw_part(n), whole(hi), ALU.subtract).then_inc(self.lo_ready, 1)


class Norm:

    def __init__(self, mem, name, eps, passed):
        self.eps, self.passed = eps, passed
        self.stats = mem.sb(name + "_stats", [P, GT, 6])
        self.meanvar = mem.sb(name + "_meanvar", [P, GT, 2])
        self.vareps = mem.sb(name + "_vareps", [P, GT])
        self.rstd = mem.sb(name + "_rstd", [P, GT])
        self.minus_half = mem.sb(name + "_minus_half", [P, GT])
        self.stats_ready, self.meanvar_ready = mem.sem(name + "_stats_ready"), mem.sem(name + "_meanvar_ready")
        self.half_set, self.vareps_ready = mem.sem(name + "_half_set"), mem.sem(name + "_vareps_ready")
        self.rstd_ready, self.normed = mem.sem(name + "_rstd_ready"), mem.sem(name + "_normed")

    def pool_start(self, pool):
        pool.memset(self.minus_half[:, :], -0.5).then_inc(self.half_set, 1)
        pool.wait_ge(self.half_set, 1)

    def on_pool(self, pool, n):
        wait_alone(pool, self.meanvar_ready, n * GT + GT, self.passed)
        pool.tensor_scalar(self.vareps[:, :], self.meanvar[:, :, 1], self.eps, None, ALU.add).then_inc(self.vareps_ready, 1)
        pool.wait_ge(self.vareps_ready, n + 1)
        wait_count(pool, self.normed, n * GT)
        pool.tensor_tensor(self.rstd[:, :], self.vareps[:, :], self.minus_half[:, :], ALU.pow).then_inc(self.rstd_ready, 1)

    def stats_on_vector(self, dve, n, i, row):
        dve.bn_stats(self.stats[:, i, :], row).then_inc(self.stats_ready, 1)

    def meanvar_on_vector(self, dve, n):
        for i in range(GT):
            wait_alone(dve, self.stats_ready, n * GT + i + 1, self.passed)
            dve.bn_aggr(self.meanvar[:, i, :], self.stats[:, i, :]).then_inc(self.meanvar_ready, 1)
        dve.wait_ge(self.rstd_ready, n + 1)

    def rows_on_vector(self, dve, i, row, out):
        dve.tensor_scalar(out, row, self.meanvar[:, i, 0:1], self.rstd[:, i:i + 1],
                          ALU.subtract, ALU.mult).then_inc(self.normed, 1)


def query_stage(nc, kept, io):
    FILLS = 2 * KD
    with ExitStack() as ctx:
        mem = Memory(nc, ctx)
        sb, sem = mem.sb, mem.sem
        w_up, w_head, w_gate = mem.pair("w_up0", [P, D]), mem.pair("w_head", [P, D]), mem.pair("w_ogate", [P, KD, D])
        split = Split(mem, "query_w",
                      [(io["wup_t"], w_up[0][:, :], w_up[1][:, :], D),
                       (io["heads"].rearrange("h p e -> p h e"), w_head[0][:, :], w_head[1][:, :], D)]
                      + [(io["wg"][k * P:(k + 1) * P, :], w_gate[0][:, k], w_gate[1][:, k], D) for k in range(KD)])
        norm = Norm(mem, "query_norm", LN_EPS, kept.passed)
        accp = mem.pair("accp", [P, GW])
        xn = sb("xn2", [P, 2, D])
        xnt = mem.pair("xn2t", [P, 2, KD, GW])
        row_bank = [mem.bank(f"row{i}") for i in range(2)]
        turn_bank = [mem.bank(f"turn2{i}") for i in range(2)]
        out_bank = [mem.bank(f"out2{i}") for i in range(4)]
        acc_hi, acc_lo = sem("accp_hi"), sem("accp_lo")
        row_filled, row_added = sem("row_filled"), sem("row_added")
        turned, hi_ready, lo_ready = sem("turned2"), sem("xn2t_hi"), sem("xn2t_lo")
        filled, read = sem("filled2"), sem("read2")
        block = ctx.enter_context(nc.Block())

        def by_chunk(ap):
            return ap.rearrange("p (c t) -> p c t", c=KD)

        @block.gpsimd
        def _(pool):
            norm.pool_start(pool)
            split.on_pool(pool)
            with pool.Fori(0, NG) as g:
                norm.on_pool(pool, g)

        @block.scalar
        def _(act):
            split.on_scalar(act)

            def rows(g):
                wait_count(act, row_filled, g * GT)
                act.activation(accp[0][:, :], kept.latent[:, bass.ds(g * GW, GW)], ACT.Copy).then_inc(acc_hi, 1)
                for i in range(GT):
                    act.wait_ge(turned, g * GT + i + 1)
                    act.activation(xnt[0][:, g % 2, :, i * P:(i + 1) * P], by_chunk(turn_bank[i % 2][:, :]),
                                   ACT.Copy).then_inc(hi_ready, 1)

            def outputs(g):
                part = bass.ds(g * GW, GW)
                for m in range(FILLS):
                    act.wait_ge(filled, g * FILLS + m + 1)
                    out = kept.queries[:, m, part] if m < KD else kept.ogate[:, m - KD, part]
                    act.activation(out, out_bank[m % 4][:, :], ACT.Copy if m < KD else ACT.Relu).then_inc(read, 1)

            skewed(act, rows, outputs)

        @block.vector
        def _(dve):
            def rows(g):
                dve.wait_ge(acc_hi, g + 1)
                dve.tensor_tensor(accp[1][:, :], kept.latent[:, bass.ds(g * GW, GW)], whole(accp[0][:, :]),
                                  ALU.subtract).then_inc(acc_lo, 1)
                for i in range(GT):
                    row = kept.x[:, g * GT + i, :]
                    dve.wait_ge(row_filled, g * GT + i + 1)
                    dve.tensor_tensor(row, row, row_bank[i % 2][:, :], ALU.add).then_inc(row_added, 1)
                    if i > 0:
                        wait_alone(dve, row_added, g * GT + i, kept.passed)
                        norm.stats_on_vector(dve, g, i - 1, kept.x[:, g * GT + i - 1, :])
                wait_alone(dve, row_added, g * GT + GT, kept.passed)
                norm.stats_on_vector(dve, g, GT - 1, kept.x[:, g * GT + GT - 1, :])
                norm.meanvar_on_vector(dve, g)
                for i in range(GT):
                    wait_count(dve, turned, g * GT + i - 1)
                    norm.rows_on_vector(dve, i, kept.x[:, g * GT + i, :], xn[:, i % 2, :])
                for i in range(GT):
                    part = slice(i * P, (i + 1) * P)
                    dve.wait_ge(hi_ready, g * GT + i + 1)
                    dve.tensor_tensor(xnt[1][:, g % 2, :, part], by_chunk(turn_bank[i % 2][:, :]),
                                      whole(xnt[0][:, g % 2, :, part]), ALU.subtract).then_inc(lo_ready, 1)

            rows(0)
            with dve.Fori(1, NG) as g:
                rows(g)

        @block.tensor
        def _(pe):
            pe.wait_ge(split.lo_ready, 1)

            def rows(g):
                pe.wait_ge(acc_lo, g + 1)
                for i in range(GT):
                    wait_count(pe, row_added, g * GT + i - 1)
                    product(pe, row_bank[i % 2][:, :], [a[:, i * P:(i + 1) * P] for a in accp],
                            [w[:, :] for w in w_up]).then_inc(row_filled, 1)
                for i in range(GT):
                    pe.wait_ge(norm.normed, g * GT + i + 1)
                    wait_count(pe, lo_ready, g * GT + i - 1)
                    for c in range(KD):
                        done = pe.transpose(turn_bank[i % 2][:, c * P:(c + 1) * P], xn[:, i % 2, c * P:(c + 1) * P],
                                            kept.ident[:, :])
                    done.then_inc(turned, 1)

            def outputs(g):
                pe.wait_ge(lo_ready, g * GT + GT)
                pe.wait_ge(split.lo_ready, len(split.parts))
                for m in range(FILLS):
                    wait_count(pe, read, g * FILLS + m - 3)
                    if m < KD:
                        done = product(pe, out_bank[m % 4][:, :], [w[:, m * P:(m + 1) * P] for w in w_head],
                                       [x[:, g % 2, m, :] for x in xnt])
                    else:
                        for k in range(KD):
                            col = (m - KD) * P
                            done = product(pe, out_bank[m % 4][:, :], [w[:, k, col:col + P] for w in w_gate],
                                           [x[:, g % 2, k, :] for x in xnt], first=(k == 0), last=(k == KD - 1))
                    done.then_inc(filled, 1)

            skewed(pe, rows, outputs)


def attention_stage(nc, kept, io):
    H2 = S // 2
    MASKED = S + H2
    with ExitStack() as ctx:
        mem = Memory(nc, ctx)
        sb, sem = mem.sb, mem.sem
        mask = sb("mask", [P, KD, MASKED])
        w_raw = sb("head_raw", [P, D])
        w_all = mem.pair("head_w_all", [P, D])
        w_head = mem.pair("head_w", [P, P])
        ctx_raw = sb("ctx_raw", [P, T])
        ctxp = mem.pair("ctxp", [P, T])
        keys = sb("keys", [P, T])
        keyp = mem.pair("keyp", [P, T])
        queryp = mem.pair("queryp", [P, T])
        valuep = mem.pair("valuep", [P, 2, B, P])
        scores = sb("scores", [P, MASKED])
        att = sb("att", [P, MASKED])
        attp = mem.pair("attp", [P, 2, S])
        key_bank = [mem.bank(f"key{i}") for i in range(2)]
        value_bank = [mem.bank(f"value{i}") for i in range(2)]
        score_bank = [mem.bank(f"score{i}") for i in range(2)]
        o_bank = [mem.bank(f"o{i}") for i in range(2)]
        mask_loaded, w_loaded, w_hi, w_lo, w_slot = (sem("mask_loaded"), sem("head_w_loaded"), sem("head_w_hi"),
                                                     sem("head_w_lo"), sem("head_w_slot"))
        ctx_loaded, ctx_hi, ctx_lo = sem("ctx3_loaded"), sem("ctx3_hi"), sem("ctx3_lo")
        key_filled, keys_read, key_hi, key_lo = sem("key_filled"), sem("keys_read"), sem("key_hi"), sem("key_lo")
        query_hi, query_lo = sem("query_hi"), sem("query_lo")
        value_turned, value_hi, value_lo = sem("value_turned"), sem("value_hi"), sem("value_lo")
        scored, masked, att_ready, att_hi, att_lo = (sem("scored"), sem("masked"), sem("att_ready"),
                                                     sem("att_hi"), sem("att_lo"))
        ones_set, o_filled, o_read = sem("att_ones_set"), sem("o_filled"), sem("o_read")
        block = ctx.enter_context(nc.Block())

        def part(g):
            return slice(g * GW, (g + 1) * GW)

        @block.sync
        def _(sp):
            sp.dma_start(w_raw[:, :].rearrange("p (h e) -> p h e", h=KD), io["heads"].rearrange("h p e -> p h e")
                         ).then_inc(w_loaded, 16)
            sp.dma_start(ctx_raw[:, :], io["ctx_t"][0:P, :]).then_inc(ctx_loaded, 16)
            sp.dma_start(mask[:, :, :], io["mask"]).then_inc(mask_loaded, 16)
            with sp.Fori(1, KD) as h:
                sp.wait_ge(ctx_lo, h * NG)
                sp.dma_start(ctx_raw[:, :], io["ctx_t"][bass.ds(h * P, P), :]).then_inc(ctx_loaded, 16)

        @block.gpsimd
        def _(pool):
            pool.memset(attp[0][:, 1, 0:H2].bitcast(F32), 1.0)
            pool.memset(attp[1][:, 1, 0:H2].bitcast(F32), 0.0).then_inc(ones_set, 1)
            pool.wait_ge(w_hi, 1)
            pool.tensor_tensor(w_all[1][:, :], w_raw[:, :], whole(w_all[0][:, :]), ALU.subtract).then_inc(w_lo, 1)
            pool.wait_ge(w_lo, 1)
            with pool.Fori(0, KD) as h:
                wait_count(pool, key_filled, h * NG)
                for n in range(2):
                    pool.tensor_copy(w_head[n][:, :], whole(w_all[n][:, bass.ds(h * P, P)])).then_inc(w_slot, 1)

        @block.scalar
        def _(act):
            act.wait_ge(w_loaded, 16)
            act.activation(w_all[0][:, :], w_raw[:, :], ACT.Copy).then_inc(w_hi, 1)

            def ctx_parts(h):
                act.wait_ge(ctx_loaded, h * 16 + 16)
                wait_count(act, key_filled, h * NG)
                for g in range(NG):
                    act.activation(ctxp[0][:, part(g)], ctx_raw[:, part(g)], ACT.Copy).then_inc(ctx_hi, 1)

            def read_keys(h):
                for g in range(NG):
                    act.wait_ge(key_filled, h * NG + g + 1)
                    if g == 0:
                        wait_count(act, value_turned, h * NG)
                        wait_count(act, key_lo, h * NG)
                    act.activation(keys[:, part(g)], key_bank[g % 2][:, :], ACT.Copy).then_inc(keys_read, 1)

            def queries(h):
                wait_count(act, scored, h * 2)
                for g in range(NG):
                    act.activation(queryp[0][:, part(g)], kept.queries[:, h, part(g)], ACT.Copy).then_inc(query_hi, 1)

            def values(h):
                for g in range(NG):
                    act.wait_ge(value_turned, h * NG + g + 1)
                    if g == 0:
                        wait_count(act, o_filled, h * 4)
                    act.activation(valuep[0][:, :, 2 * g:2 * g + 2, :].rearrange("p t b d -> p b t d"),
                                   value_bank[g % 2][:, :].rearrange("p (b t d) -> p b t d", b=2, t=2),
                                   ACT.Copy).then_inc(value_hi, 1)

            def outputs(h):
                act.wait_ge(query_lo, h * NG + NG)
                for n in range(4):
                    s, half = n // 2, n % 2
                    act.wait_ge(o_filled, h * 4 + n + 1)
                    act.activation(kept.queries[:, h, :].rearrange("p (b s d) -> p b s d", s=2, d=P)[:, 4 * half:4 * half + 4, s, :],
                                   o_bank[n % 2][:, :].rearrange("p (b d) -> p b d", b=4), ACT.Copy).then_inc(o_read, 1)

            def head(h, more):
                values(h)
                if more:
                    ctx_parts(h + 1)
                    read_keys(h + 1)
                    outputs(h)
                    queries(h + 1)
                else:
                    outputs(h)

            ctx_parts(0)
            queries(0)
            read_keys(0)
            head(0, True)
            with act.Fori(1, KD - 1) as h:
                head(h, True)
            head(KD - 1, False)

        @block.vector
        def _(dve):
            def ctx_parts(h):
                for g in range(NG):
                    dve.wait_ge(ctx_hi, h * NG + g + 1)
                    dve.tensor_tensor(ctxp[1][:, part(g)], ctx_raw[:, part(g)], whole(ctxp[0][:, part(g)]),
                                      ALU.subtract).then_inc(ctx_lo, 1)

            def split_keys(h):
                wait_count(dve, scored, h * 2)
                for g in range(NG):
                    dve.wait_ge(keys_read, h * NG + g + 1)
                    dve.tensor_copy(keyp[0][:, part(g)], keys[:, part(g)]).then_inc(key_hi, 1)
                for g in range(NG):
                    dve.wait_ge(key_hi, h * NG + g + 1)
                    dve.tensor_tensor(keyp[1][:, part(g)], keys[:, part(g)], whole(keyp[0][:, part(g)]),
                                      ALU.subtract).then_inc(key_lo, 1)

            def queries(h):
                for g in range(NG):
                    dve.wait_ge(query_hi, h * NG + g + 1)
                    dve.tensor_tensor(queryp[1][:, part(g)], kept.queries[:, h, part(g)], whole(queryp[0][:, part(g)]),
                                      ALU.subtract).then_inc(query_lo, 1)

            def values(h):
                for g in range(NG):
                    dve.wait_ge(value_hi, h * NG + g + 1)
                    for b in range(2):
                        done = dve.tensor_tensor(valuep[1][:, :, 2 * g + b, :],
                                                 value_bank[g % 2][:, b * S:(b + 1) * S].rearrange("p (t d) -> p t d", t=2),
                                                 whole(valuep[0][:, :, 2 * g + b, :]), ALU.subtract)
                    done.then_inc(value_lo, 1)

            def attention(h):
                for t, (a, b) in enumerate(((0, S), (S, MASKED))):
                    n = 2 * h + t
                    place = (slice(None), t, slice(H2 * t, S))
                    dve.wait_ge(scored, n + 1)
                    dve.tensor_tensor(scores[:, a:b], score_bank[t][:, 0:b - a], mask[:, h, a:b], ALU.mult).then_inc(masked, 1)
                    dve.wait_ge(masked, n + 1)
                    dve.scalar_tensor_tensor(att[:, a:b], scores[:, a:b], -1.0, scores[:, a:b], ALU.mult, ALU.max
                                             ).then_inc(att_ready, 1)
                    dve.wait_ge(att_ready, n + 1)
                    dve.tensor_scalar(attp[0][place], att[:, a:b], 1.0, None, ALU.max).then_inc(att_hi, 1)
                    dve.wait_ge(att_hi, n + 1)
                    dve.scalar_tensor_tensor(attp[1][place], att[:, a:b], 1.0, whole(attp[0][place]),
                                             ALU.max, ALU.subtract).then_inc(att_lo, 1)

            def head(h, more):
                values(h)
                if more:
                    ctx_parts(h + 1)
                wait_count(dve, o_filled, h * 4)
                attention(h)
                if more:
                    split_keys(h + 1)
                    queries(h + 1)

            dve.wait_ge(mask_loaded, 16)
            ctx_parts(0)
            queries(0)
            split_keys(0)
            with dve.Fori(0, KD - 1) as h:
                head(h, True)
            head(KD - 1, False)

        @block.tensor
        def _(pe):
            pe.wait_ge(ones_set, 1)

            def make_keys(h):
                pe.wait_ge(w_slot, h * 2 + 2)
                for g in range(NG):
                    pe.wait_ge(ctx_lo, h * NG + g + 1)
                    wait_count(pe, keys_read, h * NG + g - 1)
                    product(pe, key_bank[g % 2][:, :], [w[:, :] for w in w_head],
                            [c[:, part(g)] for c in ctxp]).then_inc(key_filled, 1)

            def head(h, more):
                for g in range(NG):
                    pe.wait_ge(keys_read, h * NG + g + 1)
                    wait_count(pe, value_lo, h * NG + g - 1)
                    for i in range(GT):
                        col = g * GW + i * P
                        done = pe.transpose(value_bank[g % 2][:, i * P:(i + 1) * P], keys[:, col:col + P], kept.ident[:, :])
                    done.then_inc(value_turned, 1)
                pe.wait_ge(key_lo, h * NG + NG)
                pe.wait_ge(query_lo, h * NG + NG)
                wait_count(pe, masked, h * 2)
                for t in range(2):
                    for b in range(B):
                        k, q = b * S + t * H2, b * S + t * H2
                        done = product(pe, score_bank[t][:, 0:S - t * H2], [w[:, k:k + P] for w in keyp],
                                       [x[:, q:(b + 1) * S] for x in queryp], first=(b == 0), last=(b == B - 1))
                    done.then_inc(scored, 1)
                if more:
                    make_keys(h + 1)
                pe.wait_ge(value_lo, h * NG + NG)
                pe.wait_ge(att_lo, h * 2 + 2)
                for n in range(4):
                    s, half = n // 2, n % 2
                    wait_count(pe, o_read, h * 4 + n - 1)
                    for t in range(2):
                        done = product(pe, o_bank[n % 2][:, :], [a[:, t, s * P:(s + 1) * P] for a in attp],
                                       [v[:, t, 4 * half:4 * half + 4, :] for v in valuep], first=(t == 0), last=(t == 1))
                    done.then_inc(o_filled, 1)

            make_keys(0)
            head(0, True)
            with pe.Fori(1, KD - 1) as h:
                head(h, True)
            head(KD - 1, False)


def output_stage(nc, kept, io):
    GN_EPS = 1e-3
    with ExitStack() as ctx:
        mem = Memory(nc, ctx)
        sb, sem = mem.sb, mem.sem
        w_out = mem.pair("w_out", [P, KD, D])
        split = Split(mem, "out_w", [(io["wo"][k * P:(k + 1) * P, :], w_out[0][:, k], w_out[1][:, k], D) for k in range(KD)])
        norm = Norm(mem, "out_norm", GN_EPS, kept.passed)
        gamma_beta = sb("gamma_beta", [P, 2, KD])
        yn = sb("yn", [P, GT, D])
        yt = sb("yt", [P, 2, GW])
        z = sb("z", [P, 2, GW])
        zp = mem.pair("zp", [P, KD, GW])
        turn_bank = [mem.bank(f"turn4{c}") for c in range(KD)]
        row_bank = [mem.bank(f"row4{i}") for i in range(4)]
        small_loaded = sem("gamma_loaded")
        turned, y_read, z_ready, z_hi, z_lo = sem("turned4"), sem("y_read"), sem("z_ready"), sem("z_hi"), sem("z_lo")
        row_filled, row_added = sem("row4_filled"), sem("row4_added")
        block = ctx.enter_context(nc.Block())

        def out_row(g, i):
            return kept.queries[:, :, bass.ds(g * GW + i * P, P)]

        @block.gpsimd
        def _(pool):
            norm.pool_start(pool)
            split.on_pool(pool)
            with pool.Fori(0, NG) as g:
                norm.on_pool(pool, g)

        @block.scalar
        def _(act):
            act.dma_start(gamma_beta[:, :, :], io["gamma_beta"]).then_inc(small_loaded, 16)
            split.on_scalar(act)
            act.wait_ge(small_loaded, 16)

            def gated(g):
                for c in range(KD):
                    n = g * KD + c
                    act.wait_ge(turned, n + 1)
                    wait_count(act, z_ready, n - 1)
                    act.activation(yt[:, c % 2], turn_bank[c][:, :], ACT.Identity, scale=gamma_beta[:, 0, c:c + 1],
                                   bias=gamma_beta[:, 1, c:c + 1]).then_inc(y_read, 1)
                    act.wait_ge(z_ready, n + 1)
                    if c == 0:
                        wait_count(act, row_filled, g * GT)
                    act.activation(zp[0][:, c], z[:, c % 2], ACT.Copy).then_inc(z_hi, 1)

            gated(0)
            with act.Fori(1, NG) as g:
                gated(g)

        @block.vector
        def _(dve):
            def norms(g):
                for i in range(GT):
                    norm.stats_on_vector(dve, g, i, out_row(g, i))
                norm.meanvar_on_vector(dve, g)
                wait_count(dve, turned, g * KD)
                for i in range(GT):
                    norm.rows_on_vector(dve, i, out_row(g, i), yn[:, i, :].rearrange("p (h d) -> p h d", h=KD))

            def gated(g):
                for c in range(KD):
                    n = g * KD + c
                    dve.wait_ge(y_read, n + 1)
                    dve.tensor_tensor(z[:, c % 2], yt[:, c % 2], kept.ogate[:, c, bass.ds(g * GW, GW)], ALU.mult
                                      ).then_inc(z_ready, 1)
                    dve.wait_ge(z_hi, n + 1)
                    dve.tensor_tensor(zp[1][:, c], z[:, c % 2], whole(zp[0][:, c]), ALU.subtract).then_inc(z_lo, 1)

            def rows(g):
                for i in range(GT):
                    row = kept.x[:, g * GT + i, :]
                    dve.wait_ge(row_filled, g * GT + i + 1)
                    dve.tensor_tensor(row, row, row_bank[i][:, :], ALU.add).then_inc(row_added, 1)

            norms(0)
            with dve.Fori(0, NG - 1) as g:
                gated(g)
                norms(g + 1)
                rows(g)
            gated(NG - 1)
            rows(NG - 1)

        @block.tensor
        def _(pe):
            def turns(g):
                pe.wait_ge(norm.normed, g * GT + GT)
                for c in range(KD):
                    wait_count(pe, y_read, (g - 1) * KD + c + 1 if isinstance(g, int) else g * KD - KD + c + 1)
                    for i in range(GT):
                        done = pe.transpose(turn_bank[c][:, i * P:(i + 1) * P], yn[:, i, c * P:(c + 1) * P], kept.ident[:, :])
                    done.then_inc(turned, 1)

            def rows(g):
                pe.wait_ge(z_lo, g * KD + KD)
                for i in range(GT):
                    wait_count(pe, row_added, g * GT - GT + i + 1)
                    for k in range(KD):
                        done = product(pe, row_bank[i][:, :], [x[:, k, i * P:(i + 1) * P] for x in zp],
                                       [w[:, k] for w in w_out], first=(k == 0), last=(k == KD - 1))
                    done.then_inc(row_filled, 1)

            turns(0)
            pe.wait_ge(split.lo_ready, KD)
            rows(0)
            with pe.Fori(1, NG) as g:
                turns(g)
                rows(g)


def router_stage(nc, kept, io):
    NH = 2 * HID // P
    with ExitStack() as ctx:
        mem = Memory(nc, ctx)
        sb, sem = mem.sb, mem.sem
        w_route, w_up, w_down = mem.pair("w_route", [P, KD, P]), mem.pair("w_shup", [P, KD, D]), mem.pair("w_shdown", [P, NH, D])
        split = Split(mem, "shared_w",
                      [(io["w_router"].rearrange("(k p) e -> p k e", p=P), w_route[0][:, :, 0:E1], w_route[1][:, :, 0:E1], KD * E1)]
                      + [(io["wsh_up"][k * P:(k + 1) * P, :], w_up[0][:, k], w_up[1][:, k], D) for k in range(KD)]
                      + [(io["wsh_down"][j * P:(j + 1) * P, :], w_down[0][:, j], w_down[1][:, j], D) for j in range(NH)])
        norm = Norm(mem, "route_norm", LN_EPS, kept.passed)
        xn = sb("xn3", [P, 2, D])
        xnt = mem.pair("xn3t", [P, KD, T])
        hid = sb("hid5", [P, 2, GW])
        hidp = mem.pair("hid5p", [P, NH, GW])
        logit_t = sb("logit5_t", [E1, GW])
        logits = sb("logits5", [P, NT, E1])
        peak, total_exp = sb("peak", [P, NT]), sb("total_exp", [P, NT])
        probs = sb("probs5", [P, NT, E1])
        top8, index8 = sb("top8_5", [P, NT, 8]), sb("index8", [P, NT, 8], U32)
        expert_no, slot_no, lane_no = sb("expert_no", [P, E1]), sb("slot_no", [P, SLOTS]), sb("lane_no", [P, P])
        tile_ends, tile_no, row_no = sb("tile_ends", [P, NT + 1]), sb("tile_no", [P, NT]), sb("row_no", [P, 1])
        keep = sb("keep", [P, E1, NT])
        before_me, all_ones = sb("before_me", [P, P], BF16), sb("all_ones", [P, P], BF16)
        choice = sb("choice", [P, 2, NT])
        picked = sb("picked", [P, 2, NT, E1])
        member = sb("member", [P, NT, E1], BF16)
        counts = sb("counts", [P, E1, NT])
        base = sb("base", [P, NT, E1])
        wide = sb("wide", [P, SLOTS, E1])
        tiles, slot_end, slot_start = sb("tiles5", [P, E1]), sb("slot_end", [P, E1]), sb("slot_start", [P, E1])
        slot_of = sb("slot_of", [P, SLOTS])
        rank, first, skip, lane = (sb(n, [P, 2, NT]) for n in ("rank", "first_slot", "skip_slots", "lane"))
        lane_hot = sb("lane_hot", [P, 2, NT, P], BF16)
        slot_hot = sb("slot_hot", [P, 2, NT, SLOTS])
        slot_ids = sb("slot_ids", [P, 2, NT, 2, SLOTS], BF16)
        id_part = sb("id_part", [P, SLOTS])

        turn_bank = [mem.bank(f"turn5{i}") for i in range(2)]
        logit_bank, plan_bank = mem.bank("logit5"), mem.bank("plan5")
        up_bank = [mem.bank(f"up5{i}") for i in range(2)]
        row_bank = [mem.bank(f"row5{i}") for i in range(2)]
        set_pool, set_dve = sem("set5_pool"), sem("set5_dve")
        row_stored = [sem("row_stored_even"), sem("row_stored_odd")]
        turned, hi_ready, lo_ready = sem("turned5"), sem("xn3t_hi"), sem("xn3t_lo")
        logit_filled, logit_read = sem("logit_filled"), sem("logit_read")
        logit_turned, logits_ready = sem("logit_turned"), sem("logits_ready")
        up_filled, gelu_ready, hid_hi, hid_lo = sem("up5_filled"), sem("gelu_ready"), sem("hid5_hi"), sem("hid5_lo")
        row_filled, row_added = sem("row5_filled"), sem("row5_added")
        shifted, exped, plan = sem("shifted"), sem("exped"), sem("plan_steps")
        member_ready, counted, ids_hot, ids_filled = sem("member_ready"), sem("counted"), sem("ids_hot"), sem("ids_filled")
        block = ctx.enter_context(nc.Block())

        def by_chunk(ap):
            return ap.rearrange("p (c t) -> p c t", c=KD)

        def flat(ap):
            return ap.rearrange("p a b -> p (a b)")

        def staggered(ahead, logits_part, shared_part):
            for g in range(NG + 1):
                if g < NG:
                    ahead(g)
                if g > 0:
                    logits_part(g - 1)
                if 2 <= g < NG:
                    shared_part(g - 2)

        @block.sync
        def _(sp):
            rows = kept.xn_dram.rearrange("(n p) d -> p n d", p=P)
            with sp.Fori(0, NT // 2) as pair:
                for i in range(2):
                    j = 2 * pair
                    sp.wait_ge(norm.normed, j + i + 1)
                    sp.dma_start(rows[:, bass.ds(j + i, 1), :].rearrange("p n d -> p (n d)"), xn[:, i, :]
                                 ).then_inc(row_stored[i], 16)
            for i in range(2):
                sp.wait_ge(row_stored[i], 16 * (NT // 2))

        @block.gpsimd
        def _(pool):
            norm.pool_start(pool)
            for tile, pattern, base_value, per_partition in (
                    (expert_no[:, :], [[1, E1]], 0, 0), (slot_no[:, :], [[1, SLOTS]], 0, 0),
                    (lane_no[:, :], [[1, P]], 0, 0), (tile_ends[:, :], [[P, NT + 1]], 0, 0),
                    (tile_no[:, :], [[1, NT]], 0, 0), (row_no[:, :], [[1, 1]], 0, 1)):
                pool.iota(tile, pattern, base=base_value, channel_multiplier=per_partition,
                          allow_small_or_imprecise_dtypes=True)
            pool.memset(keep[:, :, :], 1.0)
            pool.memset(all_ones[:, :], 1.0).then_inc(set_pool, 1)
            pool.wait_ge(set_pool, 1)
            pool.memset(keep[:, :, 0:1], 0.0)
            pool.affine_select(out=before_me[:, :], in_=kept.ones[:, :], pattern=[[1, P]], compare_op=ALU.is_gt,
                               fill=0.0, base=0, channel_multiplier=-1).then_inc(set_pool, 1)
            split.on_pool(pool)
            with pool.Fori(0, NG) as g:
                norm.on_pool(pool, g)

        @block.scalar
        def _(act):
            split.on_scalar(act)

            def ahead(g):
                for i in range(GT):
                    act.wait_ge(turned, g * GT + i + 1)
                    act.activation(xnt[0][:, :, bass.ds(g * GW + i * P, P)], by_chunk(turn_bank[i % 2][:, :]),
                                   ACT.Copy).then_inc(hi_ready, 1)

            def logits_part(g):
                act.wait_ge(logit_filled, g + 1)
                wait_count(act, logit_turned, g)
                act.activation(logit_t[:, :], logit_bank[0:E1, :], ACT.Copy).then_inc(logit_read, 1)
                act.wait_ge(logit_turned, g + 1)
                act.activation(flat(logits[:, bass.ds(g * GT, GT), :]), plan_bank[:, 0:GT * E1], ACT.Copy
                               ).then_inc(logits_ready, 1)

            def shared_part(g):
                for j in range(NH):
                    n = g * NH + j
                    act.wait_ge(up_filled, n + 1)
                    wait_count(act, hid_lo, n - 1)
                    act.activation(hid[:, j % 2], up_bank[j % 2][:, :], ACT.Gelu).then_inc(gelu_ready, 1)
                    act.wait_ge(gelu_ready, n + 1)
                    if j == 0:
                        wait_count(act, row_filled, g * GT)
                    act.activation(hidp[0][:, j], hid[:, j % 2], ACT.Copy).then_inc(hid_hi, 1)

            staggered(ahead, logits_part, shared_part)
            act.wait_ge(shifted, 1)
            act.activation(flat(probs[:, :, :]), flat(logits[:, :, :]), ACT.Exp).then_inc(exped, 1)
            shared_part(NG - 2)
            shared_part(NG - 1)

        @block.vector
        def _(dve):
            for part in w_route:
                dve.memset(part[:, :, E1:P].bitcast(F32), 0.0).then_inc(set_dve, 1)

            def ahead(g):
                for i in range(GT):
                    norm.stats_on_vector(dve, g, i, kept.x[:, g * GT + i, :])
                norm.meanvar_on_vector(dve, g)
                for i in range(GT):
                    wait_count(dve, turned, g * GT + i - 1)
                    if i > 1:
                        dve.wait_ge(row_stored[i % 2], 16 * 2 * g + 16)
                    else:
                        wait_count(dve, row_stored[i % 2], 16 * 2 * g)
                    norm.rows_on_vector(dve, i, kept.x[:, g * GT + i, :], xn[:, i % 2, :])
                for i in range(GT):
                    part = bass.ds(g * GW + i * P, P)
                    dve.wait_ge(hi_ready, g * GT + i + 1)
                    dve.tensor_tensor(xnt[1][:, :, part], by_chunk(turn_bank[i % 2][:, :]), whole(xnt[0][:, :, part]),
                                      ALU.subtract).then_inc(lo_ready, 1)

            def shared_part(g):
                for j in range(NH):
                    n = g * NH + j
                    dve.wait_ge(hid_hi, n + 1)
                    dve.tensor_tensor(hidp[1][:, j], hid[:, j % 2], whole(hidp[0][:, j]), ALU.subtract).then_inc(hid_lo, 1)
                for i in range(GT):
                    row = kept.x[:, g * GT + i, :]
                    dve.wait_ge(row_filled, g * GT + i + 1)
                    dve.tensor_tensor(row, row, row_bank[i % 2][:, :], ALU.add).then_inc(row_added, 1)

            step = Ticks(plan)

            def on(ins):
                dve.wait_ge(plan, step.tick(ins))

            def along(ap, n, axis):
                shape = list(ap.shape)
                shape.insert(axis, n)
                return ap.unsqueeze(axis).to_broadcast(shape)

            def choose():
                dve.wait_ge(logits_ready, NG)
                on(dve.tensor_reduce(peak[:, :], logits[:, :, :], AX_X, ALU.max))
                dve.tensor_tensor(logits[:, :, :], logits[:, :, :], along(peak[:, :], E1, 2), ALU.subtract).then_inc(shifted, 1)
                dve.wait_ge(exped, 1)
                on(dve.tensor_reduce(total_exp[:, :], probs[:, :, :], AX_X, ALU.add))
                on(dve.reciprocal(total_exp[:, :], total_exp[:, :]))
                on(dve.tensor_tensor(probs[:, :, :], probs[:, :, :], along(total_exp[:, :], E1, 2), ALU.mult))
                for j in range(NT):
                    last = step.tick(dve.max(top8[:, j], probs[:, j]))
                for j in range(NT):
                    dve.wait_ge(plan, last - NT + 1 + j)
                    found = step.tick(dve.max_index(index8[:, j], top8[:, j], probs[:, j]))
                step.tick(dve.tensor_copy(kept.route_gate[:, :, :], top8[:, :, 0:2].rearrange("p j c -> p c j")))
                dve.wait_ge(plan, found)
                on(dve.tensor_copy(choice[:, :, :], index8[:, :, 0:2].rearrange("p j c -> p c j")))
                dve.wait_ge(set_pool, 2)
                for c in range(2):
                    last = step.tick(dve.tensor_tensor(picked[:, c], along(expert_no[:, :], NT, 1),
                                                       along(choice[:, c], E1, 2), ALU.is_equal))
                dve.wait_ge(plan, last)
                dve.tensor_tensor(member[:, :, :], picked[:, 0], picked[:, 1], ALU.add).then_inc(member_ready, 1)

            def place():
                before = plan_bank[:, 0:NT * E1].rearrange("p (j e) -> p j e", j=NT)
                total = plan_bank[:, NT * E1:2 * NT * E1].rearrange("p (j e) -> p j e", j=NT)
                dve.wait_ge(counted, 1)
                on(dve.tensor_copy(counts[:, :, :], total.rearrange("p j e -> p e j")))
                on(dve.tensor_tensor_scan(flat(counts[:, :, :]), flat(keep[:, :, :]), flat(counts[:, :, :]), 0.0,
                                          ALU.mult, ALU.add))
                on(dve.tensor_tensor(base[:, :, :], counts[:, :, :].rearrange("p e j -> p j e"), total, ALU.subtract))
                on(dve.tensor_tensor(base[:, :, :], base[:, :, :], before, ALU.add))
                on(dve.tensor_tensor(wide[:, 0:E1, :], along(counts[:, :, NT - 1], NT, 2), along(tile_ends[:, 0:NT], E1, 1),
                                     ALU.is_gt))
                on(dve.tensor_reduce(tiles[:, :], wide[:, 0:E1, :], AX_X, ALU.add))
                on(dve.tensor_tensor_scan(slot_end[:, :], all_ones[:, 0:E1], tiles[:, :], 0.0, ALU.mult, ALU.add))
                on(dve.tensor_tensor(slot_start[:, :], slot_end[:, :], tiles[:, :], ALU.subtract))
                on(dve.tensor_tensor(wide[:, :, :], along(slot_end[:, :], SLOTS, 1), along(slot_no[:, :], E1, 2), ALU.is_le))
                on(dve.tensor_reduce(slot_of[:, :], wide[:, :, :], AX_X, ALU.add))
                on(dve.tensor_scalar(kept.slot_expert[:, :], slot_of[:, :], float(E1 - 1), None, ALU.min))
                for c in range(2):
                    part = wide[:, 16 * c:16 * c + NT, :]
                    on(dve.tensor_tensor(part, picked[:, c], base[:, :, :], ALU.mult))
                    on(dve.tensor_reduce(rank[:, c], part, AX_X, ALU.add))
                    on(dve.tensor_tensor(part, picked[:, c], along(slot_start[:, :], NT, 1), ALU.mult))
                    on(dve.tensor_reduce(first[:, c], part, AX_X, ALU.add))
                    on(dve.tensor_tensor(part, along(rank[:, c], NT, 2), along(tile_ends[:, 1:NT + 1], NT, 1), ALU.is_ge))
                    on(dve.tensor_reduce(skip[:, c], part, AX_X, ALU.add))
                on(dve.tensor_tensor(first[:, :, :], first[:, :, :], skip[:, :, :], ALU.add))
                on(dve.scalar_tensor_tensor(lane[:, :, :], skip[:, :, :], float(-P), rank[:, :, :], ALU.mult, ALU.add))
                on(dve.scalar_tensor_tensor(kept.route_row[:, :, :], first[:, :, :], float(P), lane[:, :, :],
                                            ALU.mult, ALU.add))
                for c in range(2):
                    step.tick(dve.tensor_tensor(lane_hot[:, c], along(lane_no[:, :], NT, 1), along(lane[:, c], P, 2),
                                                ALU.is_equal))
                    on(dve.tensor_tensor(slot_hot[:, c], along(slot_no[:, :], NT, 1), along(first[:, c], SLOTS, 2),
                                         ALU.is_equal))
                    step.tick(dve.tensor_scalar(slot_ids[:, c, :, 0, :], slot_hot[:, c], row_no[:, 0:1], None, ALU.mult))
                    dve.tensor_tensor(slot_ids[:, c, :, 1, :], slot_hot[:, c], along(tile_no[:, :], SLOTS, 2),
                                      ALU.mult).then_inc(ids_hot, 1)

            staggered(ahead, lambda g: None, shared_part)
            choose()
            shared_part(NG - 2)
            place()
            shared_part(NG - 1)
            dve.wait_ge(ids_filled, 1)
            on(dve.tensor_copy(id_part[:, :], plan_bank[:, 0:SLOTS]))
            on(dve.scalar_tensor_tensor(kept.slot_token[:, :], plan_bank[:, SLOTS:2 * SLOTS], float(P), id_part[:, :],
                                        ALU.mult, ALU.add))

        @block.tensor
        def _(pe):
            pe.wait_ge(set_dve, 2)

            def ahead(g):
                for i in range(GT):
                    pe.wait_ge(norm.normed, g * GT + i + 1)
                    wait_count(pe, lo_ready, g * GT + i - 1)
                    for c in range(KD):
                        done = pe.transpose(turn_bank[i % 2][:, c * P:(c + 1) * P], xn[:, i % 2, c * P:(c + 1) * P],
                                            kept.ident[:, :])
                    done.then_inc(turned, 1)

            def logits_part(g):
                pe.wait_ge(lo_ready, g * GT + GT)
                pe.wait_ge(split.lo_ready, 1)
                wait_count(pe, logit_read, g)
                for k in range(KD):
                    done = product(pe, logit_bank[:, :], [w[:, k] for w in w_route],
                                   [x[:, k, bass.ds(g * GW, GW)] for x in xnt], first=(k == 0), last=(k == KD - 1))
                done.then_inc(logit_filled, 1)
                pe.wait_ge(logit_read, g + 1)
                wait_count(pe, logits_ready, g)
                for i in range(GT):
                    done = pe.transpose(plan_bank[:, i * E1:(i + 1) * E1], logit_t[:, i * P:(i + 1) * P],
                                        kept.ident[0:E1, 0:E1])
                done.then_inc(logit_turned, 1)

            def shared_part(g):
                pe.wait_ge(split.lo_ready, len(split.parts))
                for j in range(NH):
                    n = g * NH + j
                    wait_count(pe, gelu_ready, n - 1)
                    for k in range(KD):
                        done = product(pe, up_bank[j % 2][:, :], [w[:, k, j * P:(j + 1) * P] for w in w_up],
                                       [x[:, k, bass.ds(g * GW, GW)] for x in xnt], first=(k == 0), last=(k == KD - 1))
                    done.then_inc(up_filled, 1)
                pe.wait_ge(hid_lo, g * NH + NH)
                for i in range(GT):
                    wait_count(pe, row_added, g * GT + i - 1)
                    for j in range(NH):
                        done = product(pe, row_bank[i % 2][:, :], [h[:, j, i * P:(i + 1) * P] for h in hidp],
                                       [w[:, j] for w in w_down], first=(j == 0), last=(j == NH - 1))
                    done.then_inc(row_filled, 1)

            staggered(ahead, logits_part, shared_part)
            shared_part(NG - 2)
            pe.wait_ge(member_ready, 1)
            pe.wait_ge(logits_ready, NG)
            pe.wait_ge(set_pool, 2)
            pe.matmul(plan_bank[:, 0:NT * E1], before_me[:, :], flat(member[:, :, :]), start=True, stop=True)
            pe.matmul(plan_bank[:, NT * E1:2 * NT * E1], all_ones[:, :], flat(member[:, :, :]), start=True, stop=True
                      ).then_inc(counted, 1)
            shared_part(NG - 1)
            pe.wait_ge(ids_hot, 2)
            for c in range(2):
                for j in range(NT):
                    done = pe.matmul(plan_bank[:, 0:2 * SLOTS], lane_hot[:, c, j], flat(slot_ids[:, c, j]),
                                     start=(c == 0 and j == 0), stop=(c == 1 and j == NT - 1))
            done.then_inc(ids_filled, 1)


def routed_stage(nc, kept, io):
    CU, CD = KD * HID, HJ * D
    with ExitStack() as ctx:
        mem = Memory(nc, ctx)
        sb, sem = mem.sb, mem.sem
        w_up, w_down = sb("w_rt_up", [P, E1, CU]), sb("w_rt_down", [P, E1, CD])
        rows = sb("slot_rows", [P, 2, D])
        index = [sb(f"slot_index{i}", [P, 1], I32) for i in range(2)]
        xt = [sb(f"slot_xt{i}", [P, KD, P]) for i in range(2)]
        mid = [sb(f"slot_mid{i}", [P, HID]) for i in range(2)]
        mid_t = [sb(f"slot_mid_t{i}", [P, HJ, P]) for i in range(2)]
        y = sb("slot_y", [P, 2, D])
        turn_bank = [mem.bank(f"turn6{i}") for i in range(2)]
        up_bank = [mem.bank(f"up6{i}") for i in range(2)]
        mid_bank = [mem.bank(f"mid6{i}") for i in range(2)]
        y_bank = [mem.bank(f"y6{i}") for i in range(2)]
        w_loaded = sem("rt_w_loaded")
        fetched, indexed = [sem("fetched_even"), sem("fetched_odd")], sem("indexed")
        turned, xt_ready = sem("rows_turned"), sem("xt_ready")
        up_filled, mid_ready, mid_turned, mid_t_ready = sem("up6_filled"), sem("mid_ready"), sem("mid_turned"), sem("mid_t_ready")
        y_filled, y_ready = sem("y6_filled"), sem("y6_ready")
        y_stored = [sem("y_stored_even"), sem("y_stored_odd")]
        block = ctx.enter_context(nc.Block())

        def slots(eng, one):
            one(0, 0)
            one(1, 1)
            with eng.Fori(1, SLOTS // 2) as pair:
                s = 2 * pair
                one(s, 0)
                one(s + 1, 1)
            one(SLOTS - 1, (SLOTS - 1) % 2)

        @block.sync
        def _(sp):
            with sp.Fori(0, E1) as e:
                sp.dma_start(w_up[:, bass.ds(e, 1), :].rearrange("p o m -> p (o m)"),
                             io["wrt_up"][bass.ds(e, 1)].rearrange("o p m -> (o p) m")).then_inc(w_loaded, 16)
                sp.dma_start(w_down[:, bass.ds(e, 1), :].rearrange("p o m -> p (o m)"),
                             io["wrt_down"][bass.ds(e, 1)].rearrange("o p m -> (o p) m")).then_inc(w_loaded, 16)

            def store(s, i):
                sp.wait_ge(y_ready, s + 1)
                sp.dma_start(kept.y_dram[bass.ds(s * P, P), :], y[:, i, :]).then_inc(y_stored[i], 16)

            slots(sp, store)
            sp.wait_ge(y_stored[0], 16 * ((SLOTS + 1) // 2))
            sp.wait_ge(y_stored[1], 16 * (SLOTS // 2))

        @block.gpsimd
        def _(pool):
            def fetch(s, i):
                wait_count(pool, fetched[i], (s - i) * 8)
                pool.tensor_copy(index[i][:, :], kept.slot_token[:, bass.ds(s, 1)]).then_inc(indexed, 1)
                pool.wait_ge(indexed, s + 1)
                wait_alone(pool, turned, s - 1, kept.passed)
                pool.indirect_dma_start(rows[:, i, :], None, kept.xn_dram, bass.IndirectOffsetOnAxis(index[i][:, :], 0)
                                        ).then_inc(fetched[i], 16)

            slots(pool, fetch)

        @block.scalar
        def _(act):
            def hidden(s, i):
                act.wait_ge(up_filled, s + 1)
                wait_count(act, mid_turned, s - 1)
                act.activation(mid[i][:, :], up_bank[i][:, 0:HID], ACT.Gelu).then_inc(mid_ready, 1)
                act.wait_ge(mid_turned, s + 1)
                wait_count(act, y_filled, s - 1)
                act.activation(mid_t[i][:, :, :].rearrange("p j t -> p (j t)"), mid_bank[i][:, 0:HID], ACT.Copy
                               ).then_inc(mid_t_ready, 1)

            slots(act, hidden)

        @block.vector
        def _(dve):
            def turned_rows(s, i):
                dve.wait_ge(turned, s + 1)
                wait_count(dve, up_filled, s - 1)
                dve.tensor_copy(xt[i][:, :, :].rearrange("p k t -> p (k t)"), turn_bank[i][:, :]).then_inc(xt_ready, 1)

            def result(s, i):
                dve.wait_ge(y_filled, s + 1)
                stored = (s - i) * 8
                wait_count(dve, y_stored[i], stored)
                dve.tensor_copy(y[:, i, :], y_bank[i][:, :]).then_inc(y_ready, 1)

            turned_rows(0, 0)
            turned_rows(1, 1)
            result(0, 0)
            turned_rows(2, 0)
            result(1, 1)
            with dve.Fori(1, SLOTS // 2) as pair:
                s = 2 * pair
                turned_rows(s + 1, 1)
                result(s, 0)
                turned_rows(s + 2, 0)
                result(s + 1, 1)
            result(SLOTS - 1, 0)

        @block.tensor
        def _(pe):
            def turn(s, i):
                pe.wait_ge(fetched[i], (s - i) * 8 + 16)
                wait_count(pe, xt_ready, s - 1)
                for c in range(KD):
                    done = pe.transpose(turn_bank[i][:, c * P:(c + 1) * P], rows[:, i, c * P:(c + 1) * P], kept.ident[:, :])
                done.then_inc(turned, 1)

            def turn_mid(s, i):
                pe.wait_ge(mid_ready, s + 1)
                wait_count(pe, mid_t_ready, s - 1)
                for j in range(HJ):
                    done = pe.transpose(mid_bank[i][:, j * P:(j + 1) * P], mid[i][:, j * P:(j + 1) * P], kept.ident[:, :])
                done.then_inc(mid_turned, 1)

            def up(s, i, e):
                pe.wait_ge(xt_ready, s + 1)
                wait_count(pe, mid_ready, s - 1)
                for k in range(KD):
                    done = pe.matmul(up_bank[i][:, 0:HID], xt[i][:, k], w_up[:, bass.ds(e, 1), k * HID:(k + 1) * HID]
                                     .rearrange("p o m -> p (o m)"), start=(k == 0), stop=(k == KD - 1))
                done.then_inc(up_filled, 1)

            def down(s, i, e):
                pe.wait_ge(mid_t_ready, s + 1)
                wait_count(pe, y_ready, s - 1)
                for j in range(HJ):
                    done = pe.matmul(y_bank[i][:, :], mid_t[i][:, j], w_down[:, bass.ds(e, 1), j * D:(j + 1) * D]
                                     .rearrange("p o m -> p (o m)"), start=(j == 0), stop=(j == HJ - 1))
                done.then_inc(y_filled, 1)

            def expert(s):
                return pe.value_load(kept.slot_expert[0:1, bass.ds(s, 1)], min_val=0, max_val=E1 - 1)

            def step(s, i, turn_next=True, behind=True):
                if turn_next:
                    turn(s + 1, 1 - i)
                if behind:
                    turn_mid(s - 1, 1 - i)
                up(s, i, expert(s))
                if behind:
                    down(s - 1, 1 - i, expert(s - 1))

            pe.wait_ge(w_loaded, 32 * E1)
            turn(0, 0)
            step(0, 0, behind=False)
            step(1, 1)
            with pe.Fori(1, SLOTS // 2) as pair:
                s = 2 * pair
                step(s, 0)
                step(s + 1, 1)
            step(SLOTS - 1, 0, turn_next=False)
            turn_mid(SLOTS - 1, 0)
            down(SLOTS - 1, 0, expert(SLOTS - 1))


def combine_stage(nc, kept, io):
    SETS = 4
    with ExitStack() as ctx:
        mem = Memory(nc, ctx)
        sb, sem = mem.sb, mem.sem
        picks = sb("picks", [P, SETS, 2, D])
        index = [[sb(f"pick_index{i}_{c}", [P, 1], I32) for c in range(2)] for i in range(SETS)]
        indexed = sem("pick_indexed")
        fetched = [sem(f"picks_fetched{i}") for i in range(SETS)]
        half, added, stored = sem("first_added"), sem("both_added"), sem("out_stored")
        block = ctx.enter_context(nc.Block())

        def tiles(eng, one):
            with eng.Fori(0, NT // SETS) as r:
                for i in range(SETS):
                    one(r * SETS + i, i, r)

        @block.gpsimd
        def _(pool):
            def fetch(j, i, r):
                if not isinstance(r, int) or r > 0:
                    pool.wait_ge(added, j - SETS + 1)
                for c in range(2):
                    pool.tensor_copy(index[i][c][:, :], kept.route_row[:, c, bass.ds(j, 1)]).then_inc(indexed, 1)
                    wait_alone(pool, indexed, 2 * j + c + 1, kept.passed)
                    pool.indirect_dma_start(picks[:, i, c, :], None, kept.y_dram, bass.IndirectOffsetOnAxis(index[i][c][:, :], 0)
                                            ).then_inc(fetched[i], 16)

            for i in range(SETS):
                fetch(i, i, 0)
            with pool.Fori(1, NT // SETS) as r:
                for i in range(SETS):
                    fetch(r * SETS + i, i, r)

        @block.vector
        def _(dve):
            def add(j, i, r):
                row = kept.x[:, bass.ds(j, 1), :].rearrange("p o d -> p (o d)")
                dve.wait_ge(fetched[i], r * 32 + 32)
                dve.scalar_tensor_tensor(row, picks[:, i, 0, :], kept.route_gate[:, 0, bass.ds(j, 1)], row,
                                         ALU.mult, ALU.add).then_inc(half, 1)
                dve.wait_ge(half, j + 1)
                dve.scalar_tensor_tensor(row, picks[:, i, 1, :], kept.route_gate[:, 1, bass.ds(j, 1)], row,
                                         ALU.mult, ALU.add).then_inc(added, 1)

            tiles(dve, add)

        @block.sync
        def _(sp):
            out = io["out"].rearrange("(n p) d -> p n d", p=P)

            def store(j, i, r):
                sp.wait_ge(added, j + 1)
                sp.dma_start(out[:, bass.ds(j, 1), :], kept.x[:, bass.ds(j, 1), :]).then_inc(stored, 16)

            tiles(sp, store)
            sp.wait_ge(stored, 16 * NT)


class Kept:
    pass


def build(nc, io):
    kept = Kept()
    with ExitStack() as ctx:
        mem = Memory(nc, ctx)
        kept.gate_dram = nc.dram_tensor("gate_scratch", [E0, T], F32).ap()
        kept.passed = mem.sem("passed")
        kept.x = mem.sb("x_rows", [P, NT, D])
        kept.ident = mem.sb("ident", [P, P])
        kept.ones = mem.sb("ones", [P, P])
        with ExitStack() as latent_ctx:
            kept.latent = Memory(nc, latent_ctx).sb("latent", [P, T])
            clear(nc, mix_stage(nc, kept, io))
            latent_moe_stage(nc, kept, io)
            with ExitStack() as att_ctx:
                att = Memory(nc, att_ctx)
                kept.queries = att.sb("queries", [P, KD, T])
                kept.ogate = att.sb("ogate", [P, KD, T])
                query_stage(nc, kept, io)
                attention_stage(nc, kept, io)
                output_stage(nc, kept, io)
        moe_stages(nc, kept, io, mem)


def moe_stages(nc, kept, io, mem):
    kept.xn_dram = nc.dram_tensor("xn_scratch", [T, D], F32).ap()
    kept.y_dram = nc.dram_tensor("y_scratch", [SLOTS * P, D], F32).ap()
    kept.slot_token = mem.sb("slot_token", [P, SLOTS], I32)
    kept.slot_expert = mem.sb("slot_expert", [P, SLOTS], I32)
    kept.route_row = mem.sb("route_row", [P, 2, NT], I32)
    kept.route_gate = mem.sb("route_gate", [P, 2, NT])
    router_stage(nc, kept, io)
    routed_stage(nc, kept, io)
    combine_stage(nc, kept, io)


def decay_mask():
    import numpy as np

    gam = 1.0 - 2.0 ** (-5.0 - np.arange(KD, dtype=np.float64))
    expo = np.arange(S, dtype=np.float64)[None, :] - np.arange(S, dtype=np.float64)[:, None]
    table = np.where(expo[None] <= 0, gam[:, None, None] ** np.minimum(expo, 0.0)[None], 0.0)
    table = table / np.sqrt(table.sum(axis=-1))[:, None, :] / np.sqrt(float(P))
    turned = table.transpose(2, 0, 1)
    return np.ascontiguousarray(np.concatenate([turned[0:P], turned[P:S, :, P:S]], axis=2).astype(np.float32))


def layouts(a):
    import numpy as np

    def rows(x):
        return np.ascontiguousarray(x)

    return {
        "x": rows(a["x"].reshape(T, D)),
        "ctx_t": rows(a["ctx_2048"].reshape(T, D).T),
        "decay_first": rows(np.stack([a["L0_xattn_time_decay"].reshape(KD, P).T,
                                      a["L0_xattn_time_first"].reshape(KD, P).T], axis=1)),
        "bias": rows(a["L0_ffn_biases"].reshape(1, E0)),
        "w_front": rows(np.concatenate([a["L0_ffn_Wdown"].T, a["L0_ffn_swg"].T, a["L0_ffn_sw1"].T,
                                        a["L0_ffn_Wg"].T], axis=1)),
        "sw2_t": rows(a["L0_ffn_sw2"].T),
        "wup_t": rows(a["L0_ffn_Wup"].T),
        "heads": rows(a["L1_xattn_Wh"]),
        "wg": rows(a["L1_xattn_wg_w"]),
        "wo": rows(a["L1_xattn_wo_w"]),
        "gamma_beta": rows(np.stack([a["L1_xattn_gn_gamma"].reshape(KD, P).T,
                                     a["L1_xattn_gn_beta"].reshape(KD, P).T], axis=1)),
        "mask": decay_mask(),
        "w_router": rows(a["L1_ffn_W_router"]),
        "wsh_up": rows(a["L1_ffn_Wsh_up"].transpose(1, 0, 2).reshape(D, 2 * HID)),
        "wsh_down": rows(a["L1_ffn_Wsh_down"].reshape(2 * HID, D)),
        "wrt_up": rows(a["L1_ffn_Wrt_up"].reshape(E1, KD, P, HID).transpose(0, 2, 1, 3).reshape(E1, P, KD * HID)),
        "wrt_down": rows(a["L1_ffn_Wrt_down"].reshape(E1, HJ, P, D).transpose(0, 2, 1, 3).reshape(E1, P, HJ * D)),
        "experts": rows(np.concatenate([a["L0_ffn_rw1"].transpose(0, 2, 1), a["L0_ffn_rwg"].transpose(0, 2, 1),
                                        a["L0_ffn_rw2"].transpose(0, 2, 1).reshape(E0, HJ, P, LAT)
                                        .transpose(0, 2, 1, 3).reshape(E0, P, HJ * LAT)], axis=2)),
    }


def kernel(**inputs):
    import concourse.bacc as bacc
    from concourse.bass_utils import run_bass_kernel_spmd

    nc = bacc.Bacc("TRN2", target_bir_lowering=False, num_devices=1)
    arrays, io = {}, {}
    for name, a in layouts(inputs).items():
        arrays["in_" + name] = a
        io[name] = nc.dram_tensor("in_" + name, a.shape, mybir.dt.from_np(a.dtype), kind="ExternalInput").ap()
    io["out"] = nc.dram_tensor("out_rows", [T, D], F32, kind="ExternalOutput").ap()
    build(nc, io)
    result = run_bass_kernel_spmd(nc, [arrays], core_ids=[0])
    return result.results[0]["out_rows"].reshape(B, S, D)
```

```python
from contextlib import ExitStack

import concourse.bass as bass
from concourse import mybir

F32 = mybir.dt.float32
F32R = mybir.dt.float32r
BF16 = mybir.dt.bfloat16
I32 = mybir.dt.int32
U32 = mybir.dt.uint32
ALU = mybir.AluOpType
ACT = mybir.ActivationFunctionType
AX_X = mybir.AxisListType.X

P = 128
B, S, D = 8, 256, 512
T = B * S
NT = T // P
GT = 4
GW = GT * P
NG = NT // GT
KD = D // P
LAT, HID, E0 = 128, 256, 16
TOP0 = 8
SCALE0 = 2.5
HJ = HID // P
E1 = 16
SLOTS = 2 * NT + E1 - 1
LN_EPS = 1e-5
NEVER = -1e38


class Ticks:

    def __init__(self, sem, base=0):
        self.sem, self.base, self.n = sem, base, 0

    def tick(self, ins):
        ins.then_inc(self.sem, 1)
        self.n += 1
        return self.base + self.n


def product(pe, out, w, x, first=True, last=True):
    pe.matmul(out, w[0], x[0], start=first, stop=False)
    pe.matmul(out, w[0], x[1], start=False, stop=False)
    return pe.matmul(out, w[1], x[0], start=False, stop=last)


def whole(ap):
    return ap.bitcast(F32)


class Memory:

    def __init__(self, nc, ctx):
        self.nc, self.ctx, self.sems = nc, ctx, []

    def sb(self, name, shape, dtype=F32):
        return self.ctx.enter_context(self.nc.sbuf_tensor(name, shape, dtype))

    def pair(self, name, shape):
        return self.sb(name + "_hi", shape, F32R), self.sb(name + "_lo", shape, F32R)

    def bank(self, name, dtype=F32):
        return self.ctx.enter_context(self.nc.psum_tensor(name, [P, 512], dtype))

    def sem(self, name):
        self.sems.append(self.ctx.enter_context(self.nc.semaphore(name)))
        return self.sems[-1]


def wait_count(eng, sem, count):
    if not isinstance(count, int) or count > 0:
        eng.wait_ge(sem, count)


def wait_alone(eng, sem, count, passed):
    if not isinstance(count, int) or count > 0:
        eng.wait_ge(sem, count)
        if not isinstance(count, int):
            eng.sem_inc(passed, 1)


def starts(n):
    return isinstance(n, int) and n == 0


def side_by_side(eng, group, in_place_of_moe=None):
    def run(g):
        return lambda part, *args: part(g, *args)

    def leave_out(part, *args):
        pass

    group(run(0), in_place_of_moe or leave_out)
    group(run(1), run(0))
    with eng.Fori(2, NG) as g:
        group(run(g), run(g - 1))
    group(leave_out, run(NG - 1))


def mix_stage(nc, kept, io):
    C_DOWN, C_SGATE, C_SUP, C_ROUTE = 0, LAT, LAT + HID, LAT + 2 * HID
    C_ALL = C_ROUTE + P
    LOGIT, LOGIT_T, LATENT, HIDDEN, ROWS, GATE_T = 0, 1, 2, 3, 7, 11
    FILLS = 12
    ACT_READS = [LOGIT, LOGIT_T, LATENT, HIDDEN, HIDDEN + 2, GATE_T]
    DVE_READS = [HIDDEN + 1, HIDDEN + 3, ROWS, ROWS + 1, ROWS + 2, ROWS + 3]
    DVE_MIX, DVE_MOE = 64, 18

    with ExitStack() as ctx:
        mem = Memory(nc, ctx)
        sb, sem = mem.sb, mem.sem
        front = mem.pair("w_front", [P, KD, C_ALL])
        raw = sb("w_raw", [P, 2, C_ROUTE + E0])
        shared_down = mem.pair("w_shared_down", [P, HJ, D])
        bias = sb("gate_bias", [P, E0])
        small = sb("time_decay_and_first", [P, 2, KD])
        exp_decay = sb("exp_decay", [P, KD])
        decay = sb("decay", [P, KD])
        minus_half = sb("minus_half", [P, GT])
        ctx_t = sb("ctx_t", [P, 2, KD, GW])
        stats = sb("stats", [P, GT, 6])
        meanvar = sb("meanvar", [P, GT, 2])
        vareps = sb("vareps", [P, GT])
        rstd = sb("rstd", [P, GT])
        xn = sb("xn", [P, 2, D])
        key = sb("key", [P, KD, GW])
        xnt = mem.pair("xnt", [P, 2, KD, GW])
        top = sb("wkv_top", [P, 2, S + 1])
        num_state = sb("wkv_num_state", [P, 2, S + 1])
        den_state = sb("wkv_den_state", [P, 2, S + 1])
        gap = sb("wkv_gap", [P, GW])
        weight = sb("wkv_weight", [P, 2, 4, GW])
        v_in = sb("wkv_v_in", [P, 2, GW])
        v_now = sb("wkv_v_now", [P, 2, GW])
        den = sb("wkv_den", [P, 2, GW])
        num = sb("wkv_num", [P, 2, GW])
        guess = sb("wkv_guess", [P, 2, GW])
        miss = sb("wkv_miss", [P, GW])
        logit_t = sb("logit_t", [E0, GW])
        minus_exp = sb("exp_minus_logit", [P, GT, E0])
        prob = sb("prob", [P, GT, E0])
        biased = sb("biased", [P, GT, E0])
        cut = sb("cut", [P, GT, E0])
        top8 = sb("top8", [P, GT, TOP0])
        prob_sum = sb("prob_sum", [P, GT])
        gate = sb("gate", [P, GT, E0])
        gate_t = sb("gate_t", [E0, GW])
        relu = sb("shared_relu", [P, GW])
        relu2 = sb("shared_relu2", [P, HJ, GW])
        hid = sb("shared_hid", [P, GW])
        hidp = mem.pair("shared_hidp", [P, HJ, GW])
        turn_bank = [mem.bank(f"turn{i}") for i in range(2)]
        y_bank = [mem.bank(f"y{i}") for i in range(2)]
        out_bank = [mem.bank(f"out{i}") for i in range(4)]

        x_loaded, ctx_loaded = sem("x_loaded"), sem("ctx_loaded")
        small_loaded, w_loaded = sem("small_loaded"), [sem("w_loaded_even"), sem("w_loaded_odd")]
        w_hi_ready, w_lo_ready = sem("w_hi_ready"), sem("w_lo_ready")
        set_dve, set_pool = sem("set_by_dve"), sem("set_by_pool")
        decay_exp = sem("decay_exp")
        meanvar_ready, rstd_ready, vareps_ready = sem("meanvar_ready"), sem("rstd_ready"), sem("vareps_ready")
        normed, turned = sem("normed"), sem("turned")
        key_ready = sem("key_ready")
        expo_ready, weight_ready, v_ready = sem("expo_ready"), sem("weight_ready"), sem("v_ready")
        den_ready, num_ready = sem("den_ready"), sem("num_ready")
        log_ready, guess_ready = sem("log_ready"), sem("guess_ready")
        y_ready, y_turned, y_added = sem("y_ready"), sem("y_turned"), sem("y_added")
        hi_ready, lo_ready = sem("xnt_hi_ready"), sem("xnt_lo_ready")
        filled, read_act, read_dve = sem("filled"), sem("read_by_act"), sem("read_by_dve")
        relu2_ready, hidden_ready = sem("relu2_ready"), sem("hidden_ready")
        gate_ready, gate_stored = sem("gate_ready"), sem("gate_stored")
        dve_mix, dve_moe = sem("dve_mix_steps"), sem("dve_moe_steps")
        block = ctx.enter_context(nc.Block())

        def act_read(g, fill):
            return g * len(ACT_READS) + ACT_READS.index(fill) + 1

        def dve_read(g, fill):
            return g * len(DVE_READS) + DVE_READS.index(fill) + 1

        weight_parts = [(front[0][:, k, 0:C_ROUTE + E0], front[1][:, k, 0:C_ROUTE + E0], C_ROUTE + E0) for k in range(KD)]
        weight_parts += [(shared_down[0][:, j, :], shared_down[1][:, j, :], D) for j in range(HJ)]

        def load_weights(eng, n):
            src = io["w_front"][n * P:(n + 1) * P, :] if n < KD else io["sw2_t"][(n - KD) * P:(n - KD + 1) * P, :]
            eng.dma_start(raw[:, n % 2, 0:weight_parts[n][2]], src).then_inc(w_loaded[n % 2], 16)

        def by_chunk(ap):
            return ap.rearrange("p (c t) -> p c t", c=KD)

        def by_batch(ap):
            return ap.rearrange("p (b t) -> p b t", b=2)

        @block.sync
        def _(sp):
            x_in = io["x"].rearrange("(n p) d -> p n d", p=P)
            ctx_in = io["ctx_t"].rearrange("(c p) t -> p c t", p=P)
            for g in range(NG):
                sp.dma_start(kept.x[:, g * GT:(g + 1) * GT, :], x_in[:, g * GT:(g + 1) * GT, :]
                             ).then_inc(x_loaded, 16)
                if g == 0:
                    sp.wait_ge(x_loaded, 16)
                    for slot in range(2):
                        sp.dma_start(ctx_t[:, slot], ctx_in[:, :, slot * GW:(slot + 1) * GW]
                                     ).then_inc(ctx_loaded, 16)
                        sp.wait_ge(ctx_loaded, 16 * slot + 16)
                sp.wait_ge(x_loaded, 16 * g + 16)
            with sp.Fori(2, NG) as g:
                sp.wait_ge(v_ready, g * KD - KD)
                sp.dma_start(ctx_t[:, g % 2], ctx_in[:, :, bass.ds(g * GW, GW)]).then_inc(ctx_loaded, 16)
                sp.wait_ge(ctx_loaded, g * 16 + 16)
                sp.wait_ge(read_act, (g - 2) * len(ACT_READS) + len(ACT_READS))
                sp.dma_start(kept.gate_dram[:, bass.ds((g - 2) * GW, GW)], gate_t[:, :]).then_inc(gate_stored, 16)
            with sp.Fori(NG - 2, NG) as g:
                sp.wait_ge(read_act, g * len(ACT_READS) + len(ACT_READS))
                sp.dma_start(kept.gate_dram[:, bass.ds(g * GW, GW)], gate_t[:, :]).then_inc(gate_stored, 16)
            sp.wait_ge(gate_stored, 16 * NG)

        @block.gpsimd
        def _(pool):
            pool.memset(kept.ones[:, :], 1.0).then_inc(set_pool, 1)
            pool.memset(minus_half[:, :], -0.5).then_inc(set_pool, 1)
            pool.wait_ge(set_pool, 1)
            pool.affine_select(out=kept.ident[:, :], in_=kept.ones[:, :], pattern=[[-1, P]],
                               compare_op=ALU.is_equal, fill=0.0, base=0,
                               channel_multiplier=1).then_inc(set_pool, 1)
            pool.wait_ge(set_pool, 3)

            def rstds(g, norm):
                n = 2 * g + norm
                wait_alone(pool, meanvar_ready, n * GT + GT, kept.passed)
                pool.tensor_scalar(vareps[:, :], meanvar[:, :, 1], LN_EPS, None, ALU.add).then_inc(vareps_ready, 1)
                pool.wait_ge(vareps_ready, n + 1)
                wait_count(pool, normed, n * GT)
                pool.tensor_tensor(rstd[:, :], vareps[:, :], minus_half[:, :], ALU.pow).then_inc(rstd_ready, 1)

            def split_weights(parts):
                for n in parts:
                    hi, lo, width = weight_parts[n]
                    pool.wait_ge(w_hi_ready, n + 1)
                    pool.tensor_tensor(lo, raw[:, n % 2, 0:width], whole(hi), ALU.subtract).then_inc(w_lo_ready, 1)

            def mix(g, splits=((), (), (), (), ())):
                rstds(g, 0)
                pool.wait_ge(ctx_loaded, g * 16 + 16)
                for c in range(KD):
                    k = g * KD + c
                    pool.wait_ge(weight_ready, k + 1)
                    wait_count(pool, num_ready, k - 1)
                    pool.tensor_tensor(v_in[:, c % 2], weight[:, c % 2, 1], ctx_t[:, g % 2, c], ALU.mult)
                    pool.tensor_tensor(v_now[:, c % 2], weight[:, c % 2, 3], ctx_t[:, g % 2, c],
                                       ALU.mult).then_inc(v_ready, 1)
                    split_weights(splits[c])
                rstds(g, 1)
                split_weights(splits[KD])

            mix(0, splits=((0,), (1,), (2,), (3,), (4, 5)))
            with pool.Fori(1, NG) as g:
                mix(g)

        @block.scalar
        def _(act):
            act.dma_start(small[:, :, :], io["decay_first"]).then_inc(small_loaded, 16)
            act.dma_start(bias[:, :], io["bias"].to_broadcast([P, E0])).then_inc(small_loaded, 16)
            load_weights(act, 0)
            load_weights(act, 1)
            act.preload_act_table_set("natural_log_exp_and_others")
            act.wait_ge(small_loaded, 32)
            act.activation(exp_decay[:, :], small[:, 0, :], ACT.Exp).then_inc(decay_exp, 1)


            def keys(g):
                for i in range(GT):
                    act.wait_ge(turned, 2 * g * GT + i + 1)
                    act.activation(key[:, :, i * P:(i + 1) * P], by_chunk(turn_bank[i % 2][:, :]),
                                   ACT.Copy).then_inc(key_ready, 1)

            def weights(g, c):
                act.wait_ge(expo_ready, g * KD + c + 1)
                act.activation(weight[:, c % 2], weight[:, c % 2], ACT.Exp).then_inc(weight_ready, 1)

            def guesses(g, c):
                k = g * KD
                act.wait_ge(den_ready, k + c + 1)
                wait_count(act, y_ready, k + c - 1)
                act.activation(guess[:, c % 2], den[:, c % 2], ACT.Ln).then_inc(log_ready, 1)
                act.wait_ge(log_ready, k + c + 1)
                act.activation(guess[:, c % 2], guess[:, c % 2], ACT.Exp, scale=-1.0).then_inc(guess_ready, 1)

            def second_norm(g):
                for i in range(GT):
                    act.wait_ge(turned, 2 * g * GT + GT + i + 1)
                    act.activation(xnt[0][:, g % 2, :, i * P:(i + 1) * P], by_chunk(turn_bank[i % 2][:, :]),
                                   ACT.Copy).then_inc(hi_ready, 1)

            def logit(g):
                act.wait_ge(filled, g * FILLS + LOGIT + 1)
                act.activation(logit_t[:, :], out_bank[0][0:E0, :], ACT.Copy).then_inc(read_act, 1)

            def turned_logit_and_latent(g):
                act.wait_ge(filled, g * FILLS + LOGIT_T + 1)
                act.activation(minus_exp[:, :, :].rearrange("p i e -> p (i e)"), out_bank[1][:, 0:GT * E0],
                               ACT.Exp, scale=-1.0).then_inc(read_act, 1)
                act.wait_ge(filled, g * FILLS + LATENT + 1)
                act.activation(kept.latent[:, bass.ds(g * GW, GW)], out_bank[2][:, :], ACT.Copy).then_inc(read_act, 1)

            def squares(g, j):
                act.wait_ge(filled, g * FILLS + HIDDEN + 2 * j + 1)
                wait_count(act, relu2_ready, g * HJ + j)
                act.activation(relu[:, :], out_bank[(HIDDEN + 2 * j) % 4][:, :], ACT.Relu).then_inc(read_act, 1)
                act.wait_ge(read_act, act_read(g, HIDDEN + 2 * j))
                act.activation(relu2[:, j], relu[:, :], ACT.Square).then_inc(relu2_ready, 1)

            def turned_gates(g):
                act.wait_ge(filled, g * FILLS + GATE_T + 1)
                wait_count(act, gate_stored, g * 16)
                act.activation(gate_t[:, :], out_bank[3][0:E0, :], ACT.Copy).then_inc(read_act, 1)

            def group(mix, moe):
                mix(keys)
                mix(weights, 0)
                moe(logit)
                mix(weights, 1)
                moe(turned_logit_and_latent)
                mix(guesses, 0)
                mix(weights, 2)
                moe(squares, 0)
                mix(guesses, 1)
                mix(weights, 3)
                moe(squares, 1)
                mix(guesses, 2)
                mix(guesses, 3)
                moe(turned_gates)
                mix(second_norm)

            weight_turns = iter(range(len(weight_parts)))

            def split_weights(moe_part, *args):
                for n in [next(weight_turns)] + (list(weight_turns) if moe_part is turned_gates else []):
                    if n > 1:
                        act.wait_ge(w_lo_ready, n - 1)
                        load_weights(act, n)
                    act.wait_ge(w_loaded[n % 2], 16 * (n // 2) + 16)
                    hi, _, width = weight_parts[n]
                    act.activation(hi, raw[:, n % 2, 0:width], ACT.Copy).then_inc(w_hi_ready, 1)

            side_by_side(act, group, in_place_of_moe=split_weights)

        @block.vector
        def _(dve):
            dve.memset(top[:, :, 0:1], NEVER)
            dve.memset(num_state[:, :, 0:1], 0.0)
            dve.memset(den_state[:, :, 0:1], 0.0)
            dve.memset(front[0][:, :, C_ROUTE + E0:C_ALL].bitcast(F32), 0.0)
            dve.memset(front[1][:, :, C_ROUTE + E0:C_ALL].bitcast(F32), 0.0).then_inc(set_dve, 1)
            dve.wait_ge(decay_exp, 1)
            dve.tensor_scalar(decay[:, :], exp_decay[:, :], -1.0, None, ALU.mult).then_inc(set_dve, 1)
            dve.wait_ge(set_dve, 2)

            def norm(g, which, step):
                for i in range(GT):
                    last = step.tick(dve.bn_stats(stats[:, i, :], kept.x[:, g * GT + i, :]))
                for i in range(GT):
                    wait_alone(dve, step.sem, last - GT + 1 + i, kept.passed)
                    dve.bn_aggr(meanvar[:, i, :], stats[:, i, :]).then_inc(meanvar_ready, 1)
                dve.wait_ge(rstd_ready, 2 * g + which + 1)
                for i in range(GT):
                    wait_count(dve, turned, (2 * g + which) * GT + i - 1)
                    dve.tensor_scalar(xn[:, i % 2, :], kept.x[:, g * GT + i, :], meanvar[:, i, 0:1],
                                      rstd[:, i:i + 1], ALU.subtract, ALU.mult).then_inc(normed, 1)

            mixed = Ticks(dve_mix)
            routed = Ticks(dve_moe)

            def first_norm(g):
                mixed.base, mixed.n = g * DVE_MIX, 0
                wait_alone(dve, x_loaded, g * 16 + 16, kept.passed)
                norm(g, 0, mixed)
                dve.wait_ge(key_ready, g * KD + KD)

            def exponents(g, c):
                slot, keys = c % 2, key[:, c, :]
                before, after = top[:, :, 0:S], top[:, :, 1:S + 1]
                for b in range(2):
                    scanned = mixed.tick(dve.tensor_tensor_scan(
                        top[:, b, 1:S + 1], decay[:, c:c + 1].to_broadcast([P, S]),
                        key[:, c, b * S:(b + 1) * S], NEVER, ALU.add, ALU.max))
                dve.wait_ge(dve_mix, scanned)
                wait_count(dve, num_ready, g * KD + c - 1)
                mixed.tick(dve.scalar_tensor_tensor(by_batch(weight[:, slot, 0]), before, decay[:, c:c + 1], after,
                                                    ALU.add, ALU.subtract))
                mixed.tick(dve.tensor_tensor(by_batch(weight[:, slot, 1]), by_batch(keys), after, ALU.subtract))
                gapped = mixed.tick(dve.scalar_tensor_tensor(by_batch(gap[:, :]), by_batch(keys), small[:, 1, c:c + 1],
                                                             before, ALU.add, ALU.subtract))
                dve.wait_ge(dve_mix, gapped)
                mixed.tick(dve.tensor_scalar(weight[:, slot, 2], gap[:, :], -1.0, 0.0, ALU.mult, ALU.min))
                dve.tensor_scalar(weight[:, slot, 3], gap[:, :], 0.0, None, ALU.min).then_inc(expo_ready, 1)

            def states(g, c):
                slot, k = c % 2, g * KD
                keep, old, now = weight[:, slot, 0], weight[:, slot, 2], weight[:, slot, 3]
                dve.wait_ge(v_ready, k + c + 1)
                for b in range(2):
                    part = slice(b * S, (b + 1) * S)
                    mixed.tick(dve.tensor_tensor_scan(den_state[:, b, 1:S + 1], keep[:, part],
                                                      weight[:, slot, 1, part], 0.0, ALU.mult, ALU.add))
                for b in range(2):
                    part = slice(b * S, (b + 1) * S)
                    scanned = mixed.tick(dve.tensor_tensor_scan(num_state[:, b, 1:S + 1], keep[:, part],
                                                                v_in[:, slot, part], 0.0, ALU.mult, ALU.add))
                dve.wait_ge(dve_mix, scanned - 2)
                wait_count(dve, log_ready, k + c - 1)
                a = mixed.tick(dve.tensor_tensor(by_batch(den[:, slot]), by_batch(old), den_state[:, :, 0:S], ALU.mult))
                dve.wait_ge(dve_mix, scanned)
                wait_count(dve, y_turned, k + c - 1)
                b = mixed.tick(dve.tensor_tensor(by_batch(num[:, slot]), by_batch(old), num_state[:, :, 0:S], ALU.mult))
                dve.wait_ge(dve_mix, a)
                dve.tensor_tensor(den[:, slot], den[:, slot], now, ALU.add).then_inc(den_ready, 1)
                dve.wait_ge(dve_mix, b)
                dve.tensor_tensor(num[:, slot], num[:, slot], v_now[:, slot], ALU.add).then_inc(num_ready, 1)

            def quotient(g, c):
                slot = c % 2
                dve.wait_ge(guess_ready, g * KD + c + 1)
                dve.wait_ge(num_ready, g * KD + c + 1)
                mixed.tick(dve.tensor_tensor(miss[:, :], den[:, slot], guess[:, slot], ALU.mult))
                both = mixed.tick(dve.tensor_tensor(num[:, slot], num[:, slot], guess[:, slot], ALU.mult))
                dve.wait_ge(dve_mix, both)
                dve.scalar_tensor_tensor(num[:, slot], miss[:, :], 2.0, num[:, slot],
                                         ALU.subtract, ALU.mult).then_inc(y_ready, 1)

            def add(g, c):
                dve.wait_ge(y_turned, g * KD + c + 1)
                part = kept.x[:, bass.ds(g * GT, GT), c * P:(c + 1) * P]
                dve.tensor_tensor(part, part, y_bank[c % 2][:, :].rearrange("p (i d) -> p i d", i=GT),
                                  ALU.subtract).then_inc(y_added, 1)

            def second_norm(g):
                wait_alone(dve, y_added, g * KD + KD, kept.passed)
                norm(g, 1, mixed)
                for i in range(GT):
                    dve.wait_ge(hi_ready, g * GT + i + 1)
                    part = slice(i * P, (i + 1) * P)
                    dve.tensor_tensor(xnt[1][:, g % 2, :, part], by_chunk(turn_bank[i % 2][:, :]),
                                      whole(xnt[0][:, g % 2, :, part]), ALU.subtract).then_inc(lo_ready, 1)
                assert mixed.n == DVE_MIX, mixed.n

            def on(ins):
                dve.wait_ge(dve_moe, routed.tick(ins))

            def gates(g):
                routed.base, routed.n = g * DVE_MOE, 0
                dve.wait_ge(read_act, act_read(g, LOGIT_T))
                on(dve.tensor_scalar(minus_exp[:, :, :], minus_exp[:, :, :], 1.0, None, ALU.add))
                on(dve.reciprocal(prob[:, :, :], minus_exp[:, :, :]))
                wait_alone(dve, dve_moe, routed.tick(dve.tensor_tensor(
                    biased[:, :, :], prob[:, :, :], bias[:, :].unsqueeze(1).to_broadcast([P, GT, E0]), ALU.add)), kept.passed)
                for i in range(GT):
                    last = routed.tick(dve.max(top8[:, i], biased[:, i]))
                for i in range(GT):
                    wait_alone(dve, dve_moe, last - GT + 1 + i, kept.passed)
                    chosen = routed.tick(dve.match_replace(cut[:, i], top8[:, i], biased[:, i], NEVER))
                dve.wait_ge(dve_moe, chosen)
                on(dve.tensor_tensor(cut[:, :, :], cut[:, :, :], biased[:, :, :], ALU.not_equal))
                on(dve.tensor_tensor(cut[:, :, :], cut[:, :, :], prob[:, :, :], ALU.mult))
                on(dve.tensor_reduce(prob_sum[:, :], cut[:, :, :], AX_X, ALU.add))
                on(dve.reciprocal(prob_sum[:, :], prob_sum[:, :]))
                on(dve.tensor_scalar(prob_sum[:, :], prob_sum[:, :], SCALE0, None, ALU.mult))
                dve.tensor_tensor(gate[:, :, :], cut[:, :, :], prob_sum[:, :].unsqueeze(2).to_broadcast([P, GT, E0]),
                                  ALU.mult).then_inc(gate_ready, 1)

            def hidden(g, j):
                dve.wait_ge(relu2_ready, g * HJ + j + 1)
                dve.wait_ge(filled, g * FILLS + HIDDEN + 2 * j + 2)
                dve.tensor_tensor(hid[:, :], out_bank[(HIDDEN + 2 * j + 1) % 4][:, :], relu2[:, j],
                                  ALU.mult).then_inc(read_dve, 1)
                dve.wait_ge(read_dve, dve_read(g, HIDDEN + 2 * j + 1))
                on(dve.tensor_copy(hidp[0][:, j], hid[:, :]))
                dve.tensor_tensor(hidp[1][:, j], hid[:, :], whole(hidp[0][:, j]), ALU.subtract).then_inc(hidden_ready, 1)
                dve.wait_ge(hidden_ready, g * HJ + j + 1)

            def add_rows(g, tiles):
                for i in tiles:
                    dve.wait_ge(filled, g * FILLS + ROWS + i + 1)
                    dve.tensor_tensor(kept.x[:, g * GT + i, :], kept.x[:, g * GT + i, :],
                                      out_bank[(ROWS + i) % 4][:, :], ALU.add).then_inc(read_dve, 1)

            def group(mix, moe):
                mix(first_norm)
                mix(exponents, 0)
                mix(exponents, 1)
                mix(states, 0)
                moe(gates)
                mix(exponents, 2)
                mix(states, 1)
                moe(hidden, 0)
                mix(quotient, 0)
                mix(exponents, 3)
                mix(states, 2)
                mix(add, 0)
                mix(quotient, 1)
                moe(hidden, 1)
                mix(states, 3)
                mix(add, 1)
                mix(quotient, 2)
                moe(add_rows, (0, 1))
                mix(add, 2)
                mix(quotient, 3)
                moe(add_rows, (2, 3))
                mix(add, 3)
                mix(second_norm)

            side_by_side(dve, group)

        @block.tensor
        def _(pe):
            pe.wait_ge(set_pool, 3)

            def turn(g, which):
                for i in range(GT):
                    pe.wait_ge(normed, 2 * g * GT + which * GT + i + 1)
                    if which == 0 and i < 2:
                        wait_count(pe, lo_ready, g * GT - 1 + i)
                    elif which == 0:
                        pe.wait_ge(key_ready, g * GT + i - 1)
                    elif i < 2:
                        pe.wait_ge(key_ready, g * GT + i + 3)
                    else:
                        pe.wait_ge(lo_ready, g * GT + i - 1)
                    for c in range(KD):
                        done = pe.transpose(turn_bank[i % 2][:, c * P:(c + 1) * P], xn[:, i % 2, c * P:(c + 1) * P],
                                            kept.ident[:, :])
                    done.then_inc(turned, 1)

            def turn_y(g, c):
                pe.wait_ge(y_ready, g * KD + c + 1)
                wait_count(pe, y_added, g * KD + c - 1)
                for i in range(GT):
                    done = pe.transpose(y_bank[c % 2][:, i * P:(i + 1) * P], num[:, c % 2, i * P:(i + 1) * P],
                                        kept.ident[:, :])
                done.then_inc(y_turned, 1)

            def from_norm(g, bank, col):
                for k in range(KD):
                    done = product(pe, out_bank[bank][:, :],
                                   [w[:, k, col:col + P] for w in front], [x[:, g % 2, k, :] for x in xnt],
                                   first=(k == 0), last=(k == KD - 1))
                done.then_inc(filled, 1)

            def logits_and_latent(g):
                pe.wait_ge(w_lo_ready, KD)
                pe.wait_ge(lo_ready, g * GT + GT)
                wait_count(pe, read_dve, g * len(DVE_READS) - 2)
                from_norm(g, 0, C_ROUTE)
                pe.wait_ge(read_act, act_read(g, LOGIT))
                wait_alone(pe, read_dve, g * len(DVE_READS) - 1, kept.passed)
                for i in range(GT):
                    done = pe.transpose(out_bank[1][:, i * E0:(i + 1) * E0], logit_t[:, i * P:(i + 1) * P],
                                        kept.ident[0:E0, 0:E0])
                done.then_inc(filled, 1)
                wait_count(pe, read_dve, g * len(DVE_READS))
                from_norm(g, 2, C_DOWN)

            def hidden(g, j):
                if j == 0:
                    wait_count(pe, read_act, g * len(ACT_READS))
                    from_norm(g, 3, C_SGATE)
                    from_norm(g, 0, C_SUP)
                else:
                    pe.wait_ge(read_act, act_read(g, LOGIT_T))
                    from_norm(g, 1, C_SGATE + P)
                    pe.wait_ge(read_act, act_read(g, LATENT))
                    from_norm(g, 2, C_SUP + P)

            def rows(g):
                pe.wait_ge(w_lo_ready, KD + HJ)
                pe.wait_ge(hidden_ready, g * HJ + HJ)
                for i in range(GT):
                    if i == 0:
                        pe.wait_ge(read_act, act_read(g, HIDDEN))
                    if i == 1:
                        pe.wait_ge(read_dve, dve_read(g, HIDDEN + 1))
                    if i == 2:
                        pe.wait_ge(read_act, act_read(g, HIDDEN + 2))
                    if i == 3:
                        pe.wait_ge(read_dve, dve_read(g, HIDDEN + 3))
                    for j in range(HJ):
                        done = product(pe, out_bank[(ROWS + i) % 4][:, :],
                                       [h[:, j, i * P:(i + 1) * P] for h in hidp], [w[:, j, :] for w in shared_down],
                                       first=(j == 0), last=(j == HJ - 1))
                    done.then_inc(filled, 1)

            def turn_gates(g):
                pe.wait_ge(gate_ready, g + 1)
                pe.wait_ge(read_dve, dve_read(g, ROWS))
                for i in range(GT):
                    done = pe.transpose(out_bank[3][0:E0, i * P:(i + 1) * P], gate[:, i, :], kept.ident[:, :])
                done.then_inc(filled, 1)

            def group(mix, moe):
                mix(turn, 0)
                moe(logits_and_latent)
                moe(hidden, 0)
                mix(turn_y, 0)
                moe(hidden, 1)
                mix(turn_y, 1)
                moe(rows)
                mix(turn_y, 2)
                moe(turn_gates)
                mix(turn_y, 3)
                mix(turn, 1)

            side_by_side(pe, group)
    return mem.sems


def clear(nc, sems):
    with nc.Block() as block:
        @block.gpsimd
        def _(pool):
            for sem in sems:
                pool.sem_clear(sem)


def latent_moe_stage(nc, kept, io):
    HALVES = NG * HJ
    C_UP, C_GATE, C_DOWN = 0, HID, 2 * HID
    C_ALL = 2 * HID + HJ * LAT
    SPLIT_LAG, DOWN_LAG = 2, 4
    with ExitStack() as ctx:
        mem = Memory(nc, ctx)
        sb, sem = mem.sb, mem.sem
        latp = mem.pair("latent_p", [P, T])
        raw = sb("expert_raw", [P, 2, C_ALL])
        wp = [mem.pair(f"expert_w{i}", [P, C_ALL]) for i in range(2)]
        gates = sb("expert_gates", [P, 2, T])
        zeros = sb("expert_zeros", [P, GW], BF16)
        relu = sb("expert_relu", [P, 2, GW])
        relu2 = sb("expert_relu2", [P, 2, GW])
        prod = sb("expert_prod", [P, 2, GW])
        hid = sb("expert_hid", [P, 4, GW])
        hidp = mem.pair("expert_hidp", [P, 4, GW])
        acc = [mem.bank(f"acc{g}") for g in range(NG)]
        up_bank = [mem.bank(f"up{i}") for i in range(2)]
        gate_bank = [mem.bank(f"gate{i}") for i in range(2)]

        w_loaded = [sem("expert_w_even"), sem("expert_w_odd")]
        gates_loaded = [sem("expert_gates_even"), sem("expert_gates_odd")]
        acc_read = sem("acc_read")
        zeros_set, acc_opened = sem("zeros_set"), sem("acc_opened")
        lat_hi, lat_lo = sem("latent_hi"), sem("latent_lo")
        w_hi, w_lo = sem("expert_w_hi"), sem("expert_w_lo")
        gate_filled, up_filled, down_done = sem("gate_filled"), sem("up_filled"), sem("down_done")
        relu_done, relu2_ready = sem("relu_done"), sem("expert_relu2_ready")
        prod_ready, hid_ready, hid_hi, hid_lo = sem("prod_ready"), sem("hid_ready"), sem("hid_hi"), sem("hid_lo")
        block = ctx.enter_context(nc.Block())

        def load(eng, e, i):
            eng.dma_start(raw[:, i, :], io["experts"][bass.ds(e + i, 1)].rearrange("o p m -> (o p) m")
                          ).then_inc(w_loaded[i], 16)
            eng.dma_start(gates[:, i, :], kept.gate_dram[bass.ds(e + i, 1), :].to_broadcast([P, T])
                          ).then_inc(gates_loaded[i], 16)

        @block.sync
        def _(sp):
            load(sp, 0, 0)
            load(sp, 0, 1)
            with sp.Fori(1, E0 // 2) as pair:
                e = 2 * pair
                for i in range(2):
                    wait_alone(sp, w_lo, e + i - 1, kept.passed)
                    wait_alone(sp, hid_ready, (e + i - 1) * HALVES, kept.passed)
                    load(sp, e, i)

        @block.gpsimd
        def _(pool):
            pool.memset(zeros[:, :], 0.0).then_inc(zeros_set, 1)

            def pair_of_experts(e):
                for m in range(2 * HALVES):
                    n = e * HALVES + m
                    i, g = m // HALVES, m % HALVES // HJ
                    if m % HALVES == 0:
                        pool.wait_ge(gates_loaded[i], e * 8 + 16)
                    pool.wait_ge(prod_ready, n + 1)
                    wait_count(pool, hid_lo, n - 3)
                    pool.tensor_tensor(hid[:, m % 4], prod[:, m % 2], gates[:, i, g * GW:(g + 1) * GW],
                                       ALU.mult).then_inc(hid_ready, 1)

            pair_of_experts(0)
            with pool.Fori(1, E0 // 2) as pair:
                e = 2 * pair
                pair_of_experts(e)

        @block.scalar
        def _(act):
            for g in range(NG):
                part = slice(g * GW, (g + 1) * GW)
                act.activation(latp[0][:, part], kept.latent[:, part], ACT.Copy).then_inc(lat_hi, 1)

            def hi(n, m):
                act.wait_ge(hid_ready, n + 1)
                wait_count(act, down_done, n - 3)
                act.activation(hidp[0][:, m % 4], hid[:, m % 4], ACT.Copy).then_inc(hid_hi, 1)

            def pair_of_experts(e):
                for m in range(2 * HALVES):
                    n = e * HALVES + m
                    act.wait_ge(gate_filled, n + 1)
                    wait_count(act, relu2_ready, n - 1)
                    act.activation(relu[:, m % 2], gate_bank[m % 2][:, :], ACT.Relu).then_inc(relu_done, 1)
                    if m >= SPLIT_LAG or not starts(e):
                        hi(n - SPLIT_LAG, m - SPLIT_LAG)
                    act.wait_ge(relu_done, n + 1)
                    wait_count(act, prod_ready, n - 1)
                    act.activation(relu2[:, m % 2], relu[:, m % 2], ACT.Square).then_inc(relu2_ready, 1)

            pair_of_experts(0)
            with act.Fori(1, E0 // 2) as pair:
                e = 2 * pair
                pair_of_experts(e)
            for m in range(2 * HALVES - SPLIT_LAG, 2 * HALVES):
                hi((E0 - 2) * HALVES + m, m)
            act.wait_ge(down_done, E0 * HALVES)
            for g in range(NG):
                act.activation(kept.latent[:, g * GW:(g + 1) * GW], acc[g][:, :], ACT.Copy).then_inc(acc_read, 1)

        @block.vector
        def _(dve):
            for g in range(NG):
                part = slice(g * GW, (g + 1) * GW)
                dve.wait_ge(lat_hi, g + 1)
                dve.tensor_tensor(latp[1][:, part], kept.latent[:, part], whole(latp[0][:, part]),
                                  ALU.subtract).then_inc(lat_lo, 1)

            def split_weights(e, i):
                dve.wait_ge(w_loaded[i], (e - i) * 8 + 16)
                dve.tensor_copy(wp[i][0][:, :], raw[:, i]).then_inc(w_hi, 1)
                dve.wait_ge(w_hi, e + 1)
                dve.tensor_tensor(wp[i][1][:, :], raw[:, i], whole(wp[i][0][:, :]), ALU.subtract).then_inc(w_lo, 1)

            def lo(n, m):
                dve.wait_ge(hid_hi, n + 1)
                dve.tensor_tensor(hidp[1][:, m % 4], hid[:, m % 4], whole(hidp[0][:, m % 4]),
                                  ALU.subtract).then_inc(hid_lo, 1)

            def pair_of_experts(e, last=False):
                for m in range(2 * HALVES):
                    n = e * HALVES + m
                    dve.wait_ge(relu2_ready, n + 1)
                    dve.wait_ge(up_filled, n + 1)
                    wait_count(dve, hid_ready, n - 1)
                    dve.tensor_tensor(prod[:, m % 2], up_bank[m % 2][:, :], relu2[:, m % 2],
                                      ALU.mult).then_inc(prod_ready, 1)
                    if m >= SPLIT_LAG or not starts(e):
                        lo(n - SPLIT_LAG, m - SPLIT_LAG)
                    if m % HALVES == 6 and not (last and m > HALVES):
                        i = m // HALVES
                        wait_count(dve, down_done, (e + i) * HALVES)
                        split_weights(e + i + 1, (i + 1) % 2)

            split_weights(0, 0)
            pair_of_experts(0)
            with dve.Fori(1, E0 // 2 - 1) as pair:
                e = 2 * pair
                pair_of_experts(e)
            pair_of_experts(E0 - 2, last=True)
            for m in range(2 * HALVES - SPLIT_LAG, 2 * HALVES):
                lo((E0 - 2) * HALVES + m, m)

        @block.tensor
        def _(pe):
            pe.wait_ge(zeros_set, 1)
            for g in range(NG):
                done = pe.matmul(acc[g][:, :], zeros[:, 0:P], zeros[:, :], start=True, stop=True)
            done.then_inc(acc_opened, 1)
            pe.wait_ge(lat_lo, NG)

            def up(n, m):
                i, g, j = m // HALVES, m % HALVES // HJ, m % HJ
                x = [t[:, g * GW:(g + 1) * GW] for t in latp]
                wait_count(pe, prod_ready, n - 1)
                product(pe, gate_bank[m % 2][:, :], [w[:, C_GATE + j * P:C_GATE + (j + 1) * P] for w in wp[i]],
                        x).then_inc(gate_filled, 1)
                product(pe, up_bank[m % 2][:, :], [w[:, C_UP + j * P:C_UP + (j + 1) * P] for w in wp[i]],
                        x).then_inc(up_filled, 1)

            def down(n, m):
                m = m % (2 * HALVES)
                i, g, j = m // HALVES, m % HALVES // HJ, m % HJ
                w = [t[:, C_DOWN + j * LAT:C_DOWN + (j + 1) * LAT] for t in wp[i]]
                pe.wait_ge(hid_lo, n + 1)
                h = [t[:, m % 4] for t in hidp]
                for a, b in ((0, 0), (0, 1), (1, 0)):
                    done = pe.matmul(acc[g][:, :], w[a][:, :], h[b], start=False, stop=False, skip_group_check=True)
                done.then_inc(down_done, 1)

            def pair_of_experts(e):
                for m in range(2 * HALVES):
                    n = e * HALVES + m
                    if m % HALVES == 0:
                        pe.wait_ge(w_lo, e + m // HALVES + 1)
                    up(n, m)
                    if m >= DOWN_LAG or not starts(e):
                        down(n - DOWN_LAG, m - DOWN_LAG)

            pair_of_experts(0)
            with pe.Fori(1, E0 // 2) as pair:
                e = 2 * pair
                pair_of_experts(e)
            for m in range(2 * HALVES - DOWN_LAG, 2 * HALVES):
                down((E0 - 2) * HALVES + m, m)


class Split:

    def __init__(self, mem, name, parts):
        self.parts = parts
        self.raw = mem.sb(name + "_raw", [P, len(parts), max(p[3] for p in parts)])
        self.first_loaded, self.rest_loaded = mem.sem(name + "_first_loaded"), mem.sem(name + "_rest_loaded")
        self.hi_ready, self.lo_ready = mem.sem(name + "_hi_ready"), mem.sem(name + "_lo_ready")

    def raw_part(self, n):
        _, hi, _, width = self.parts[n]
        flat = self.raw[:, n, 0:width]
        return flat.rearrange("p (k e) -> p k e", k=hi.shape[1]) if len(hi.shape) == 3 else flat

    def load(self, eng):
        for n, (src, hi, _, width) in enumerate(self.parts):
            out = self.raw_part(n) if len(src.shape) == 3 and len(hi.shape) == 3 else self.raw[:, n, 0:width]
            eng.dma_start(out, src).then_inc(self.rest_loaded if n else self.first_loaded, 16)

    def on_scalar(self, act, parts):
        for n in parts:
            if n == 0:
                act.wait_ge(self.first_loaded, 16)
            if n == 1:
                act.wait_ge(self.rest_loaded, 16 * (len(self.parts) - 1))
            act.activation(self.parts[n][1], self.raw_part(n), ACT.Copy).then_inc(self.hi_ready, 1)

    def on_pool(self, pool, parts):
        for n in parts:
            _, hi, lo, _ = self.parts[n]
            pool.wait_ge(self.hi_ready, n + 1)
            pool.tensor_tensor(lo, self.raw_part(n), whole(hi), ALU.subtract).then_inc(self.lo_ready, 1)


class Norm:

    def __init__(self, mem, name, eps, passed):
        self.eps, self.passed = eps, passed
        self.stats = mem.sb(name + "_stats", [P, GT, 6])
        self.meanvar = mem.sb(name + "_meanvar", [P, GT, 2])
        self.vareps = mem.sb(name + "_vareps", [P, GT])
        self.rstd = mem.sb(name + "_rstd", [P, GT])
        self.minus_half = mem.sb(name + "_minus_half", [P, GT])
        self.stats_ready, self.meanvar_ready = mem.sem(name + "_stats_ready"), mem.sem(name + "_meanvar_ready")
        self.half_set, self.vareps_ready = mem.sem(name + "_half_set"), mem.sem(name + "_vareps_ready")
        self.rstd_ready, self.normed = mem.sem(name + "_rstd_ready"), mem.sem(name + "_normed")

    def pool_start(self, pool):
        pool.memset(self.minus_half[:, :], -0.5).then_inc(self.half_set, 1)
        pool.wait_ge(self.half_set, 1)

    def on_pool(self, pool, n):
        wait_alone(pool, self.meanvar_ready, n * GT + GT, self.passed)
        pool.tensor_scalar(self.vareps[:, :], self.meanvar[:, :, 1], self.eps, None, ALU.add).then_inc(self.vareps_ready, 1)
        pool.wait_ge(self.vareps_ready, n + 1)
        wait_count(pool, self.normed, n * GT)
        pool.tensor_tensor(self.rstd[:, :], self.vareps[:, :], self.minus_half[:, :], ALU.pow).then_inc(self.rstd_ready, 1)

    def stats_on_vector(self, dve, n, i, row):
        dve.bn_stats(self.stats[:, i, :], row).then_inc(self.stats_ready, 1)

    def meanvar_on_vector(self, dve, n):
        for i in range(GT):
            wait_alone(dve, self.stats_ready, n * GT + i + 1, self.passed)
            dve.bn_aggr(self.meanvar[:, i, :], self.stats[:, i, :]).then_inc(self.meanvar_ready, 1)
        dve.wait_ge(self.rstd_ready, n + 1)

    def rows_on_vector(self, dve, i, row, out):
        dve.tensor_scalar(out, row, self.meanvar[:, i, 0:1], self.rstd[:, i:i + 1],
                          ALU.subtract, ALU.mult).then_inc(self.normed, 1)


def query_stage(nc, kept, io):
    FILLS = 2 * KD
    with ExitStack() as ctx:
        mem = Memory(nc, ctx)
        sb, sem = mem.sb, mem.sem
        w_up, w_head, w_gate = mem.pair("w_up0", [P, D]), mem.pair("w_head", [P, D]), mem.pair("w_ogate", [P, KD, D])
        split = Split(mem, "query_w",
                      [(io["wup_t"], w_up[0][:, :], w_up[1][:, :], D),
                       (io["heads"].rearrange("h p e -> p h e"), w_head[0][:, :], w_head[1][:, :], D)]
                      + [(io["wg"][k * P:(k + 1) * P, :], w_gate[0][:, k], w_gate[1][:, k], D) for k in range(KD)])
        norm = Norm(mem, "query_norm", LN_EPS, kept.passed)
        accp = mem.pair("accp", [P, GW])
        xn = sb("xn2", [P, 2, D])
        xnt = mem.pair("xn2t", [P, 2, KD, GW])
        row_bank = [mem.bank(f"row{i}") for i in range(2)]
        turn_bank = [mem.bank(f"turn2{i}") for i in range(2)]
        out_bank = [mem.bank(f"out2{i}") for i in range(4)]
        acc_hi, acc_lo = sem("accp_hi"), sem("accp_lo")
        row_filled, row_added = sem("row_filled"), sem("row_added")
        turned, hi_ready, lo_ready = sem("turned2"), sem("xn2t_hi"), sem("xn2t_lo")
        filled, read = sem("filled2"), sem("read2")
        block = ctx.enter_context(nc.Block())

        def by_chunk(ap):
            return ap.rearrange("p (c t) -> p c t", c=KD)

        def staggered(eng, sums, between, turns, outputs):
            def both(g):
                sums(g)
                outputs(g - 1, range(0, 6))
                turns(g)
                outputs(g - 1, range(6, FILLS))

            sums(0)
            between()
            turns(0)
            both(1)
            with eng.Fori(2, NG) as g:
                both(g)
            outputs(NG - 1, range(FILLS))

        @block.gpsimd
        def _(pool):
            norm.pool_start(pool)
            split.on_pool(pool, range(1))
            norm.on_pool(pool, 0)
            split.on_pool(pool, range(1, len(split.parts)))
            norm.on_pool(pool, 1)
            with pool.Fori(2, NG) as g:
                norm.on_pool(pool, g)

        @block.sync
        def _(sp):
            split.load(sp)

        @block.scalar
        def _(act):
            def sums(g):
                wait_count(act, row_filled, g * GT)
                act.activation(accp[0][:, :], kept.latent[:, bass.ds(g * GW, GW)], ACT.Copy).then_inc(acc_hi, 1)

            def turned_rows(g):
                for i in range(GT):
                    act.wait_ge(turned, g * GT + i + 1)
                    act.activation(xnt[0][:, g % 2, :, i * P:(i + 1) * P], by_chunk(turn_bank[i % 2][:, :]),
                                   ACT.Copy).then_inc(hi_ready, 1)

            def outputs(g, fills):
                part = bass.ds(g * GW, GW)
                for m in fills:
                    act.wait_ge(filled, g * FILLS + m + 1)
                    out = kept.queries[:, m, part] if m < KD else kept.ogate[:, m - KD, part]
                    act.activation(out, out_bank[m % 4][:, :], ACT.Copy if m < KD else ACT.Relu).then_inc(read, 1)

            split.on_scalar(act, range(1))
            staggered(act, sums, lambda: split.on_scalar(act, range(1, len(split.parts))), turned_rows, outputs)

        @block.vector
        def _(dve):
            def rows(g):
                dve.wait_ge(acc_hi, g + 1)
                dve.tensor_tensor(accp[1][:, :], kept.latent[:, bass.ds(g * GW, GW)], whole(accp[0][:, :]),
                                  ALU.subtract).then_inc(acc_lo, 1)
                for i in range(GT):
                    row = kept.x[:, g * GT + i, :]
                    dve.wait_ge(row_filled, g * GT + i + 1)
                    dve.tensor_tensor(row, row, row_bank[i % 2][:, :], ALU.add).then_inc(row_added, 1)
                    if i > 0:
                        wait_alone(dve, row_added, g * GT + i, kept.passed)
                        norm.stats_on_vector(dve, g, i - 1, kept.x[:, g * GT + i - 1, :])
                wait_alone(dve, row_added, g * GT + GT, kept.passed)
                norm.stats_on_vector(dve, g, GT - 1, kept.x[:, g * GT + GT - 1, :])
                norm.meanvar_on_vector(dve, g)
                for i in range(GT):
                    wait_count(dve, turned, g * GT + i - 1)
                    norm.rows_on_vector(dve, i, kept.x[:, g * GT + i, :], xn[:, i % 2, :])
                for i in range(GT):
                    part = slice(i * P, (i + 1) * P)
                    dve.wait_ge(hi_ready, g * GT + i + 1)
                    dve.tensor_tensor(xnt[1][:, g % 2, :, part], by_chunk(turn_bank[i % 2][:, :]),
                                      whole(xnt[0][:, g % 2, :, part]), ALU.subtract).then_inc(lo_ready, 1)

            rows(0)
            with dve.Fori(1, NG) as g:
                rows(g)

        @block.tensor
        def _(pe):
            pe.wait_ge(split.lo_ready, 1)

            def sums(g):
                pe.wait_ge(acc_lo, g + 1)
                for i in range(GT):
                    wait_count(pe, row_added, g * GT + i - 1)
                    product(pe, row_bank[i % 2][:, :], [a[:, i * P:(i + 1) * P] for a in accp],
                            [w[:, :] for w in w_up]).then_inc(row_filled, 1)

            def turns(g):
                for i in range(GT):
                    pe.wait_ge(norm.normed, g * GT + i + 1)
                    wait_count(pe, lo_ready, g * GT + i - 1)
                    for c in range(KD):
                        done = pe.transpose(turn_bank[i % 2][:, c * P:(c + 1) * P], xn[:, i % 2, c * P:(c + 1) * P],
                                            kept.ident[:, :])
                    done.then_inc(turned, 1)

            def outputs(g, fills):
                pe.wait_ge(lo_ready, g * GT + GT)
                pe.wait_ge(split.lo_ready, len(split.parts))
                for m in fills:
                    wait_count(pe, read, g * FILLS + m - 3)
                    if m < KD:
                        done = product(pe, out_bank[m % 4][:, :], [w[:, m * P:(m + 1) * P] for w in w_head],
                                       [x[:, g % 2, m, :] for x in xnt])
                    else:
                        for k in range(KD):
                            col = (m - KD) * P
                            done = product(pe, out_bank[m % 4][:, :], [w[:, k, col:col + P] for w in w_gate],
                                           [x[:, g % 2, k, :] for x in xnt], first=(k == 0), last=(k == KD - 1))
                    done.then_inc(filled, 1)

            staggered(pe, sums, lambda: None, turns, outputs)


def attention_stage(nc, kept, io):
    H2 = S // 2
    MASKED = S + H2
    with ExitStack() as ctx:
        mem = Memory(nc, ctx)
        sb, sem = mem.sb, mem.sem
        mask = sb("mask", [P, KD, MASKED])
        w_raw = sb("head_raw", [P, D])
        w_all = mem.pair("head_w_all", [P, D])
        w_head = mem.pair("head_w", [P, P])
        ctx_raw = sb("ctx_raw", [P, T])
        ctxp = mem.pair("ctxp", [P, T])
        keys = sb("keys", [P, T])
        keyp = mem.pair("keyp", [P, T])
        queryp = mem.pair("queryp", [P, T])
        valuep = mem.pair("valuep", [P, 2, B, P])
        scores = sb("scores", [P, MASKED])
        att = sb("att", [P, MASKED])
        attp = mem.pair("attp", [P, 2, S])
        key_bank = [mem.bank(f"key{i}") for i in range(2)]
        value_bank = [mem.bank(f"value{i}") for i in range(2)]
        score_bank = [mem.bank(f"score{i}") for i in range(2)]
        o_bank = [mem.bank(f"o{i}") for i in range(2)]
        mask_loaded, w_loaded, w_hi, w_lo, w_slot = (sem("mask_loaded"), sem("head_w_loaded"), sem("head_w_hi"),
                                                     sem("head_w_lo"), sem("head_w_slot"))
        ctx_loaded, ctx_hi, ctx_lo = sem("ctx3_loaded"), sem("ctx3_hi"), sem("ctx3_lo")
        key_filled, keys_read, key_hi, key_lo = sem("key_filled"), sem("keys_read"), sem("key_hi"), sem("key_lo")
        query_hi, query_lo = sem("query_hi"), sem("query_lo")
        value_turned, value_hi, value_lo = sem("value_turned"), sem("value_hi"), sem("value_lo")
        scored, masked, att_ready, att_hi, att_lo = (sem("scored"), sem("masked"), sem("att_ready"),
                                                     sem("att_hi"), sem("att_lo"))
        ones_set, o_filled, o_read = sem("att_ones_set"), sem("o_filled"), sem("o_read")
        block = ctx.enter_context(nc.Block())

        def part(g):
            return slice(g * GW, (g + 1) * GW)

        @block.sync
        def _(sp):
            sp.dma_start(w_raw[:, :].rearrange("p (h e) -> p h e", h=KD), io["heads"].rearrange("h p e -> p h e")
                         ).then_inc(w_loaded, 16)
            sp.dma_start(ctx_raw[:, :], io["ctx_t"][0:P, :]).then_inc(ctx_loaded, 16)
            sp.dma_start(mask[:, :, :], io["mask"]).then_inc(mask_loaded, 16)
            with sp.Fori(1, KD) as h:
                sp.wait_ge(ctx_lo, h * NG)
                sp.dma_start(ctx_raw[:, :], io["ctx_t"][bass.ds(h * P, P), :]).then_inc(ctx_loaded, 16)

        @block.gpsimd
        def _(pool):
            pool.memset(attp[0][:, 1, 0:H2].bitcast(F32), 1.0)
            pool.memset(attp[1][:, 1, 0:H2].bitcast(F32), 0.0).then_inc(ones_set, 1)
            pool.wait_ge(w_hi, 1)
            pool.tensor_tensor(w_all[1][:, :], w_raw[:, :], whole(w_all[0][:, :]), ALU.subtract).then_inc(w_lo, 1)
            pool.wait_ge(w_lo, 1)

            def place_weights(h):
                wait_count(pool, key_filled, h * NG)
                for n in range(2):
                    pool.tensor_copy(w_head[n][:, :], whole(w_all[n][:, bass.ds(h * P, P)])).then_inc(w_slot, 1)

            place_weights(0)
            with pool.Fori(1, KD) as h:
                place_weights(h)

        @block.scalar
        def _(act):
            act.wait_ge(w_loaded, 16)
            act.activation(w_all[0][:, :], w_raw[:, :], ACT.Copy).then_inc(w_hi, 1)

            def ctx_parts(h):
                act.wait_ge(ctx_loaded, h * 16 + 16)
                wait_count(act, key_filled, h * NG)
                for g in range(NG):
                    act.activation(ctxp[0][:, part(g)], ctx_raw[:, part(g)], ACT.Copy).then_inc(ctx_hi, 1)

            def read_keys(h):
                for g in range(NG):
                    act.wait_ge(key_filled, h * NG + g + 1)
                    if g == 0:
                        wait_count(act, value_turned, h * NG)
                        wait_count(act, key_lo, h * NG)
                    act.activation(keys[:, part(g)], key_bank[g % 2][:, :], ACT.Copy).then_inc(keys_read, 1)

            def queries(h):
                wait_count(act, scored, h * 2)
                for g in range(NG):
                    act.activation(queryp[0][:, part(g)], kept.queries[:, h, part(g)], ACT.Copy).then_inc(query_hi, 1)

            def values(h):
                for g in range(NG):
                    act.wait_ge(value_turned, h * NG + g + 1)
                    if g == 0:
                        wait_count(act, o_filled, h * 4)
                    act.activation(valuep[0][:, :, 2 * g:2 * g + 2, :].rearrange("p t b d -> p b t d"),
                                   value_bank[g % 2][:, :].rearrange("p (b t d) -> p b t d", b=2, t=2),
                                   ACT.Copy).then_inc(value_hi, 1)

            def outputs(h):
                act.wait_ge(query_lo, h * NG + NG)
                for n in range(4):
                    s, half = n // 2, n % 2
                    act.wait_ge(o_filled, h * 4 + n + 1)
                    act.activation(kept.queries[:, h, :].rearrange("p (b s d) -> p b s d", s=2, d=P)[:, 4 * half:4 * half + 4, s, :],
                                   o_bank[n % 2][:, :].rearrange("p (b d) -> p b d", b=4), ACT.Copy).then_inc(o_read, 1)

            def head(h, more):
                values(h)
                if more:
                    ctx_parts(h + 1)
                    read_keys(h + 1)
                    outputs(h)
                    queries(h + 1)
                else:
                    outputs(h)

            ctx_parts(0)
            queries(0)
            read_keys(0)
            head(0, True)
            with act.Fori(1, KD - 1) as h:
                head(h, True)
            head(KD - 1, False)

        @block.vector
        def _(dve):
            def ctx_parts(h):
                for g in range(NG):
                    dve.wait_ge(ctx_hi, h * NG + g + 1)
                    dve.tensor_tensor(ctxp[1][:, part(g)], ctx_raw[:, part(g)], whole(ctxp[0][:, part(g)]),
                                      ALU.subtract).then_inc(ctx_lo, 1)

            def split_keys(h):
                wait_count(dve, scored, h * 2)
                for g in range(NG):
                    dve.wait_ge(keys_read, h * NG + g + 1)
                    dve.tensor_copy(keyp[0][:, part(g)], keys[:, part(g)]).then_inc(key_hi, 1)
                for g in range(NG):
                    dve.wait_ge(key_hi, h * NG + g + 1)
                    dve.tensor_tensor(keyp[1][:, part(g)], keys[:, part(g)], whole(keyp[0][:, part(g)]),
                                      ALU.subtract).then_inc(key_lo, 1)

            def queries(h):
                for g in range(NG):
                    dve.wait_ge(query_hi, h * NG + g + 1)
                    dve.tensor_tensor(queryp[1][:, part(g)], kept.queries[:, h, part(g)], whole(queryp[0][:, part(g)]),
                                      ALU.subtract).then_inc(query_lo, 1)

            def values(h):
                for g in range(NG):
                    dve.wait_ge(value_hi, h * NG + g + 1)
                    for b in range(2):
                        done = dve.tensor_tensor(valuep[1][:, :, 2 * g + b, :],
                                                 value_bank[g % 2][:, b * S:(b + 1) * S].rearrange("p (t d) -> p t d", t=2),
                                                 whole(valuep[0][:, :, 2 * g + b, :]), ALU.subtract)
                    done.then_inc(value_lo, 1)

            def attention(h):
                for t, (a, b) in enumerate(((0, S), (S, MASKED))):
                    n = 2 * h + t
                    place = (slice(None), t, slice(H2 * t, S))
                    dve.wait_ge(scored, n + 1)
                    dve.tensor_tensor(scores[:, a:b], score_bank[t][:, 0:b - a], mask[:, h, a:b], ALU.mult).then_inc(masked, 1)
                    dve.wait_ge(masked, n + 1)
                    dve.scalar_tensor_tensor(att[:, a:b], scores[:, a:b], -1.0, scores[:, a:b], ALU.mult, ALU.max
                                             ).then_inc(att_ready, 1)
                    dve.wait_ge(att_ready, n + 1)
                    dve.tensor_scalar(attp[0][place], att[:, a:b], 1.0, None, ALU.max).then_inc(att_hi, 1)
                    dve.wait_ge(att_hi, n + 1)
                    dve.scalar_tensor_tensor(attp[1][place], att[:, a:b], 1.0, whole(attp[0][place]),
                                             ALU.max, ALU.subtract).then_inc(att_lo, 1)

            def head(h, more):
                values(h)
                if more:
                    ctx_parts(h + 1)
                wait_count(dve, o_filled, h * 4)
                attention(h)
                if more:
                    split_keys(h + 1)
                    queries(h + 1)

            dve.wait_ge(mask_loaded, 16)
            ctx_parts(0)
            queries(0)
            split_keys(0)
            head(0, True)
            with dve.Fori(1, KD - 1) as h:
                head(h, True)
            head(KD - 1, False)

        @block.tensor
        def _(pe):
            pe.wait_ge(ones_set, 1)

            def make_keys(h):
                pe.wait_ge(w_slot, h * 2 + 2)
                for g in range(NG):
                    pe.wait_ge(ctx_lo, h * NG + g + 1)
                    wait_count(pe, keys_read, h * NG + g - 1)
                    product(pe, key_bank[g % 2][:, :], [w[:, :] for w in w_head],
                            [c[:, part(g)] for c in ctxp]).then_inc(key_filled, 1)

            def head(h, more):
                for g in range(NG):
                    pe.wait_ge(keys_read, h * NG + g + 1)
                    wait_count(pe, value_lo, h * NG + g - 1)
                    for i in range(GT):
                        col = g * GW + i * P
                        done = pe.transpose(value_bank[g % 2][:, i * P:(i + 1) * P], keys[:, col:col + P], kept.ident[:, :])
                    done.then_inc(value_turned, 1)
                pe.wait_ge(key_lo, h * NG + NG)
                pe.wait_ge(query_lo, h * NG + NG)
                wait_count(pe, masked, h * 2)
                for t in range(2):
                    for b in range(B):
                        k, q = b * S + t * H2, b * S + t * H2
                        done = product(pe, score_bank[t][:, 0:S - t * H2], [w[:, k:k + P] for w in keyp],
                                       [x[:, q:(b + 1) * S] for x in queryp], first=(b == 0), last=(b == B - 1))
                    done.then_inc(scored, 1)
                if more:
                    make_keys(h + 1)
                pe.wait_ge(value_lo, h * NG + NG)
                pe.wait_ge(att_lo, h * 2 + 2)
                for n in range(4):
                    s, half = n // 2, n % 2
                    wait_count(pe, o_read, h * 4 + n - 1)
                    for t in range(2):
                        done = product(pe, o_bank[n % 2][:, :], [a[:, t, s * P:(s + 1) * P] for a in attp],
                                       [v[:, t, 4 * half:4 * half + 4, :] for v in valuep], first=(t == 0), last=(t == 1))
                    done.then_inc(o_filled, 1)

            make_keys(0)
            head(0, True)
            with pe.Fori(1, KD - 1) as h:
                head(h, True)
            head(KD - 1, False)


def output_stage(nc, kept, io):
    GN_EPS = 1e-3
    with ExitStack() as ctx:
        mem = Memory(nc, ctx)
        sb, sem = mem.sb, mem.sem
        w_out = mem.pair("w_out", [P, KD, D])
        split = Split(mem, "out_w", [(io["wo"][k * P:(k + 1) * P, :], w_out[0][:, k], w_out[1][:, k], D) for k in range(KD)])
        norm = Norm(mem, "out_norm", GN_EPS, kept.passed)
        gamma_beta = sb("gamma_beta", [P, 2, KD])
        yn = sb("yn", [P, GT, D])
        yt = sb("yt", [P, 2, GW])
        z = sb("z", [P, 2, GW])
        zp = [mem.pair(f"zp{i}", [P, KD, GW]) for i in range(2)]
        turn_bank = [mem.bank(f"turn4{c}") for c in range(KD)]
        row_bank = [mem.bank(f"row4{i}") for i in range(4)]
        small_loaded = sem("gamma_loaded")
        turned, y_read, z_ready, z_hi, z_lo = sem("turned4"), sem("y_read"), sem("z_ready"), sem("z_hi"), sem("z_lo")
        row_filled, row_added = sem("row4_filled"), sem("row4_added")
        block = ctx.enter_context(nc.Block())

        def out_row(g, i):
            return kept.queries[:, :, bass.ds(g * GW + i * P, P)]

        @block.gpsimd
        def _(pool):
            norm.pool_start(pool)
            norm.on_pool(pool, 0)
            split.on_pool(pool, range(len(split.parts)))
            norm.on_pool(pool, 1)
            with pool.Fori(2, NG) as g:
                norm.on_pool(pool, g)

        @block.sync
        def _(sp):
            split.load(sp)

        @block.scalar
        def _(act):
            act.dma_start(gamma_beta[:, :, :], io["gamma_beta"]).then_inc(small_loaded, 16)
            split.on_scalar(act, range(len(split.parts)))
            act.wait_ge(small_loaded, 16)

            def gated(g, slot):
                for c in range(KD):
                    n = g * KD + c
                    act.wait_ge(turned, n + 1)
                    wait_count(act, z_ready, n - 1)
                    act.activation(yt[:, c % 2], turn_bank[c][:, :], ACT.Identity, scale=gamma_beta[:, 0, c:c + 1],
                                   bias=gamma_beta[:, 1, c:c + 1]).then_inc(y_read, 1)
                    act.wait_ge(z_ready, n + 1)
                    if c == 0:
                        wait_count(act, row_filled, g * GT - GT)
                    act.activation(zp[slot][0][:, c], z[:, c % 2], ACT.Copy).then_inc(z_hi, 1)

            for g in range(NG):
                gated(g, g % 2)

        @block.vector
        def _(dve):
            def norms(g):
                for i in range(GT):
                    norm.stats_on_vector(dve, g, i, out_row(g, i))
                norm.meanvar_on_vector(dve, g)
                wait_count(dve, turned, g * KD)
                for i in range(GT):
                    norm.rows_on_vector(dve, i, out_row(g, i), yn[:, i, :].rearrange("p (h d) -> p h d", h=KD))

            def gated(g, slot):
                for c in range(KD):
                    n = g * KD + c
                    dve.wait_ge(y_read, n + 1)
                    dve.tensor_tensor(z[:, c % 2], yt[:, c % 2], kept.ogate[:, c, bass.ds(g * GW, GW)], ALU.mult
                                      ).then_inc(z_ready, 1)
                    dve.wait_ge(z_hi, n + 1)
                    dve.tensor_tensor(zp[slot][1][:, c], z[:, c % 2], whole(zp[slot][0][:, c]), ALU.subtract).then_inc(z_lo, 1)

            def rows(g):
                for i in range(GT):
                    row = kept.x[:, g * GT + i, :]
                    dve.wait_ge(row_filled, g * GT + i + 1)
                    dve.tensor_tensor(row, row, row_bank[i][:, :], ALU.add).then_inc(row_added, 1)

            def step(g, slot):
                norms(g + 1)
                gated(g, slot)
                rows(g - 1)

            norms(0)
            norms(1)
            gated(0, 0)
            step(1, 1)
            step(2, 0)
            gated(NG - 1, 1)
            rows(NG - 2)
            rows(NG - 1)

        @block.tensor
        def _(pe):
            def turns(g):
                pe.wait_ge(norm.normed, g * GT + GT)
                for c in range(KD):
                    wait_count(pe, y_read, (g - 1) * KD + c + 1)
                    for i in range(GT):
                        done = pe.transpose(turn_bank[c][:, i * P:(i + 1) * P], yn[:, i, c * P:(c + 1) * P], kept.ident[:, :])
                    done.then_inc(turned, 1)

            def rows(g):
                pe.wait_ge(z_lo, g * KD + KD)
                for i in range(GT):
                    wait_count(pe, row_added, g * GT - GT + i + 1)
                    for k in range(KD):
                        done = product(pe, row_bank[i][:, :], [x[:, k, i * P:(i + 1) * P] for x in zp[g % 2]],
                                       [w[:, k] for w in w_out], first=(k == 0), last=(k == KD - 1))
                    done.then_inc(row_filled, 1)

            pe.wait_ge(split.lo_ready, KD)
            turns(0)
            for g in range(NG):
                if g + 1 < NG:
                    turns(g + 1)
                rows(g)


def router_stage(nc, kept, io):
    NH = 2 * HID // P
    with ExitStack() as ctx:
        mem = Memory(nc, ctx)
        sb, sem = mem.sb, mem.sem
        w_route, w_up, w_down = mem.pair("w_route", [P, KD, P]), mem.pair("w_shup", [P, KD, D]), mem.pair("w_shdown", [P, NH, D])
        split = Split(mem, "shared_w",
                      [(io["w_router"].rearrange("(k p) e -> p k e", p=P), w_route[0][:, :, 0:E1], w_route[1][:, :, 0:E1], KD * E1)]
                      + [(io["wsh_up"][k * P:(k + 1) * P, :], w_up[0][:, k], w_up[1][:, k], D) for k in range(KD)]
                      + [(io["wsh_down"][j * P:(j + 1) * P, :], w_down[0][:, j], w_down[1][:, j], D) for j in range(NH)])
        norm = Norm(mem, "route_norm", LN_EPS, kept.passed)
        xn = sb("xn3", [P, 2, D])
        xnt = mem.pair("xn3t", [P, KD, T])
        hid = sb("hid5", [P, 2, GW])
        hidp = mem.pair("hid5p", [P, NH, GW])
        logit_t = sb("logit5_t", [E1, GW])
        logits = sb("logits5", [P, NT, E1])
        peak, total_exp = sb("peak", [P, NT]), sb("total_exp", [P, NT])
        probs = sb("probs5", [P, NT, E1])
        top8, index8 = sb("top8_5", [P, NT, 8]), sb("index8", [P, NT, 8], U32)
        expert_no, slot_no, lane_no = sb("expert_no", [P, E1]), sb("slot_no", [P, SLOTS]), sb("lane_no", [P, P])
        tile_ends, tile_no, row_no = sb("tile_ends", [P, NT + 1]), sb("tile_no", [P, NT]), sb("row_no", [P, 1])
        keep = sb("keep", [P, E1, NT])
        before_me, all_ones = sb("before_me", [P, P], BF16), sb("all_ones", [P, P], BF16)
        choice = sb("choice", [P, 2, NT])
        picked = sb("picked", [P, 2, NT, E1])
        member = sb("member", [P, NT, E1], BF16)
        counts = sb("counts", [P, E1, NT])
        base = sb("base", [P, NT, E1])
        wide = sb("wide", [P, SLOTS, E1])
        tiles, slot_end, slot_start = sb("tiles5", [P, E1]), sb("slot_end", [P, E1]), sb("slot_start", [P, E1])
        slot_of = sb("slot_of", [P, SLOTS])
        rank, first, skip, lane = (sb(n, [P, 2, NT]) for n in ("rank", "first_slot", "skip_slots", "lane"))
        lane_hot = sb("lane_hot", [P, 2, NT, P], BF16)
        slot_ids = sb("slot_ids", [P, 2, NT, 2, SLOTS], BF16)
        id_part = sb("id_part", [P, SLOTS])

        turn_bank = [mem.bank(f"turn5{i}") for i in range(2)]
        logit_bank, plan_bank = mem.bank("logit5"), mem.bank("plan5")
        up_bank = [mem.bank(f"up5{i}") for i in range(2)]
        row_bank = [mem.bank(f"row5{i}") for i in range(2)]
        set_pool, set_dve = sem("set5_pool"), sem("set5_dve")
        row_stored = [sem("row_stored_even"), sem("row_stored_odd")]
        turned, hi_ready, lo_ready = sem("turned5"), sem("xn3t_hi"), sem("xn3t_lo")
        logit_filled, logit_read = sem("logit_filled"), sem("logit_read")
        logit_turned, logits_ready = sem("logit_turned"), sem("logits_ready")
        up_filled, gelu_ready, hid_hi, hid_lo = sem("up5_filled"), sem("gelu_ready"), sem("hid5_hi"), sem("hid5_lo")
        row_filled, row_added = sem("row5_filled"), sem("row5_added")
        shifted, exped, plan = sem("shifted"), sem("exped"), sem("plan_steps")
        member_ready, counted, ids_hot, ids_filled = sem("member_ready"), sem("counted"), sem("ids_hot"), sem("ids_filled")
        block = ctx.enter_context(nc.Block())

        def by_chunk(ap):
            return ap.rearrange("p (c t) -> p c t", c=KD)

        def flat(ap):
            return ap.rearrange("p a b -> p (a b)")

        def staggered(ahead, logits_part, shared_part):
            for g in range(NG + 1):
                if g < NG:
                    ahead(g)
                if g > 0:
                    logits_part(g - 1)
                if 2 <= g < NG:
                    shared_part(g - 2)

        @block.sync
        def _(sp):
            rows = kept.xn_dram.rearrange("(n p) d -> p n d", p=P)
            with sp.Fori(0, NT // 2) as pair:
                for i in range(2):
                    j = 2 * pair
                    sp.wait_ge(norm.normed, j + i + 1)
                    sp.dma_start(rows[:, bass.ds(j + i, 1), :].rearrange("p n d -> p (n d)"), xn[:, i, :]
                                 ).then_inc(row_stored[i], 16)
            for i in range(2):
                sp.wait_ge(row_stored[i], 16 * (NT // 2))

        @block.gpsimd
        def _(pool):
            norm.pool_start(pool)
            for tile, pattern, base_value, per_partition in (
                    (expert_no[:, :], [[1, E1]], 0, 0), (slot_no[:, :], [[1, SLOTS]], 0, 0),
                    (lane_no[:, :], [[1, P]], 0, 0), (tile_ends[:, :], [[P, NT + 1]], 0, 0),
                    (tile_no[:, :], [[1, NT]], 0, 0), (row_no[:, :], [[1, 1]], 0, 1)):
                pool.iota(tile, pattern, base=base_value, channel_multiplier=per_partition,
                          allow_small_or_imprecise_dtypes=True)
            pool.memset(keep[:, :, :], 1.0)
            pool.memset(all_ones[:, :], 1.0).then_inc(set_pool, 1)
            pool.wait_ge(set_pool, 1)
            pool.memset(keep[:, :, 0:1], 0.0)
            pool.affine_select(out=before_me[:, :], in_=kept.ones[:, :], pattern=[[1, P]], compare_op=ALU.is_gt,
                               fill=0.0, base=0, channel_multiplier=-1).then_inc(set_pool, 1)
            norm.on_pool(pool, 0)
            split.on_pool(pool, range(1 + KD))
            norm.on_pool(pool, 1)
            split.on_pool(pool, range(1 + KD, len(split.parts)))
            with pool.Fori(2, NG) as g:
                norm.on_pool(pool, g)

        @block.scalar
        def _(act):
            split.load(act)
            split.on_scalar(act, range(len(split.parts)))

            def ahead(g):
                for i in range(GT):
                    act.wait_ge(turned, g * GT + i + 1)
                    act.activation(xnt[0][:, :, bass.ds(g * GW + i * P, P)], by_chunk(turn_bank[i % 2][:, :]),
                                   ACT.Copy).then_inc(hi_ready, 1)

            def logits_part(g):
                act.wait_ge(logit_filled, g + 1)
                wait_count(act, logit_turned, g)
                act.activation(logit_t[:, :], logit_bank[0:E1, :], ACT.Copy).then_inc(logit_read, 1)
                act.wait_ge(logit_turned, g + 1)
                act.activation(flat(logits[:, bass.ds(g * GT, GT), :]), plan_bank[:, 0:GT * E1], ACT.Copy
                               ).then_inc(logits_ready, 1)

            def shared_part(g):
                for j in range(NH):
                    n = g * NH + j
                    act.wait_ge(up_filled, n + 1)
                    wait_count(act, hid_lo, n - 1)
                    act.activation(hid[:, j % 2], up_bank[j % 2][:, :], ACT.Gelu).then_inc(gelu_ready, 1)
                    act.wait_ge(gelu_ready, n + 1)
                    if j == 0:
                        wait_count(act, row_filled, g * GT)
                    act.activation(hidp[0][:, j], hid[:, j % 2], ACT.Copy).then_inc(hid_hi, 1)

            staggered(ahead, logits_part, shared_part)
            act.wait_ge(shifted, 1)
            act.activation(flat(probs[:, :, :]), flat(logits[:, :, :]), ACT.Exp).then_inc(exped, 1)
            shared_part(NG - 2)
            shared_part(NG - 1)

        @block.vector
        def _(dve):
            for part in w_route:
                dve.memset(part[:, :, E1:P].bitcast(F32), 0.0).then_inc(set_dve, 1)

            def ahead(g):
                for i in range(GT):
                    norm.stats_on_vector(dve, g, i, kept.x[:, g * GT + i, :])
                norm.meanvar_on_vector(dve, g)
                for i in range(GT):
                    wait_count(dve, turned, g * GT + i - 1)
                    if i > 1:
                        dve.wait_ge(row_stored[i % 2], 16 * 2 * g + 16)
                    else:
                        wait_count(dve, row_stored[i % 2], 16 * 2 * g)
                    norm.rows_on_vector(dve, i, kept.x[:, g * GT + i, :], xn[:, i % 2, :])
                for i in range(GT):
                    part = bass.ds(g * GW + i * P, P)
                    dve.wait_ge(hi_ready, g * GT + i + 1)
                    dve.tensor_tensor(xnt[1][:, :, part], by_chunk(turn_bank[i % 2][:, :]), whole(xnt[0][:, :, part]),
                                      ALU.subtract).then_inc(lo_ready, 1)

            def shared_part(g):
                for j in range(NH):
                    n = g * NH + j
                    dve.wait_ge(hid_hi, n + 1)
                    dve.tensor_tensor(hidp[1][:, j], hid[:, j % 2], whole(hidp[0][:, j]), ALU.subtract).then_inc(hid_lo, 1)
                for i in range(GT):
                    row = kept.x[:, g * GT + i, :]
                    dve.wait_ge(row_filled, g * GT + i + 1)
                    dve.tensor_tensor(row, row, row_bank[i % 2][:, :], ALU.add).then_inc(row_added, 1)

            step = Ticks(plan)

            def on(ins):
                dve.wait_ge(plan, step.tick(ins))

            def along(ap, n, axis):
                shape = list(ap.shape)
                shape.insert(axis, n)
                return ap.unsqueeze(axis).to_broadcast(shape)

            def choose():
                dve.wait_ge(logits_ready, NG)
                on(dve.tensor_reduce(peak[:, :], logits[:, :, :], AX_X, ALU.max))
                dve.tensor_tensor(logits[:, :, :], logits[:, :, :], along(peak[:, :], E1, 2), ALU.subtract).then_inc(shifted, 1)
                dve.wait_ge(exped, 1)
                on(dve.tensor_reduce(total_exp[:, :], probs[:, :, :], AX_X, ALU.add))
                on(dve.reciprocal(total_exp[:, :], total_exp[:, :]))
                on(dve.tensor_tensor(probs[:, :, :], probs[:, :, :], along(total_exp[:, :], E1, 2), ALU.mult))
                for j in range(NT):
                    last = step.tick(dve.max(top8[:, j], probs[:, j]))
                for j in range(NT):
                    dve.wait_ge(plan, last - NT + 1 + j)
                    found = step.tick(dve.max_index(index8[:, j], top8[:, j], probs[:, j]))
                step.tick(dve.tensor_copy(kept.route_gate[:, :, :], top8[:, :, 0:2].rearrange("p j c -> p c j")))
                dve.wait_ge(plan, found)
                on(dve.tensor_copy(choice[:, :, :], index8[:, :, 0:2].rearrange("p j c -> p c j")))
                dve.wait_ge(set_pool, 2)
                for c in range(2):
                    last = step.tick(dve.tensor_tensor(picked[:, c], along(expert_no[:, :], NT, 1),
                                                       along(choice[:, c], E1, 2), ALU.is_equal))
                dve.wait_ge(plan, last)
                dve.tensor_tensor(member[:, :, :], picked[:, 0], picked[:, 1], ALU.add).then_inc(member_ready, 1)

            def place():
                before = plan_bank[:, 0:NT * E1].rearrange("p (j e) -> p j e", j=NT)
                total = plan_bank[:, NT * E1:2 * NT * E1].rearrange("p (j e) -> p j e", j=NT)
                dve.wait_ge(counted, 1)
                on(dve.tensor_copy(counts[:, :, :], total.rearrange("p j e -> p e j")))
                on(dve.tensor_tensor_scan(flat(counts[:, :, :]), flat(keep[:, :, :]), flat(counts[:, :, :]), 0.0,
                                          ALU.mult, ALU.add))
                on(dve.tensor_tensor(base[:, :, :], counts[:, :, :].rearrange("p e j -> p j e"), total, ALU.subtract))
                on(dve.tensor_tensor(base[:, :, :], base[:, :, :], before, ALU.add))
                on(dve.tensor_tensor(wide[:, 0:E1, :], along(counts[:, :, NT - 1], NT, 2), along(tile_ends[:, 0:NT], E1, 1),
                                     ALU.is_gt))
                on(dve.tensor_reduce(tiles[:, :], wide[:, 0:E1, :], AX_X, ALU.add))
                on(dve.tensor_tensor_scan(slot_end[:, :], all_ones[:, 0:E1], tiles[:, :], 0.0, ALU.mult, ALU.add))
                on(dve.tensor_tensor(slot_start[:, :], slot_end[:, :], tiles[:, :], ALU.subtract))
                on(dve.tensor_tensor(wide[:, :, :], along(slot_end[:, :], SLOTS, 1), along(slot_no[:, :], E1, 2), ALU.is_le))
                on(dve.tensor_reduce(slot_of[:, :], wide[:, :, :], AX_X, ALU.add))
                on(dve.tensor_scalar(kept.slot_expert[:, :], slot_of[:, :], float(E1 - 1), None, ALU.min))
                for c in range(2):
                    part = wide[:, 16 * c:16 * c + NT, :]
                    on(dve.tensor_tensor(part, picked[:, c], base[:, :, :], ALU.mult))
                    on(dve.tensor_reduce(rank[:, c], part, AX_X, ALU.add))
                    on(dve.tensor_tensor(part, picked[:, c], along(slot_start[:, :], NT, 1), ALU.mult))
                    on(dve.tensor_reduce(first[:, c], part, AX_X, ALU.add))
                    on(dve.tensor_tensor(part, along(rank[:, c], NT, 2), along(tile_ends[:, 1:NT + 1], NT, 1), ALU.is_ge))
                    on(dve.tensor_reduce(skip[:, c], part, AX_X, ALU.add))
                on(dve.tensor_tensor(first[:, :, :], first[:, :, :], skip[:, :, :], ALU.add))
                on(dve.scalar_tensor_tensor(lane[:, :, :], skip[:, :, :], float(-P), rank[:, :, :], ALU.mult, ALU.add))
                on(dve.scalar_tensor_tensor(kept.route_row[:, :, :], first[:, :, :], float(P), lane[:, :, :],
                                            ALU.mult, ALU.add))
                for c in range(2):
                    step.tick(dve.tensor_tensor(lane_hot[:, c], along(lane_no[:, :], NT, 1), along(lane[:, c], P, 2),
                                                ALU.is_equal))
                    slot_hot = slot_ids[:, c, :, 1, :]
                    on(dve.tensor_tensor(slot_hot, along(slot_no[:, :], NT, 1), along(first[:, c], SLOTS, 2), ALU.is_equal))
                    on(dve.tensor_scalar(slot_ids[:, c, :, 0, :], slot_hot, row_no[:, 0:1], None, ALU.mult))
                    dve.tensor_tensor(slot_hot, slot_hot, along(tile_no[:, :], SLOTS, 2), ALU.mult).then_inc(ids_hot, 1)

            staggered(ahead, lambda g: None, shared_part)
            choose()
            shared_part(NG - 2)
            place()
            shared_part(NG - 1)
            dve.wait_ge(ids_filled, 1)
            on(dve.tensor_copy(id_part[:, :], plan_bank[:, 0:SLOTS]))
            on(dve.scalar_tensor_tensor(kept.slot_token[:, :], plan_bank[:, SLOTS:2 * SLOTS], float(P), id_part[:, :],
                                        ALU.mult, ALU.add))

        @block.tensor
        def _(pe):
            pe.wait_ge(set_dve, 2)

            def ahead(g):
                for i in range(GT):
                    pe.wait_ge(norm.normed, g * GT + i + 1)
                    wait_count(pe, lo_ready, g * GT + i - 1)
                    for c in range(KD):
                        done = pe.transpose(turn_bank[i % 2][:, c * P:(c + 1) * P], xn[:, i % 2, c * P:(c + 1) * P],
                                            kept.ident[:, :])
                    done.then_inc(turned, 1)

            def logits_part(g):
                pe.wait_ge(lo_ready, g * GT + GT)
                pe.wait_ge(split.lo_ready, 1)
                wait_count(pe, logit_read, g)
                for k in range(KD):
                    done = product(pe, logit_bank[:, :], [w[:, k] for w in w_route],
                                   [x[:, k, bass.ds(g * GW, GW)] for x in xnt], first=(k == 0), last=(k == KD - 1))
                done.then_inc(logit_filled, 1)
                pe.wait_ge(logit_read, g + 1)
                wait_count(pe, logits_ready, g)
                for i in range(GT):
                    done = pe.transpose(plan_bank[:, i * E1:(i + 1) * E1], logit_t[:, i * P:(i + 1) * P],
                                        kept.ident[0:E1, 0:E1])
                done.then_inc(logit_turned, 1)

            def shared_part(g):
                pe.wait_ge(split.lo_ready, len(split.parts))
                for j in range(NH):
                    n = g * NH + j
                    wait_count(pe, gelu_ready, n - 1)
                    for k in range(KD):
                        done = product(pe, up_bank[j % 2][:, :], [w[:, k, j * P:(j + 1) * P] for w in w_up],
                                       [x[:, k, bass.ds(g * GW, GW)] for x in xnt], first=(k == 0), last=(k == KD - 1))
                    done.then_inc(up_filled, 1)
                pe.wait_ge(hid_lo, g * NH + NH)
                for i in range(GT):
                    wait_count(pe, row_added, g * GT + i - 1)
                    for j in range(NH):
                        done = product(pe, row_bank[i % 2][:, :], [h[:, j, i * P:(i + 1) * P] for h in hidp],
                                       [w[:, j] for w in w_down], first=(j == 0), last=(j == NH - 1))
                    done.then_inc(row_filled, 1)

            staggered(ahead, logits_part, shared_part)
            shared_part(NG - 2)
            pe.wait_ge(member_ready, 1)
            pe.wait_ge(logits_ready, NG)
            pe.wait_ge(set_pool, 2)
            pe.matmul(plan_bank[:, 0:NT * E1], before_me[:, :], flat(member[:, :, :]), start=True, stop=True)
            pe.matmul(plan_bank[:, NT * E1:2 * NT * E1], all_ones[:, :], flat(member[:, :, :]), start=True, stop=True
                      ).then_inc(counted, 1)
            shared_part(NG - 1)
            pe.wait_ge(ids_hot, 2)
            for c in range(2):
                for j in range(NT):
                    done = pe.matmul(plan_bank[:, 0:2 * SLOTS], lane_hot[:, c, j], flat(slot_ids[:, c, j]),
                                     start=(c == 0 and j == 0), stop=(c == 1 and j == NT - 1))
            done.then_inc(ids_filled, 1)


def routed_stage(nc, kept, io):
    CU, CD = KD * HID, HJ * D
    with ExitStack() as ctx:
        mem = Memory(nc, ctx)
        sb, sem = mem.sb, mem.sem
        w_up, w_down = sb("w_rt_up", [P, E1, CU]), sb("w_rt_down", [P, E1, CD])
        rows = sb("slot_rows", [P, 2, D])
        index = [sb(f"slot_index{i}", [P, 1], I32) for i in range(2)]
        xt = [sb(f"slot_xt{i}", [P, KD, P]) for i in range(2)]
        mid = [sb(f"slot_mid{i}", [P, HID]) for i in range(2)]
        mid_t = [sb(f"slot_mid_t{i}", [P, HJ, P]) for i in range(2)]
        y = sb("slot_y", [P, 2, D])
        turn_bank = [mem.bank(f"turn6{i}") for i in range(2)]
        up_bank = [mem.bank(f"up6{i}") for i in range(2)]
        mid_bank = [mem.bank(f"mid6{i}") for i in range(2)]
        y_bank = [mem.bank(f"y6{i}") for i in range(2)]
        w_loaded, w_ready = [sem(f"rt_w_loaded{e}") for e in range(E1)], sem("rt_w_ready")
        fetched, indexed = [sem("fetched_even"), sem("fetched_odd")], sem("indexed")
        turned, xt_ready = sem("rows_turned"), sem("xt_ready")
        up_filled, mid_ready, mid_turned, mid_t_ready = sem("up6_filled"), sem("mid_ready"), sem("mid_turned"), sem("mid_t_ready")
        y_filled, y_ready = sem("y6_filled"), sem("y6_ready")
        y_stored = [sem("y_stored_even"), sem("y_stored_odd")]
        block = ctx.enter_context(nc.Block())

        def slots(eng, one):
            one(0, 0)
            one(1, 1)
            with eng.Fori(1, SLOTS // 2) as pair:
                s = 2 * pair
                one(s, 0)
                one(s + 1, 1)
            one(SLOTS - 1, (SLOTS - 1) % 2)

        @block.sync
        def _(sp):
            for e in range(E1):
                sp.dma_start(w_up[:, e], io["wrt_up"][e]).then_inc(w_loaded[e], 16)
                sp.dma_start(w_down[:, e], io["wrt_down"][e]).then_inc(w_loaded[e], 16)

            for e in range(E1):
                sp.wait_ge(w_loaded[e], 32)
                sp.sem_inc(w_ready, 1)

            def store(s, i):
                sp.wait_ge(y_ready, s + 1)
                sp.dma_start(kept.y_dram[bass.ds(s * P, P), :], y[:, i, :]).then_inc(y_stored[i], 16)

            slots(sp, store)
            sp.wait_ge(y_stored[0], 16 * ((SLOTS + 1) // 2))
            sp.wait_ge(y_stored[1], 16 * (SLOTS // 2))

        @block.gpsimd
        def _(pool):
            def fetch(s, i):
                wait_count(pool, fetched[i], (s - i) * 8)
                pool.tensor_copy(index[i][:, :], kept.slot_token[:, bass.ds(s, 1)]).then_inc(indexed, 1)
                pool.wait_ge(indexed, s + 1)
                wait_alone(pool, turned, s - 1, kept.passed)
                pool.indirect_dma_start(rows[:, i, :], None, kept.xn_dram, bass.IndirectOffsetOnAxis(index[i][:, :], 0)
                                        ).then_inc(fetched[i], 16)

            slots(pool, fetch)

        @block.scalar
        def _(act):
            def hidden(s, i):
                act.wait_ge(up_filled, s + 1)
                wait_count(act, mid_turned, s - 1)
                act.activation(mid[i][:, :], up_bank[i][:, 0:HID], ACT.Gelu).then_inc(mid_ready, 1)
                act.wait_ge(mid_turned, s + 1)
                wait_count(act, y_filled, s - 1)
                act.activation(mid_t[i][:, :, :].rearrange("p j t -> p (j t)"), mid_bank[i][:, 0:HID], ACT.Copy
                               ).then_inc(mid_t_ready, 1)

            slots(act, hidden)

        @block.vector
        def _(dve):
            def turned_rows(s, i):
                dve.wait_ge(turned, s + 1)
                wait_count(dve, up_filled, s - 1)
                dve.tensor_copy(xt[i][:, :, :].rearrange("p k t -> p (k t)"), turn_bank[i][:, :]).then_inc(xt_ready, 1)

            def result(s, i):
                dve.wait_ge(y_filled, s + 1)
                stored = (s - i) * 8
                wait_count(dve, y_stored[i], stored)
                dve.tensor_copy(y[:, i, :], y_bank[i][:, :]).then_inc(y_ready, 1)

            turned_rows(0, 0)
            turned_rows(1, 1)
            result(0, 0)
            turned_rows(2, 0)
            result(1, 1)
            with dve.Fori(1, SLOTS // 2) as pair:
                s = 2 * pair
                turned_rows(s + 1, 1)
                result(s, 0)
                turned_rows(s + 2, 0)
                result(s + 1, 1)
            result(SLOTS - 1, 0)

        @block.tensor
        def _(pe):
            def turn(s, i):
                pe.wait_ge(fetched[i], (s - i) * 8 + 16)
                wait_count(pe, xt_ready, s - 1)
                for c in range(KD):
                    done = pe.transpose(turn_bank[i][:, c * P:(c + 1) * P], rows[:, i, c * P:(c + 1) * P], kept.ident[:, :])
                done.then_inc(turned, 1)

            def turn_mid(s, i):
                pe.wait_ge(mid_ready, s + 1)
                wait_count(pe, mid_t_ready, s - 1)
                for j in range(HJ):
                    done = pe.transpose(mid_bank[i][:, j * P:(j + 1) * P], mid[i][:, j * P:(j + 1) * P], kept.ident[:, :])
                done.then_inc(mid_turned, 1)

            def up(s, i, e):
                pe.wait_ge(xt_ready, s + 1)
                wait_count(pe, mid_ready, s - 1)
                for k in range(KD):
                    done = pe.matmul(up_bank[i][:, 0:HID], xt[i][:, k], w_up[:, bass.ds(e, 1), k * HID:(k + 1) * HID]
                                     .rearrange("p o m -> p (o m)"), start=(k == 0), stop=(k == KD - 1))
                done.then_inc(up_filled, 1)

            def down(s, i, e):
                pe.wait_ge(mid_t_ready, s + 1)
                wait_count(pe, y_ready, s - 1)
                for j in range(HJ):
                    done = pe.matmul(y_bank[i][:, :], mid_t[i][:, j], w_down[:, bass.ds(e, 1), j * D:(j + 1) * D]
                                     .rearrange("p o m -> p (o m)"), start=(j == 0), stop=(j == HJ - 1))
                done.then_inc(y_filled, 1)

            def expert(s):
                return pe.value_load(kept.slot_expert[0:1, bass.ds(s, 1)], min_val=0, max_val=E1 - 1)

            def step(s, i, turn_next=True, behind=True):
                e = expert(s)
                pe.wait_ge(w_ready, e + 1)
                if turn_next:
                    turn(s + 1, 1 - i)
                if behind:
                    turn_mid(s - 1, 1 - i)
                up(s, i, e)
                if behind:
                    down(s - 1, 1 - i, expert(s - 1))

            turn(0, 0)
            step(0, 0, behind=False)
            step(1, 1)
            step(2, 0)
            step(3, 1)
            with pe.Fori(2, SLOTS // 2) as pair:
                s = 2 * pair
                step(s, 0)
                step(s + 1, 1)
            step(SLOTS - 1, 0, turn_next=False)
            turn_mid(SLOTS - 1, 0)
            down(SLOTS - 1, 0, expert(SLOTS - 1))


def combine_stage(nc, kept, io):
    SETS = 4
    with ExitStack() as ctx:
        mem = Memory(nc, ctx)
        sb, sem = mem.sb, mem.sem
        picks = sb("picks", [P, SETS, 2, D])
        index = [[sb(f"pick_index{i}_{c}", [P, 1], I32) for c in range(2)] for i in range(SETS)]
        indexed = sem("pick_indexed")
        fetched = [sem(f"picks_fetched{i}") for i in range(SETS)]
        half, added, stored = sem("first_added"), sem("both_added"), sem("out_stored")
        block = ctx.enter_context(nc.Block())

        def tiles(eng, one):
            with eng.Fori(0, NT // SETS) as r:
                for i in range(SETS):
                    one(r * SETS + i, i, r)

        @block.gpsimd
        def _(pool):
            def fetch(j, i, r):
                if not isinstance(r, int) or r > 0:
                    pool.wait_ge(added, j - SETS + 1)
                for c in range(2):
                    pool.tensor_copy(index[i][c][:, :], kept.route_row[:, c, bass.ds(j, 1)]).then_inc(indexed, 1)
                    wait_alone(pool, indexed, 2 * j + c + 1, kept.passed)
                    pool.indirect_dma_start(picks[:, i, c, :], None, kept.y_dram, bass.IndirectOffsetOnAxis(index[i][c][:, :], 0)
                                            ).then_inc(fetched[i], 16)

            for i in range(SETS):
                fetch(i, i, 0)
            with pool.Fori(1, NT // SETS) as r:
                for i in range(SETS):
                    fetch(r * SETS + i, i, r)

        @block.vector
        def _(dve):
            def add(j, i, r):
                row = kept.x[:, bass.ds(j, 1), :].rearrange("p o d -> p (o d)")
                dve.wait_ge(fetched[i], r * 32 + 32)
                dve.scalar_tensor_tensor(row, picks[:, i, 0, :], kept.route_gate[:, 0, bass.ds(j, 1)], row,
                                         ALU.mult, ALU.add).then_inc(half, 1)
                dve.wait_ge(half, j + 1)
                dve.scalar_tensor_tensor(row, picks[:, i, 1, :], kept.route_gate[:, 1, bass.ds(j, 1)], row,
                                         ALU.mult, ALU.add).then_inc(added, 1)

            tiles(dve, add)

        @block.sync
        def _(sp):
            out = io["out"].rearrange("(n p) d -> p n d", p=P)

            def store(j, i, r):
                sp.wait_ge(added, j + 1)
                sp.dma_start(out[:, bass.ds(j, 1), :], kept.x[:, bass.ds(j, 1), :]).then_inc(stored, 16)

            tiles(sp, store)
            sp.wait_ge(stored, 16 * NT)


class Kept:
    pass


def build(nc, io):
    kept = Kept()
    with ExitStack() as ctx:
        mem = Memory(nc, ctx)
        kept.gate_dram = nc.dram_tensor("gate_scratch", [E0, T], F32).ap()
        kept.passed = mem.sem("passed")
        kept.x = mem.sb("x_rows", [P, NT, D])
        kept.ident = mem.sb("ident", [P, P])
        kept.ones = mem.sb("ones", [P, P])
        with ExitStack() as latent_ctx:
            kept.latent = Memory(nc, latent_ctx).sb("latent", [P, T])
            clear(nc, mix_stage(nc, kept, io))
            latent_moe_stage(nc, kept, io)
            with ExitStack() as att_ctx:
                att = Memory(nc, att_ctx)
                kept.queries = att.sb("queries", [P, KD, T])
                kept.ogate = att.sb("ogate", [P, KD, T])
                query_stage(nc, kept, io)
                attention_stage(nc, kept, io)
                output_stage(nc, kept, io)
        moe_stages(nc, kept, io, mem)


def moe_stages(nc, kept, io, mem):
    kept.xn_dram = nc.dram_tensor("xn_scratch", [T, D], F32).ap()
    kept.y_dram = nc.dram_tensor("y_scratch", [SLOTS * P, D], F32).ap()
    kept.slot_token = mem.sb("slot_token", [P, SLOTS], I32)
    kept.slot_expert = mem.sb("slot_expert", [P, SLOTS], I32)
    kept.route_row = mem.sb("route_row", [P, 2, NT], I32)
    kept.route_gate = mem.sb("route_gate", [P, 2, NT])
    router_stage(nc, kept, io)
    routed_stage(nc, kept, io)
    combine_stage(nc, kept, io)


def decay_mask():
    import numpy as np

    gam = 1.0 - 2.0 ** (-5.0 - np.arange(KD, dtype=np.float64))
    expo = np.arange(S, dtype=np.float64)[None, :] - np.arange(S, dtype=np.float64)[:, None]
    table = np.where(expo[None] <= 0, gam[:, None, None] ** np.minimum(expo, 0.0)[None], 0.0)
    table = table / np.sqrt(table.sum(axis=-1))[:, None, :] / np.sqrt(float(P))
    turned = table.transpose(2, 0, 1)
    return np.ascontiguousarray(np.concatenate([turned[0:P], turned[P:S, :, P:S]], axis=2).astype(np.float32))


def layouts(a):
    import numpy as np

    def rows(x):
        return np.ascontiguousarray(x)

    return {
        "x": rows(a["x"].reshape(T, D)),
        "ctx_t": rows(a["ctx_2048"].reshape(T, D).T),
        "decay_first": rows(np.stack([a["L0_xattn_time_decay"].reshape(KD, P).T,
                                      a["L0_xattn_time_first"].reshape(KD, P).T], axis=1)),
        "bias": rows(a["L0_ffn_biases"].reshape(1, E0)),
        "w_front": rows(np.concatenate([a["L0_ffn_Wdown"].T, a["L0_ffn_swg"].T, a["L0_ffn_sw1"].T,
                                        a["L0_ffn_Wg"].T], axis=1)),
        "sw2_t": rows(a["L0_ffn_sw2"].T),
        "wup_t": rows(a["L0_ffn_Wup"].T),
        "heads": rows(a["L1_xattn_Wh"]),
        "wg": rows(a["L1_xattn_wg_w"]),
        "wo": rows(a["L1_xattn_wo_w"]),
        "gamma_beta": rows(np.stack([a["L1_xattn_gn_gamma"].reshape(KD, P).T,
                                     a["L1_xattn_gn_beta"].reshape(KD, P).T], axis=1)),
        "mask": decay_mask(),
        "w_router": rows(a["L1_ffn_W_router"]),
        "wsh_up": rows(a["L1_ffn_Wsh_up"].transpose(1, 0, 2).reshape(D, 2 * HID)),
        "wsh_down": rows(a["L1_ffn_Wsh_down"].reshape(2 * HID, D)),
        "wrt_up": rows(a["L1_ffn_Wrt_up"].reshape(E1, KD, P, HID).transpose(0, 2, 1, 3).reshape(E1, P, KD * HID)),
        "wrt_down": rows(a["L1_ffn_Wrt_down"].reshape(E1, HJ, P, D).transpose(0, 2, 1, 3).reshape(E1, P, HJ * D)),
        "experts": rows(np.concatenate([a["L0_ffn_rw1"].transpose(0, 2, 1), a["L0_ffn_rwg"].transpose(0, 2, 1),
                                        a["L0_ffn_rw2"].transpose(0, 2, 1).reshape(E0, HJ, P, LAT)
                                        .transpose(0, 2, 1, 3).reshape(E0, P, HJ * LAT)], axis=2)),
    }


def kernel(**inputs):
    import concourse.bacc as bacc
    from concourse.bass_utils import run_bass_kernel_spmd

    nc = bacc.Bacc("TRN2", target_bir_lowering=False, num_devices=1)
    arrays, io = {}, {}
    for name, a in layouts(inputs).items():
        arrays["in_" + name] = a
        io[name] = nc.dram_tensor("in_" + name, a.shape, mybir.dt.from_np(a.dtype), kind="ExternalInput").ap()
    io["out"] = nc.dram_tensor("out_rows", [T, D], F32, kind="ExternalOutput").ap()
    build(nc, io)
    result = run_bass_kernel_spmd(nc, [arrays], core_ids=[0])
    return result.results[0]["out_rows"].reshape(B, S, D)
```

```python
from contextlib import ExitStack

import concourse.bass as bass
from concourse import mybir

F32 = mybir.dt.float32
F32R = mybir.dt.float32r
BF16 = mybir.dt.bfloat16
I32 = mybir.dt.int32
U32 = mybir.dt.uint32
ALU = mybir.AluOpType
ACT = mybir.ActivationFunctionType
AX_X = mybir.AxisListType.X

P = 128
B, S, D = 8, 256, 512
T = B * S
NT = T // P
GT = 4
GW = GT * P
NG = NT // GT
KD = D // P
LAT, HID, E0 = 128, 256, 16
TOP0 = 8
SCALE0 = 2.5
HJ = HID // P
E1 = 16
SLOTS = 2 * NT + E1 - 1
LN_EPS = 1e-5
NEVER = -1e38


class Ticks:

    def __init__(self, sem, base=0):
        self.sem, self.base, self.n = sem, base, 0

    def tick(self, ins):
        ins.then_inc(self.sem, 1)
        self.n += 1
        return self.base + self.n


def product(pe, out, w, x, first=True, last=True):
    pe.matmul(out, w[0], x[0], start=first, stop=False)
    pe.matmul(out, w[0], x[1], start=False, stop=False)
    return pe.matmul(out, w[1], x[0], start=False, stop=last)


def whole(ap):
    return ap.bitcast(F32)


class Memory:

    def __init__(self, nc, ctx):
        self.nc, self.ctx, self.sems = nc, ctx, []

    def sb(self, name, shape, dtype=F32):
        return self.ctx.enter_context(self.nc.sbuf_tensor(name, shape, dtype))

    def pair(self, name, shape):
        return self.sb(name + "_hi", shape, F32R), self.sb(name + "_lo", shape, F32R)

    def bank(self, name, dtype=F32):
        return self.ctx.enter_context(self.nc.psum_tensor(name, [P, 512], dtype))

    def sem(self, name):
        self.sems.append(self.ctx.enter_context(self.nc.semaphore(name)))
        return self.sems[-1]


def wait_count(eng, sem, count):
    if not isinstance(count, int) or count > 0:
        eng.wait_ge(sem, count)


def wait_alone(eng, sem, count, passed):
    if not isinstance(count, int) or count > 0:
        eng.wait_ge(sem, count)
        if not isinstance(count, int):
            eng.sem_inc(passed, 1)


def starts(n):
    return isinstance(n, int) and n == 0


def is_last(g):
    return isinstance(g, int) and g == NG - 1


def side_by_side(eng, group, in_place_of_moe=None):
    def run(g):
        return lambda part, *args: part(g, *args)

    def leave_out(part, *args):
        pass

    group(run(0), in_place_of_moe or leave_out)
    group(run(1), run(0))
    with eng.Fori(2, NG) as g:
        group(run(g), run(g - 1))
    group(leave_out, run(NG - 1))


def mix_stage(nc, kept, io):
    C_DOWN, C_SGATE, C_SUP, C_ROUTE = 0, LAT, LAT + HID, LAT + 2 * HID
    C_ALL = C_ROUTE + P
    LOGIT, LOGIT_T, LATENT, HIDDEN, ROWS, GATE_T = 0, 1, 2, 3, 7, 11
    FILLS = 12
    ACT_READS = [LOGIT, LOGIT_T, LATENT, HIDDEN, HIDDEN + 2, GATE_T]
    DVE_READS = [HIDDEN + 1, HIDDEN + 3, ROWS, ROWS + 1, ROWS + 2, ROWS + 3]
    DVE_MIX, DVE_MOE = 36, 18

    with ExitStack() as ctx:
        mem = Memory(nc, ctx)
        sb, sem = mem.sb, mem.sem
        front = mem.pair("w_front", [P, KD, C_ALL])
        raw = sb("w_raw", [P, 2, C_ROUTE + E0])
        shared_down = mem.pair("w_shared_down", [P, HJ, D])
        bias = sb("gate_bias", [P, E0])
        small = sb("time_decay_and_first", [P, 2, KD])
        exp_decay = sb("exp_decay", [P, KD])
        decay = sb("decay", [P, KD])
        minus_half = sb("minus_half", [P, GT])
        ctx_t = sb("ctx_t", [P, 2, KD, GW])
        stats = sb("stats", [P, 2, GT, 6])
        meanvar = sb("meanvar", [P, 2, GT, 2])
        vareps = sb("vareps", [P, 2, GT])
        rstd = sb("rstd", [P, 2, GT])
        xn = sb("xn", [P, GT, D])
        key = sb("key", [P, KD, GW])
        xnt = mem.pair("xnt", [P, 2, KD, GW])
        top = sb("wkv_top", [P, 2, S + 1])
        num_state = sb("wkv_num_state", [P, 2, S + 1])
        den_state = sb("wkv_den_state", [P, 2, S + 1])
        gap = sb("wkv_gap", [P, GW])
        weight = sb("wkv_weight", [P, 2, 4, GW])
        v_in = sb("wkv_v_in", [P, 2, GW])
        v_now = sb("wkv_v_now", [P, 2, GW])
        den = sb("wkv_den", [P, 2, GW])
        num = sb("wkv_num", [P, 2, GW])
        guess = sb("wkv_guess", [P, 2, GW])
        logit_t = sb("logit_t", [E0, GW])
        minus_exp = sb("exp_minus_logit", [P, GT, E0])
        prob = sb("prob", [P, GT, E0])
        biased = sb("biased", [P, GT, E0])
        cut = sb("cut", [P, GT, E0])
        top8 = sb("top8", [P, GT, TOP0])
        prob_sum = sb("prob_sum", [P, GT])
        gate = sb("gate", [P, GT, E0])
        gate_t = sb("gate_t", [E0, GW])
        relu2 = sb("shared_relu2", [P, HJ, GW])
        hid = sb("shared_hid", [P, GW])
        hidp = mem.pair("shared_hidp", [P, HJ, GW])
        turn_bank = [mem.bank(f"turn{i}") for i in range(2)]
        y_bank = [mem.bank(f"y{i}") for i in range(2)]
        out_bank = [mem.bank(f"out{i}") for i in range(4)]

        x_loaded, ctx_loaded = sem("x_loaded"), sem("ctx_loaded")
        small_loaded, w_loaded = sem("small_loaded"), [sem("w_loaded_even"), sem("w_loaded_odd")]
        w_hi_ready, w_lo_ready = sem("w_hi_ready"), sem("w_lo_ready")
        set_dve, set_pool = sem("set_by_dve"), sem("set_by_pool")
        decay_exp = sem("decay_exp")
        den_scanned, den_part, num_part, miss_ready = sem("den_scanned"), sem("den_part"), sem("num_part"), sem("miss_ready")
        stats_ready, meanvar_ready, rstd_ready, vareps_ready, normed, turned = (
            [sem(f"{name}_{which}") for which in range(2)]
            for name in ("stats_ready", "meanvar_ready", "rstd_ready", "vareps_ready", "normed", "turned"))
        key_ready = sem("key_ready")
        expo_ready, weight_ready, v_ready = sem("expo_ready"), sem("weight_ready"), sem("v_ready")
        den_ready, num_ready = sem("den_ready"), sem("num_ready")
        log_ready, guess_ready = sem("log_ready"), sem("guess_ready")
        y_ready, y_turned, y_added = sem("y_ready"), sem("y_turned"), sem("y_added")
        hi_ready, lo_ready = sem("xnt_hi_ready"), sem("xnt_lo_ready")
        filled, read_act, read_dve = sem("filled"), sem("read_by_act"), sem("read_by_dve")
        relu2_ready, hidden_ready = sem("relu2_ready"), sem("hidden_ready")
        gate_ready, gate_stored = sem("gate_ready"), sem("gate_stored")
        dve_mix, dve_moe = sem("dve_mix_steps"), sem("dve_moe_steps")
        block = ctx.enter_context(nc.Block())

        def act_read(g, fill):
            return g * len(ACT_READS) + ACT_READS.index(fill) + 1

        def dve_read(g, fill):
            return g * len(DVE_READS) + DVE_READS.index(fill) + 1

        weight_parts = [(front[0][:, k, 0:C_ROUTE + E0], front[1][:, k, 0:C_ROUTE + E0], C_ROUTE + E0) for k in range(KD)]
        weight_parts += [(shared_down[0][:, j, :], shared_down[1][:, j, :], D) for j in range(HJ)]

        def load_weights(eng, n):
            src = io["w_front"][n * P:(n + 1) * P, :] if n < KD else io["sw2_t"][(n - KD) * P:(n - KD + 1) * P, :]
            eng.dma_start(raw[:, n % 2, 0:weight_parts[n][2]], src).then_inc(w_loaded[n % 2], 16)

        def by_chunk(ap):
            return ap.rearrange("p (c t) -> p c t", c=KD)

        def by_batch(ap):
            return ap.rearrange("p (b t) -> p b t", b=2)

        @block.sync
        def _(sp):
            x_in = io["x"].rearrange("(n p) d -> p n d", p=P)
            ctx_in = io["ctx_t"].rearrange("(c p) t -> p c t", p=P)
            for g in range(NG):
                sp.dma_start(kept.x[:, g * GT:(g + 1) * GT, :], x_in[:, g * GT:(g + 1) * GT, :]
                             ).then_inc(x_loaded, 16)
                if g == 0:
                    sp.wait_ge(x_loaded, 16)
                    for slot in range(2):
                        sp.dma_start(ctx_t[:, slot], ctx_in[:, :, slot * GW:(slot + 1) * GW]
                                     ).then_inc(ctx_loaded, 16)
                        sp.wait_ge(ctx_loaded, 16 * slot + 16)
                sp.wait_ge(x_loaded, 16 * g + 16)
            with sp.Fori(2, NG) as g:
                sp.wait_ge(v_ready, g * KD - KD)
                sp.dma_start(ctx_t[:, g % 2], ctx_in[:, :, bass.ds(g * GW, GW)]).then_inc(ctx_loaded, 16)
                sp.wait_ge(ctx_loaded, g * 16 + 16)
                sp.wait_ge(read_act, (g - 2) * len(ACT_READS) + len(ACT_READS))
                sp.dma_start(kept.gate_dram[:, bass.ds((g - 2) * GW, GW)], gate_t[:, :]).then_inc(gate_stored, 16)
            with sp.Fori(NG - 2, NG) as g:
                sp.wait_ge(read_act, g * len(ACT_READS) + len(ACT_READS))
                sp.dma_start(kept.gate_dram[:, bass.ds(g * GW, GW)], gate_t[:, :]).then_inc(gate_stored, 16)
            sp.wait_ge(gate_stored, 16 * NG)

        @block.gpsimd
        def _(pool):
            pool.memset(kept.ones[:, :], 1.0).then_inc(set_pool, 1)
            pool.memset(minus_half[:, :], -0.5).then_inc(set_pool, 1)
            pool.wait_ge(set_pool, 1)
            pool.affine_select(out=kept.ident[:, :], in_=kept.ones[:, :], pattern=[[-1, P]],
                               compare_op=ALU.is_equal, fill=0.0, base=0,
                               channel_multiplier=1).then_inc(set_pool, 1)
            pool.wait_ge(set_pool, 3)

            def rstds(g, norm):
                wait_alone(pool, meanvar_ready[norm], g * GT + GT, kept.passed)
                pool.tensor_scalar(vareps[:, norm], meanvar[:, norm, :, 1], LN_EPS, None, ALU.add
                                   ).then_inc(vareps_ready[norm], 1)
                pool.wait_ge(vareps_ready[norm], g + 1)
                wait_count(pool, normed[norm], g * GT)
                pool.tensor_tensor(rstd[:, norm], vareps[:, norm], minus_half[:, :], ALU.pow).then_inc(rstd_ready[norm], 1)

            def split_weights(parts):
                for n in parts:
                    hi, lo, width = weight_parts[n]
                    pool.wait_ge(w_hi_ready, n + 1)
                    pool.tensor_tensor(lo, raw[:, n % 2, 0:width], whole(hi), ALU.subtract).then_inc(w_lo_ready, 1)

            def values(g, c):
                k = g * KD + c
                if c == 0:
                    pool.wait_ge(ctx_loaded, g * 16 + 16)
                pool.wait_ge(weight_ready, k + 1)
                wait_count(pool, num_ready, k - 1)
                pool.tensor_tensor(v_in[:, c % 2], weight[:, c % 2, 1], ctx_t[:, g % 2, c], ALU.mult)
                pool.tensor_tensor(v_now[:, c % 2], weight[:, c % 2, 3], ctx_t[:, g % 2, c],
                                   ALU.mult).then_inc(v_ready, 1)

            def denominator(g, c):
                k = g * KD + c
                pool.wait_ge(den_scanned, k + 1)
                wait_count(pool, y_ready, k - 1)
                pool.tensor_tensor(by_batch(den[:, c % 2]), by_batch(weight[:, c % 2, 2]), den_state[:, :, 0:S],
                                   ALU.mult).then_inc(den_part, 1)
                pool.wait_ge(den_part, k + 1)
                pool.tensor_tensor(den[:, c % 2], den[:, c % 2], weight[:, c % 2, 3], ALU.add).then_inc(den_ready, 1)

            def numerator(g, c):
                k = g * KD + c
                pool.wait_ge(num_part, k + 1)
                pool.tensor_tensor(num[:, c % 2], num[:, c % 2], v_now[:, c % 2], ALU.add).then_inc(num_ready, 1)

            def misses(g, c):
                k = g * KD + c
                pool.wait_ge(guess_ready, k + 1)
                pool.wait_ge(den_ready, k + 1)
                pool.tensor_tensor(den[:, c % 2], den[:, c % 2], guess[:, c % 2], ALU.mult).then_inc(miss_ready, 1)

            def mix(g, splits=((), (), (), (), ())):
                rstds(g, 0)
                if not starts(g):
                    rstds(g - 1, 1)
                values(g, 0)
                split_weights(splits[0])
                values(g, 1)
                denominator(g, 0)
                numerator(g, 0)
                split_weights(splits[1])
                misses(g, 0)
                values(g, 2)
                denominator(g, 1)
                numerator(g, 1)
                split_weights(splits[2])
                misses(g, 1)
                values(g, 3)
                denominator(g, 2)
                numerator(g, 2)
                split_weights(splits[3])
                misses(g, 2)
                denominator(g, 3)
                numerator(g, 3)
                misses(g, 3)
                split_weights(splits[4])

            mix(0, splits=((0,), (1,), (2,), (3,), (4, 5)))
            mix(1)
            with pool.Fori(2, NG) as g:
                mix(g)
            rstds(NG - 1, 1)

        @block.scalar
        def _(act):
            act.dma_start(small[:, :, :], io["decay_first"]).then_inc(small_loaded, 16)
            act.dma_start(bias[:, :], io["bias"].to_broadcast([P, E0])).then_inc(small_loaded, 16)
            load_weights(act, 0)
            load_weights(act, 1)
            act.preload_act_table_set("natural_log_exp_and_others")
            act.wait_ge(small_loaded, 32)
            act.activation(exp_decay[:, :], small[:, 0, :], ACT.Exp).then_inc(decay_exp, 1)


            def keys(g):
                for i in range(GT):
                    act.wait_ge(turned[0], g * GT + i + 1)
                    act.activation(key[:, :, i * P:(i + 1) * P], by_chunk(turn_bank[i % 2][:, :]),
                                   ACT.Copy).then_inc(key_ready, 1)

            def weights(g, c):
                act.wait_ge(expo_ready, g * KD + c + 1)
                act.activation(weight[:, c % 2], weight[:, c % 2], ACT.Exp).then_inc(weight_ready, 1)

            def guesses(g, c):
                k = g * KD
                act.wait_ge(den_ready, k + c + 1)
                wait_count(act, y_ready, k + c - 1)
                act.activation(guess[:, c % 2], den[:, c % 2], ACT.Ln).then_inc(log_ready, 1)
                act.wait_ge(log_ready, k + c + 1)
                act.activation(guess[:, c % 2], guess[:, c % 2], ACT.Exp, scale=-1.0).then_inc(guess_ready, 1)

            def second_norm(g):
                for i in range(GT):
                    act.wait_ge(turned[1], g * GT + i + 1)
                    act.activation(xnt[0][:, g % 2, :, i * P:(i + 1) * P], by_chunk(turn_bank[i % 2][:, :]),
                                   ACT.Copy).then_inc(hi_ready, 1)

            def logit(g):
                act.wait_ge(filled, g * FILLS + LOGIT + 1)
                act.activation(logit_t[:, :], out_bank[0][0:E0, :], ACT.Copy).then_inc(read_act, 1)

            def turned_logit_and_latent(g):
                act.wait_ge(filled, g * FILLS + LOGIT_T + 1)
                act.activation(minus_exp[:, :, :].rearrange("p i e -> p (i e)"), out_bank[1][:, 0:GT * E0],
                               ACT.Exp, scale=-1.0).then_inc(read_act, 1)
                act.wait_ge(filled, g * FILLS + LATENT + 1)
                act.activation(kept.latent[:, bass.ds(g * GW, GW)], out_bank[2][:, :], ACT.Copy).then_inc(read_act, 1)

            def squares(g, j):
                act.wait_ge(filled, g * FILLS + HIDDEN + 2 * j + 1)
                act.activation(relu2[:, j], out_bank[(HIDDEN + 2 * j) % 4][:, :], ACT.Relu).then_inc(read_act, 1)
                act.wait_ge(read_act, act_read(g, HIDDEN + 2 * j))
                act.activation(relu2[:, j], relu2[:, j], ACT.Square).then_inc(relu2_ready, 1)

            def turned_gates(g):
                act.wait_ge(filled, g * FILLS + GATE_T + 1)
                wait_count(act, gate_stored, g * 16)
                act.activation(gate_t[:, :], out_bank[3][0:E0, :], ACT.Copy).then_inc(read_act, 1)

            def group(mix, moe):
                mix(keys)
                if moe is not split_weights:
                    moe(second_norm)
                mix(weights, 0)
                moe(logit)
                mix(weights, 1)
                moe(turned_logit_and_latent)
                mix(guesses, 0)
                mix(weights, 2)
                moe(squares, 0)
                mix(guesses, 1)
                mix(weights, 3)
                moe(squares, 1)
                mix(guesses, 2)
                mix(guesses, 3)
                moe(turned_gates)

            weight_turns = iter(range(len(weight_parts)))

            def split_weights(moe_part, *args):
                for n in [next(weight_turns)] + (list(weight_turns) if moe_part is turned_gates else []):
                    if n > 1:
                        act.wait_ge(w_lo_ready, n - 1)
                        load_weights(act, n)
                    act.wait_ge(w_loaded[n % 2], 16 * (n // 2) + 16)
                    hi, _, width = weight_parts[n]
                    act.activation(hi, raw[:, n % 2, 0:width], ACT.Copy).then_inc(w_hi_ready, 1)

            side_by_side(act, group, in_place_of_moe=split_weights)

        @block.vector
        def _(dve):
            dve.memset(top[:, :, 0:1], NEVER)
            dve.memset(num_state[:, :, 0:1], 0.0)
            dve.memset(den_state[:, :, 0:1], 0.0)
            dve.memset(front[0][:, :, C_ROUTE + E0:C_ALL].bitcast(F32), 0.0)
            dve.memset(front[1][:, :, C_ROUTE + E0:C_ALL].bitcast(F32), 0.0).then_inc(set_dve, 1)
            dve.wait_ge(decay_exp, 1)
            dve.tensor_scalar(decay[:, :], exp_decay[:, :], -1.0, None, ALU.mult).then_inc(set_dve, 1)
            dve.wait_ge(set_dve, 2)

            def statistics(g, which):
                if which == 0:
                    wait_alone(dve, x_loaded, g * 16 + 16, kept.passed)
                else:
                    wait_alone(dve, y_added, g * KD + KD, kept.passed)
                for i in range(GT):
                    dve.bn_stats(stats[:, which, i, :], kept.x[:, g * GT + i, :]).then_inc(stats_ready[which], 1)
                for i in range(GT):
                    wait_alone(dve, stats_ready[which], g * GT + i + 1, kept.passed)
                    dve.bn_aggr(meanvar[:, which, i, :], stats[:, which, i, :]).then_inc(meanvar_ready[which], 1)

            def normed_row(g, which, i):
                dve.wait_ge(rstd_ready[which], g + 1)
                if which == 0:
                    wait_count(dve, turned[1], (g - 2) * GT + i + 1)
                    wait_count(dve, turned[0], (g - 1) * GT + i + 1)
                elif is_last(g):
                    dve.wait_ge(turned[1], (g - 1) * GT + i + 1)
                else:
                    dve.wait_ge(turned[0], (g + 1) * GT + i + 1)
                dve.tensor_scalar(xn[:, i, :], kept.x[:, g * GT + i, :], meanvar[:, which, i, 0:1],
                                  rstd[:, which, i:i + 1], ALU.subtract, ALU.mult).then_inc(normed[which], 1)

            mixed = Ticks(dve_mix)
            routed = Ticks(dve_moe)

            def keys_are_there(g):
                mixed.base, mixed.n = g * DVE_MIX, 0
                dve.wait_ge(key_ready, g * KD + KD)

            def exponents(g, c):
                slot, keys = c % 2, key[:, c, :]
                before, after = top[:, :, 0:S], top[:, :, 1:S + 1]
                for b in range(2):
                    scanned = mixed.tick(dve.tensor_tensor_scan(
                        top[:, b, 1:S + 1], decay[:, c:c + 1].to_broadcast([P, S]),
                        key[:, c, b * S:(b + 1) * S], NEVER, ALU.add, ALU.max))
                dve.wait_ge(dve_mix, scanned)
                wait_count(dve, num_part, g * KD + c - 1)
                wait_count(dve, den_ready, g * KD + c - 1)
                mixed.tick(dve.scalar_tensor_tensor(by_batch(weight[:, slot, 0]), before, decay[:, c:c + 1], after,
                                                    ALU.add, ALU.subtract))
                mixed.tick(dve.tensor_tensor(by_batch(weight[:, slot, 1]), by_batch(keys), after, ALU.subtract))
                gapped = mixed.tick(dve.scalar_tensor_tensor(by_batch(gap[:, :]), by_batch(keys), small[:, 1, c:c + 1],
                                                             before, ALU.add, ALU.subtract))
                dve.wait_ge(dve_mix, gapped)
                mixed.tick(dve.tensor_scalar(weight[:, slot, 2], gap[:, :], -1.0, 0.0, ALU.mult, ALU.min))
                dve.tensor_scalar(weight[:, slot, 3], gap[:, :], 0.0, None, ALU.min).then_inc(expo_ready, 1)

            def states(g, c):
                slot, k = c % 2, g * KD
                keep, old = weight[:, slot, 0], weight[:, slot, 2]
                dve.wait_ge(v_ready, k + c + 1)
                wait_count(dve, den_part, k + c)
                for b in range(2):
                    part = slice(b * S, (b + 1) * S)
                    scanned = dve.tensor_tensor_scan(den_state[:, b, 1:S + 1], keep[:, part],
                                                     weight[:, slot, 1, part], 0.0, ALU.mult, ALU.add)
                scanned.then_inc(den_scanned, 1)
                for b in range(2):
                    part = slice(b * S, (b + 1) * S)
                    scanned = mixed.tick(dve.tensor_tensor_scan(num_state[:, b, 1:S + 1], keep[:, part],
                                                                v_in[:, slot, part], 0.0, ALU.mult, ALU.add))
                dve.wait_ge(dve_mix, scanned)
                wait_count(dve, y_turned, k + c - 1)
                dve.tensor_tensor(by_batch(num[:, slot]), by_batch(old), num_state[:, :, 0:S], ALU.mult).then_inc(num_part, 1)

            def quotient(g, c):
                slot = c % 2
                dve.wait_ge(guess_ready, g * KD + c + 1)
                dve.wait_ge(num_ready, g * KD + c + 1)
                both = mixed.tick(dve.tensor_tensor(num[:, slot], num[:, slot], guess[:, slot], ALU.mult))
                dve.wait_ge(dve_mix, both)
                dve.wait_ge(miss_ready, g * KD + c + 1)
                dve.scalar_tensor_tensor(num[:, slot], den[:, slot], 2.0, num[:, slot],
                                         ALU.subtract, ALU.mult).then_inc(y_ready, 1)

            def add(g, c):
                dve.wait_ge(y_turned, g * KD + c + 1)
                part = kept.x[:, bass.ds(g * GT, GT), c * P:(c + 1) * P]
                dve.tensor_tensor(part, part, y_bank[c % 2][:, :].rearrange("p (i d) -> p i d", i=GT),
                                  ALU.subtract).then_inc(y_added, 1)

            def split_row(g, i):
                dve.wait_ge(hi_ready, g * GT + i + 1)
                part = slice(i * P, (i + 1) * P)
                dve.tensor_tensor(xnt[1][:, g % 2, :, part], by_chunk(turn_bank[i % 2][:, :]),
                                  whole(xnt[0][:, g % 2, :, part]), ALU.subtract).then_inc(lo_ready, 1)

            def on(ins):
                dve.wait_ge(dve_moe, routed.tick(ins))

            def gates(g):
                routed.base, routed.n = g * DVE_MOE, 0
                dve.wait_ge(read_act, act_read(g, LOGIT_T))
                on(dve.tensor_scalar(minus_exp[:, :, :], minus_exp[:, :, :], 1.0, None, ALU.add))
                on(dve.reciprocal(prob[:, :, :], minus_exp[:, :, :]))
                wait_alone(dve, dve_moe, routed.tick(dve.tensor_tensor(
                    biased[:, :, :], prob[:, :, :], bias[:, :].unsqueeze(1).to_broadcast([P, GT, E0]), ALU.add)), kept.passed)
                for i in range(GT):
                    last = routed.tick(dve.max(top8[:, i], biased[:, i]))
                for i in range(GT):
                    wait_alone(dve, dve_moe, last - GT + 1 + i, kept.passed)
                    chosen = routed.tick(dve.match_replace(cut[:, i], top8[:, i], biased[:, i], NEVER))
                dve.wait_ge(dve_moe, chosen)
                on(dve.tensor_tensor(cut[:, :, :], cut[:, :, :], biased[:, :, :], ALU.not_equal))
                on(dve.tensor_tensor(cut[:, :, :], cut[:, :, :], prob[:, :, :], ALU.mult))
                on(dve.tensor_reduce(prob_sum[:, :], cut[:, :, :], AX_X, ALU.add))
                on(dve.reciprocal(prob_sum[:, :], prob_sum[:, :]))
                on(dve.tensor_scalar(prob_sum[:, :], prob_sum[:, :], SCALE0, None, ALU.mult))
                dve.tensor_tensor(gate[:, :, :], cut[:, :, :], prob_sum[:, :].unsqueeze(2).to_broadcast([P, GT, E0]),
                                  ALU.mult).then_inc(gate_ready, 1)

            def hidden(g, j):
                dve.wait_ge(relu2_ready, g * HJ + j + 1)
                dve.wait_ge(filled, g * FILLS + HIDDEN + 2 * j + 2)
                dve.tensor_tensor(hid[:, :], out_bank[(HIDDEN + 2 * j + 1) % 4][:, :], relu2[:, j],
                                  ALU.mult).then_inc(read_dve, 1)
                dve.wait_ge(read_dve, dve_read(g, HIDDEN + 2 * j + 1))
                on(dve.tensor_copy(hidp[0][:, j], hid[:, :]))
                dve.tensor_tensor(hidp[1][:, j], hid[:, :], whole(hidp[0][:, j]), ALU.subtract).then_inc(hidden_ready, 1)
                dve.wait_ge(hidden_ready, g * HJ + j + 1)

            def add_rows(g, tiles):
                for i in tiles:
                    dve.wait_ge(filled, g * FILLS + ROWS + i + 1)
                    dve.tensor_tensor(kept.x[:, g * GT + i, :], kept.x[:, g * GT + i, :],
                                      out_bank[(ROWS + i) % 4][:, :], ALU.add).then_inc(read_dve, 1)

            def all_counted(g):
                assert mixed.n == DVE_MIX, mixed.n

            def group(mix, moe):
                mix(statistics, 0)
                moe(statistics, 1)
                for i in range(GT):
                    mix(normed_row, 0, i)
                for i in range(GT):
                    moe(normed_row, 1, i)
                for i in range(GT):
                    moe(split_row, i)
                mix(keys_are_there)
                mix(exponents, 0)
                mix(exponents, 1)
                mix(states, 0)
                moe(gates)
                mix(exponents, 2)
                mix(states, 1)
                moe(hidden, 0)
                mix(quotient, 0)
                mix(exponents, 3)
                mix(states, 2)
                mix(add, 0)
                moe(hidden, 1)
                mix(quotient, 1)
                mix(states, 3)
                mix(add, 1)
                mix(quotient, 2)
                moe(add_rows, (0, 1))
                mix(add, 2)
                mix(quotient, 3)
                moe(add_rows, (2, 3))
                mix(add, 3)
                mix(all_counted)

            side_by_side(dve, group)

        @block.tensor
        def _(pe):
            pe.wait_ge(set_pool, 3)

            def turn(g, which):
                for i in range(GT):
                    pe.wait_ge(normed[which], g * GT + i + 1)
                    if i >= 2 and which == 0:
                        pe.wait_ge(key_ready, g * GT + i - 1)
                    elif i >= 2:
                        pe.wait_ge(lo_ready, g * GT + i - 1)
                    elif which == 0:
                        wait_count(pe, key_ready, (g - 1) * GT + i + 3)
                        wait_count(pe, lo_ready, (g - 2) * GT + i + 3)
                    elif is_last(g):
                        pe.wait_ge(lo_ready, (g - 1) * GT + i + 3)
                    else:
                        pe.wait_ge(key_ready, (g + 1) * GT + i + 3)
                    for c in range(KD):
                        done = pe.transpose(turn_bank[i % 2][:, c * P:(c + 1) * P], xn[:, i, c * P:(c + 1) * P],
                                            kept.ident[:, :])
                    done.then_inc(turned[which], 1)

            def turn_y(g, c):
                pe.wait_ge(y_ready, g * KD + c + 1)
                wait_count(pe, y_added, g * KD + c - 1)
                for i in range(GT):
                    done = pe.transpose(y_bank[c % 2][:, i * P:(i + 1) * P], num[:, c % 2, i * P:(i + 1) * P],
                                        kept.ident[:, :])
                done.then_inc(y_turned, 1)

            def from_norm(g, bank, col):
                for k in range(KD):
                    done = product(pe, out_bank[bank][:, :],
                                   [w[:, k, col:col + P] for w in front], [x[:, g % 2, k, :] for x in xnt],
                                   first=(k == 0), last=(k == KD - 1))
                done.then_inc(filled, 1)

            def logits_and_latent(g):
                pe.wait_ge(w_lo_ready, KD)
                pe.wait_ge(lo_ready, g * GT + GT)
                wait_count(pe, read_dve, g * len(DVE_READS) - 2)
                from_norm(g, 0, C_ROUTE)
                pe.wait_ge(read_act, act_read(g, LOGIT))
                wait_alone(pe, read_dve, g * len(DVE_READS) - 1, kept.passed)
                for i in range(GT):
                    done = pe.transpose(out_bank[1][:, i * E0:(i + 1) * E0], logit_t[:, i * P:(i + 1) * P],
                                        kept.ident[0:E0, 0:E0])
                done.then_inc(filled, 1)
                wait_count(pe, read_dve, g * len(DVE_READS))
                from_norm(g, 2, C_DOWN)

            def hidden(g, j):
                if j == 0:
                    wait_count(pe, read_act, g * len(ACT_READS))
                    from_norm(g, 3, C_SGATE)
                    from_norm(g, 0, C_SUP)
                else:
                    pe.wait_ge(read_act, act_read(g, LOGIT_T))
                    from_norm(g, 1, C_SGATE + P)
                    pe.wait_ge(read_act, act_read(g, LATENT))
                    from_norm(g, 2, C_SUP + P)

            def rows(g):
                pe.wait_ge(w_lo_ready, KD + HJ)
                pe.wait_ge(hidden_ready, g * HJ + HJ)
                for i in range(GT):
                    if i == 0:
                        pe.wait_ge(read_act, act_read(g, HIDDEN))
                    if i == 1:
                        pe.wait_ge(read_dve, dve_read(g, HIDDEN + 1))
                    if i == 2:
                        pe.wait_ge(read_act, act_read(g, HIDDEN + 2))
                    if i == 3:
                        pe.wait_ge(read_dve, dve_read(g, HIDDEN + 3))
                    for j in range(HJ):
                        done = product(pe, out_bank[(ROWS + i) % 4][:, :],
                                       [h[:, j, i * P:(i + 1) * P] for h in hidp], [w[:, j, :] for w in shared_down],
                                       first=(j == 0), last=(j == HJ - 1))
                    done.then_inc(filled, 1)

            def turn_gates(g):
                pe.wait_ge(gate_ready, g + 1)
                pe.wait_ge(read_dve, dve_read(g, ROWS))
                for i in range(GT):
                    done = pe.transpose(out_bank[3][0:E0, i * P:(i + 1) * P], gate[:, i, :], kept.ident[:, :])
                done.then_inc(filled, 1)

            def group(mix, moe):
                mix(turn, 0)
                moe(turn, 1)
                moe(logits_and_latent)
                moe(hidden, 0)
                mix(turn_y, 0)
                moe(hidden, 1)
                mix(turn_y, 1)
                moe(rows)
                mix(turn_y, 2)
                moe(turn_gates)
                mix(turn_y, 3)

            side_by_side(pe, group)
    return mem.sems


def clear(pool, sems):
    for sem in sems:
        pool.sem_clear(sem)


def latent_moe_stage(nc, kept, io):
    HALVES = NG * HJ
    C_UP, C_GATE, C_DOWN = 0, HID, 2 * HID
    C_ALL = 2 * HID + HJ * LAT
    SPLIT_LAG, DOWN_LAG = 2, 4
    with ExitStack() as ctx:
        mem = Memory(nc, ctx)
        sb, sem = mem.sb, mem.sem
        latp = mem.pair("latent_p", [P, T])
        raw = sb("expert_raw", [P, 2, C_ALL])
        wp = [mem.pair(f"expert_w{i}", [P, C_ALL]) for i in range(2)]
        gates = sb("expert_gates", [P, 2, T])
        zeros = sb("expert_zeros", [P, GW], BF16)
        relu = sb("expert_relu", [P, 2, GW])
        relu2 = sb("expert_relu2", [P, 2, GW])
        prod = sb("expert_prod", [P, 2, GW])
        hid = sb("expert_hid", [P, 4, GW])
        hidp = mem.pair("expert_hidp", [P, 4, GW])
        acc = [mem.bank(f"acc{g}") for g in range(NG)]
        up_bank = [mem.bank(f"up{i}") for i in range(2)]
        gate_bank = [mem.bank(f"gate{i}") for i in range(2)]

        w_loaded = [sem("expert_w_even"), sem("expert_w_odd")]
        gates_loaded = [sem("expert_gates_even"), sem("expert_gates_odd")]
        acc_read = sem("acc_read")
        zeros_set, acc_opened = sem("zeros_set"), sem("acc_opened")
        lat_hi, lat_lo = sem("latent_hi"), sem("latent_lo")
        w_hi, w_lo = sem("expert_w_hi"), sem("expert_w_lo")
        gate_filled, up_filled, down_done = sem("gate_filled"), sem("up_filled"), sem("down_done")
        relu_done, relu2_ready = sem("relu_done"), sem("expert_relu2_ready")
        prod_ready, hid_ready, hid_hi, hid_lo = sem("prod_ready"), sem("hid_ready"), sem("hid_hi"), sem("hid_lo")
        block = ctx.enter_context(nc.Block())

        def load(eng, e, i):
            eng.dma_start(raw[:, i, :], io["experts"][bass.ds(e + i, 1)].rearrange("o p m -> (o p) m")
                          ).then_inc(w_loaded[i], 16)
            eng.dma_start(gates[:, i, :], kept.gate_dram[bass.ds(e + i, 1), :].to_broadcast([P, T])
                          ).then_inc(gates_loaded[i], 16)

        @block.sync
        def _(sp):
            load(sp, 0, 0)
            load(sp, 0, 1)
            with sp.Fori(1, E0 // 2) as pair:
                e = 2 * pair
                for i in range(2):
                    wait_alone(sp, w_lo, e + i - 1, kept.passed)
                    wait_alone(sp, hid_ready, (e + i - 1) * HALVES, kept.passed)
                    load(sp, e, i)

        @block.gpsimd
        def _(pool):
            pool.memset(zeros[:, :], 0.0).then_inc(zeros_set, 1)
            clear(pool, kept.finished)

            def pair_of_experts(e):
                for m in range(2 * HALVES):
                    n = e * HALVES + m
                    i, g = m // HALVES, m % HALVES // HJ
                    if m % HALVES == 0:
                        pool.wait_ge(gates_loaded[i], e * 8 + 16)
                    pool.wait_ge(prod_ready, n + 1)
                    wait_count(pool, hid_lo, n - 3)
                    pool.tensor_tensor(hid[:, m % 4], prod[:, m % 2], gates[:, i, g * GW:(g + 1) * GW],
                                       ALU.mult).then_inc(hid_ready, 1)

            pair_of_experts(0)
            with pool.Fori(1, E0 // 2) as pair:
                e = 2 * pair
                pair_of_experts(e)

        @block.scalar
        def _(act):
            for g in range(NG):
                part = slice(g * GW, (g + 1) * GW)
                act.activation(latp[0][:, part], kept.latent[:, part], ACT.Copy).then_inc(lat_hi, 1)

            def hi(n, m):
                act.wait_ge(hid_ready, n + 1)
                wait_count(act, down_done, n - 3)
                act.activation(hidp[0][:, m % 4], hid[:, m % 4], ACT.Copy).then_inc(hid_hi, 1)

            def pair_of_experts(e):
                for m in range(2 * HALVES):
                    n = e * HALVES + m
                    act.wait_ge(gate_filled, n + 1)
                    wait_count(act, relu2_ready, n - 1)
                    act.activation(relu[:, m % 2], gate_bank[m % 2][:, :], ACT.Relu).then_inc(relu_done, 1)
                    if m >= SPLIT_LAG or not starts(e):
                        hi(n - SPLIT_LAG, m - SPLIT_LAG)
                    act.wait_ge(relu_done, n + 1)
                    wait_count(act, prod_ready, n - 1)
                    act.activation(relu2[:, m % 2], relu[:, m % 2], ACT.Square).then_inc(relu2_ready, 1)

            pair_of_experts(0)
            with act.Fori(1, E0 // 2) as pair:
                e = 2 * pair
                pair_of_experts(e)
            for m in range(2 * HALVES - SPLIT_LAG, 2 * HALVES):
                hi((E0 - 2) * HALVES + m, m)
            act.wait_ge(down_done, E0 * HALVES)
            for g in range(NG):
                act.activation(kept.latent[:, g * GW:(g + 1) * GW], acc[g][:, :], ACT.Copy).then_inc(acc_read, 1)

        @block.vector
        def _(dve):
            for g in range(NG):
                part = slice(g * GW, (g + 1) * GW)
                dve.wait_ge(lat_hi, g + 1)
                dve.tensor_tensor(latp[1][:, part], kept.latent[:, part], whole(latp[0][:, part]),
                                  ALU.subtract).then_inc(lat_lo, 1)

            def split_weights(e, i):
                dve.wait_ge(w_loaded[i], (e - i) * 8 + 16)
                dve.tensor_copy(wp[i][0][:, :], raw[:, i]).then_inc(w_hi, 1)
                dve.wait_ge(w_hi, e + 1)
                dve.tensor_tensor(wp[i][1][:, :], raw[:, i], whole(wp[i][0][:, :]), ALU.subtract).then_inc(w_lo, 1)

            def lo(n, m):
                dve.wait_ge(hid_hi, n + 1)
                dve.tensor_tensor(hidp[1][:, m % 4], hid[:, m % 4], whole(hidp[0][:, m % 4]),
                                  ALU.subtract).then_inc(hid_lo, 1)

            def pair_of_experts(e, last=False):
                for m in range(2 * HALVES):
                    n = e * HALVES + m
                    dve.wait_ge(relu2_ready, n + 1)
                    dve.wait_ge(up_filled, n + 1)
                    wait_count(dve, hid_ready, n - 1)
                    dve.tensor_tensor(prod[:, m % 2], up_bank[m % 2][:, :], relu2[:, m % 2],
                                      ALU.mult).then_inc(prod_ready, 1)
                    if m >= SPLIT_LAG or not starts(e):
                        lo(n - SPLIT_LAG, m - SPLIT_LAG)
                    if m % HALVES == DOWN_LAG and not (last and m > HALVES):
                        i = m // HALVES
                        wait_count(dve, down_done, (e + i) * HALVES)
                        split_weights(e + i + 1, (i + 1) % 2)

            split_weights(0, 0)
            pair_of_experts(0)
            with dve.Fori(1, E0 // 2 - 1) as pair:
                e = 2 * pair
                pair_of_experts(e)
            pair_of_experts(E0 - 2, last=True)
            for m in range(2 * HALVES - SPLIT_LAG, 2 * HALVES):
                lo((E0 - 2) * HALVES + m, m)

        @block.tensor
        def _(pe):
            pe.wait_ge(zeros_set, 1)
            for g in range(NG):
                done = pe.matmul(acc[g][:, :], zeros[:, 0:P], zeros[:, :], start=True, stop=True)
            done.then_inc(acc_opened, 1)
            pe.wait_ge(lat_lo, NG)

            def up(n, m):
                i, g, j = m // HALVES, m % HALVES // HJ, m % HJ
                x = [t[:, g * GW:(g + 1) * GW] for t in latp]
                wait_count(pe, prod_ready, n - 1)
                product(pe, gate_bank[m % 2][:, :], [w[:, C_GATE + j * P:C_GATE + (j + 1) * P] for w in wp[i]],
                        x).then_inc(gate_filled, 1)
                product(pe, up_bank[m % 2][:, :], [w[:, C_UP + j * P:C_UP + (j + 1) * P] for w in wp[i]],
                        x).then_inc(up_filled, 1)

            def down(n, m):
                m = m % (2 * HALVES)
                i, g, j = m // HALVES, m % HALVES // HJ, m % HJ
                w = [t[:, C_DOWN + j * LAT:C_DOWN + (j + 1) * LAT] for t in wp[i]]
                pe.wait_ge(hid_lo, n + 1)
                h = [t[:, m % 4] for t in hidp]
                for a, b in ((0, 0), (0, 1), (1, 0)):
                    done = pe.matmul(acc[g][:, :], w[a][:, :], h[b], start=False, stop=False, skip_group_check=True)
                done.then_inc(down_done, 1)

            def pair_of_experts(e):
                for m in range(2 * HALVES):
                    n = e * HALVES + m
                    if m % HALVES == 0:
                        pe.wait_ge(w_lo, e + m // HALVES + 1)
                    up(n, m)
                    if m >= DOWN_LAG or not starts(e):
                        down(n - DOWN_LAG, m - DOWN_LAG)

            pair_of_experts(0)
            with pe.Fori(1, E0 // 2) as pair:
                e = 2 * pair
                pair_of_experts(e)
            for m in range(2 * HALVES - DOWN_LAG, 2 * HALVES):
                down((E0 - 2) * HALVES + m, m)
    return mem.sems


class Split:

    def __init__(self, mem, name, parts):
        self.parts = parts
        self.raw = mem.sb(name + "_raw", [P, len(parts), max(p[3] for p in parts)])
        self.first_loaded, self.rest_loaded = mem.sem(name + "_first_loaded"), mem.sem(name + "_rest_loaded")
        self.hi_ready, self.lo_ready = mem.sem(name + "_hi_ready"), mem.sem(name + "_lo_ready")

    def raw_part(self, n):
        _, hi, _, width = self.parts[n]
        flat = self.raw[:, n, 0:width]
        return flat.rearrange("p (k e) -> p k e", k=hi.shape[1]) if len(hi.shape) == 3 else flat

    def load(self, eng):
        for n, (src, hi, _, width) in enumerate(self.parts):
            out = self.raw_part(n) if len(src.shape) == 3 and len(hi.shape) == 3 else self.raw[:, n, 0:width]
            eng.dma_start(out, src).then_inc(self.rest_loaded if n else self.first_loaded, 16)

    def on_scalar(self, act, parts):
        for n in parts:
            if n == 0:
                act.wait_ge(self.first_loaded, 16)
            if n == 1:
                act.wait_ge(self.rest_loaded, 16 * (len(self.parts) - 1))
            act.activation(self.parts[n][1], self.raw_part(n), ACT.Copy).then_inc(self.hi_ready, 1)

    def on_pool(self, pool, parts):
        for n in parts:
            _, hi, lo, _ = self.parts[n]
            pool.wait_ge(self.hi_ready, n + 1)
            pool.tensor_tensor(lo, self.raw_part(n), whole(hi), ALU.subtract).then_inc(self.lo_ready, 1)


class Norm:

    def __init__(self, mem, name, eps, passed):
        self.eps, self.passed = eps, passed
        self.stats = mem.sb(name + "_stats", [P, GT, 6])
        self.meanvar = mem.sb(name + "_meanvar", [P, GT, 2])
        self.vareps = mem.sb(name + "_vareps", [P, GT])
        self.rstd = mem.sb(name + "_rstd", [P, GT])
        self.minus_half = mem.sb(name + "_minus_half", [P, GT])
        self.stats_ready, self.meanvar_ready = mem.sem(name + "_stats_ready"), mem.sem(name + "_meanvar_ready")
        self.half_set, self.vareps_ready = mem.sem(name + "_half_set"), mem.sem(name + "_vareps_ready")
        self.rstd_ready, self.normed = mem.sem(name + "_rstd_ready"), mem.sem(name + "_normed")

    def pool_start(self, pool):
        pool.memset(self.minus_half[:, :], -0.5).then_inc(self.half_set, 1)
        pool.wait_ge(self.half_set, 1)

    def on_pool(self, pool, n):
        wait_alone(pool, self.meanvar_ready, n * GT + GT, self.passed)
        pool.tensor_scalar(self.vareps[:, :], self.meanvar[:, :, 1], self.eps, None, ALU.add).then_inc(self.vareps_ready, 1)
        pool.wait_ge(self.vareps_ready, n + 1)
        wait_count(pool, self.normed, n * GT)
        pool.tensor_tensor(self.rstd[:, :], self.vareps[:, :], self.minus_half[:, :], ALU.pow).then_inc(self.rstd_ready, 1)

    def stats_on_vector(self, dve, n, i, row):
        dve.bn_stats(self.stats[:, i, :], row).then_inc(self.stats_ready, 1)

    def meanvar_on_vector(self, dve, n):
        for i in range(GT):
            wait_alone(dve, self.stats_ready, n * GT + i + 1, self.passed)
            dve.bn_aggr(self.meanvar[:, i, :], self.stats[:, i, :]).then_inc(self.meanvar_ready, 1)
        dve.wait_ge(self.rstd_ready, n + 1)

    def rows_on_vector(self, dve, i, row, out):
        dve.tensor_scalar(out, row, self.meanvar[:, i, 0:1], self.rstd[:, i:i + 1],
                          ALU.subtract, ALU.mult).then_inc(self.normed, 1)


def query_stage(nc, kept, io):
    FILLS = 2 * KD
    with ExitStack() as ctx:
        mem = Memory(nc, ctx)
        sb, sem = mem.sb, mem.sem
        w_up, w_head, w_gate = mem.pair("w_up0", [P, D]), mem.pair("w_head", [P, D]), mem.pair("w_ogate", [P, KD, D])
        split = Split(mem, "query_w",
                      [(io["wup_t"], w_up[0][:, :], w_up[1][:, :], D),
                       (io["heads"].rearrange("h p e -> p h e"), w_head[0][:, :], w_head[1][:, :], D)]
                      + [(io["wg"][k * P:(k + 1) * P, :], w_gate[0][:, k], w_gate[1][:, k], D) for k in range(KD)])
        norm = Norm(mem, "query_norm", LN_EPS, kept.passed)
        accp = mem.pair("accp", [P, GW])
        xn = sb("xn2", [P, GT, D])
        xnt = mem.pair("xn2t", [P, 2, KD, GW])
        row_bank = [mem.bank(f"row{i}") for i in range(2)]
        turn_bank = [mem.bank(f"turn2{i}") for i in range(2)]
        out_bank = [mem.bank(f"out2{i}") for i in range(4)]
        acc_hi, acc_lo = sem("accp_hi"), sem("accp_lo")
        row_filled, row_added = sem("row_filled"), sem("row_added")
        turned, hi_ready, lo_ready = sem("turned2"), sem("xn2t_hi"), sem("xn2t_lo")
        filled, read = sem("filled2"), sem("read2")
        block = ctx.enter_context(nc.Block())

        def by_chunk(ap):
            return ap.rearrange("p (c t) -> p c t", c=KD)

        @block.gpsimd
        def _(pool):
            norm.pool_start(pool)
            clear(pool, kept.finished)
            split.on_pool(pool, range(1))
            norm.on_pool(pool, 0)
            split.on_pool(pool, range(1, len(split.parts)))
            norm.on_pool(pool, 1)
            with pool.Fori(2, NG) as g:
                norm.on_pool(pool, g)

        @block.sync
        def _(sp):
            split.load(sp)
            sp.dma_start(kept.head_raw[:, :].rearrange("p (h e) -> p h e", h=KD), io["heads"].rearrange("h p e -> p h e")
                         ).then_inc(kept.head_loaded, 16)
            sp.dma_start(kept.ctx_raw[:, :], io["ctx_t"][0:P, :]).then_inc(kept.ctx_loaded, 16)

        @block.scalar
        def _(act):
            def sums(g):
                wait_count(act, row_filled, g * GT)
                act.activation(accp[0][:, :], kept.latent[:, bass.ds(g * GW, GW)], ACT.Copy).then_inc(acc_hi, 1)

            def turned_rows(g):
                for i in range(GT):
                    act.wait_ge(turned, g * GT + i + 1)
                    act.activation(xnt[0][:, g % 2, :, i * P:(i + 1) * P], by_chunk(turn_bank[i % 2][:, :]),
                                   ACT.Copy).then_inc(hi_ready, 1)

            def outputs(g, fills):
                part = bass.ds(g * GW, GW)
                for m in fills:
                    act.wait_ge(filled, g * FILLS + m + 1)
                    out = kept.queries[:, m, part] if m < KD else kept.ogate[:, m - KD, part]
                    act.activation(out, out_bank[m % 4][:, :], ACT.Copy if m < KD else ACT.Relu).then_inc(read, 1)

            split.on_scalar(act, range(1))
            sums(0)
            split.on_scalar(act, range(1, len(split.parts)))
            turned_rows(0)
            sums(1)
            for g in range(1, NG):
                outputs(g - 1, range(0, 6))
                turned_rows(g)
                if g + 1 < NG:
                    sums(g + 1)
                outputs(g - 1, range(6, FILLS))
            outputs(NG - 1, range(FILLS))

        @block.vector
        def _(dve):
            def rows(g):
                dve.wait_ge(acc_hi, g + 1)
                dve.tensor_tensor(accp[1][:, :], kept.latent[:, bass.ds(g * GW, GW)], whole(accp[0][:, :]),
                                  ALU.subtract).then_inc(acc_lo, 1)
                for i in range(GT):
                    row = kept.x[:, g * GT + i, :]
                    dve.wait_ge(row_filled, g * GT + i + 1)
                    dve.tensor_tensor(row, row, row_bank[i % 2][:, :], ALU.add).then_inc(row_added, 1)
                    if i > 0:
                        wait_alone(dve, row_added, g * GT + i, kept.passed)
                        norm.stats_on_vector(dve, g, i - 1, kept.x[:, g * GT + i - 1, :])
                wait_alone(dve, row_added, g * GT + GT, kept.passed)
                norm.stats_on_vector(dve, g, GT - 1, kept.x[:, g * GT + GT - 1, :])
                norm.meanvar_on_vector(dve, g)
                for i in range(GT):
                    wait_count(dve, turned, (g - 1) * GT + i + 1)
                    norm.rows_on_vector(dve, i, kept.x[:, g * GT + i, :], xn[:, i, :])
                for i in range(GT):
                    part = slice(i * P, (i + 1) * P)
                    dve.wait_ge(hi_ready, g * GT + i + 1)
                    dve.tensor_tensor(xnt[1][:, g % 2, :, part], by_chunk(turn_bank[i % 2][:, :]),
                                      whole(xnt[0][:, g % 2, :, part]), ALU.subtract).then_inc(lo_ready, 1)

            rows(0)
            with dve.Fori(1, NG) as g:
                rows(g)

        @block.tensor
        def _(pe):
            pe.wait_ge(split.lo_ready, 1)

            def sums(g):
                pe.wait_ge(acc_lo, g + 1)
                for i in range(GT):
                    wait_count(pe, row_added, g * GT + i - 1)
                    product(pe, row_bank[i % 2][:, :], [a[:, i * P:(i + 1) * P] for a in accp],
                            [w[:, :] for w in w_up]).then_inc(row_filled, 1)

            def turns(g):
                for i in range(GT):
                    pe.wait_ge(norm.normed, g * GT + i + 1)
                    wait_count(pe, lo_ready, g * GT + i - 1)
                    for c in range(KD):
                        done = pe.transpose(turn_bank[i % 2][:, c * P:(c + 1) * P], xn[:, i, c * P:(c + 1) * P],
                                            kept.ident[:, :])
                    done.then_inc(turned, 1)

            def outputs(g, fills):
                pe.wait_ge(lo_ready, g * GT + GT)
                pe.wait_ge(split.lo_ready, len(split.parts))
                for m in fills:
                    wait_count(pe, read, g * FILLS + m - 3)
                    if m < KD:
                        done = product(pe, out_bank[m % 4][:, :], [w[:, m * P:(m + 1) * P] for w in w_head],
                                       [x[:, g % 2, m, :] for x in xnt])
                    else:
                        for k in range(KD):
                            col = (m - KD) * P
                            done = product(pe, out_bank[m % 4][:, :], [w[:, k, col:col + P] for w in w_gate],
                                           [x[:, g % 2, k, :] for x in xnt], first=(k == 0), last=(k == KD - 1))
                    done.then_inc(filled, 1)

            def both(g):
                sums(g)
                outputs(g - 1, range(0, 6))
                turns(g)
                outputs(g - 1, range(6, FILLS))

            sums(0)
            turns(0)
            both(1)
            with pe.Fori(2, NG) as g:
                both(g)
            outputs(NG - 1, range(FILLS))


def attention_stage(nc, kept, io):
    H2 = S // 2
    MASKED = S + H2
    with ExitStack() as ctx:
        mem = Memory(nc, ctx)
        sb, sem = mem.sb, mem.sem
        mask = sb("mask", [P, KD, MASKED])
        w_raw, ctx_raw = kept.head_raw, kept.ctx_raw
        w_all = mem.pair("head_w_all", [P, D])
        w_head = mem.pair("head_w", [P, P])
        ctxp = mem.pair("ctxp", [P, T])
        keys = sb("keys", [P, T])
        keyp = mem.pair("keyp", [P, T])
        queryp = mem.pair("queryp", [P, T])
        valuep = mem.pair("valuep", [P, 2, B, P])
        scores = sb("scores", [P, MASKED])
        att = sb("att", [P, MASKED])
        attp = mem.pair("attp", [P, 2, S])
        key_bank = [mem.bank(f"key{i}") for i in range(2)]
        value_bank = [mem.bank(f"value{i}") for i in range(2)]
        score_bank = [mem.bank(f"score{i}") for i in range(2)]
        o_bank = [mem.bank(f"o{i}") for i in range(2)]
        mask_loaded, w_hi, w_lo, w_slot = sem("mask_loaded"), sem("head_w_hi"), sem("head_w_lo"), sem("head_w_slot")
        ctx_loaded, ctx_hi, ctx_lo = sem("ctx3_loaded"), sem("ctx3_hi"), sem("ctx3_lo")
        key_filled, keys_read, key_hi, key_lo = sem("key_filled"), sem("keys_read"), sem("key_hi"), sem("key_lo")
        query_hi, query_lo = sem("query_hi"), sem("query_lo")
        value_turned, value_hi, value_lo = sem("value_turned"), sem("value_hi"), sem("value_lo")
        scored, masked, att_ready, att_hi, att_lo = (sem("scored"), sem("masked"), sem("att_ready"),
                                                     sem("att_hi"), sem("att_lo"))
        ones_set, o_filled, o_read = sem("att_ones_set"), sem("o_filled"), sem("o_read")
        block = ctx.enter_context(nc.Block())

        def part(g):
            return slice(g * GW, (g + 1) * GW)

        @block.sync
        def _(sp):
            sp.dma_start(mask[:, :, :], io["mask"]).then_inc(mask_loaded, 16)
            with sp.Fori(1, KD) as h:
                sp.wait_ge(ctx_lo, h * NG)
                sp.dma_start(ctx_raw[:, :], io["ctx_t"][bass.ds(h * P, P), :]).then_inc(ctx_loaded, 16)

        @block.gpsimd
        def _(pool):
            pool.memset(attp[0][:, 1, 0:H2].bitcast(F32), 1.0)
            pool.memset(attp[1][:, 1, 0:H2].bitcast(F32), 0.0).then_inc(ones_set, 1)
            pool.wait_ge(w_hi, 1)
            pool.tensor_tensor(w_all[1][:, :], w_raw[:, :], whole(w_all[0][:, :]), ALU.subtract).then_inc(w_lo, 1)
            pool.wait_ge(w_lo, 1)

            def place_weights(h):
                wait_count(pool, key_filled, h * NG)
                for n in range(2):
                    pool.tensor_copy(w_head[n][:, :], whole(w_all[n][:, bass.ds(h * P, P)])).then_inc(w_slot, 1)

            place_weights(0)
            with pool.Fori(1, KD) as h:
                place_weights(h)

        @block.scalar
        def _(act):
            act.wait_ge(kept.head_loaded, 16)
            act.activation(w_all[0][:, :], w_raw[:, :], ACT.Copy).then_inc(w_hi, 1)

            def ctx_parts(h):
                if starts(h):
                    act.wait_ge(kept.ctx_loaded, 16)
                else:
                    act.wait_ge(ctx_loaded, h * 16)
                wait_count(act, key_filled, h * NG)
                for g in range(NG):
                    act.activation(ctxp[0][:, part(g)], ctx_raw[:, part(g)], ACT.Copy).then_inc(ctx_hi, 1)

            def read_keys(h):
                for g in range(NG):
                    act.wait_ge(key_filled, h * NG + g + 1)
                    if g == 0:
                        wait_count(act, value_turned, h * NG)
                        wait_count(act, key_lo, h * NG)
                    act.activation(keys[:, part(g)], key_bank[g % 2][:, :], ACT.Copy).then_inc(keys_read, 1)

            def queries(h):
                wait_count(act, scored, h * 2)
                for g in range(NG):
                    act.activation(queryp[0][:, part(g)], kept.queries[:, h, part(g)], ACT.Copy).then_inc(query_hi, 1)

            def values(h):
                for g in range(NG):
                    act.wait_ge(value_turned, h * NG + g + 1)
                    if g == 0:
                        wait_count(act, o_filled, h * 4)
                    act.activation(valuep[0][:, :, 2 * g:2 * g + 2, :].rearrange("p t b d -> p b t d"),
                                   value_bank[g % 2][:, :].rearrange("p (b t d) -> p b t d", b=2, t=2),
                                   ACT.Copy).then_inc(value_hi, 1)

            def outputs(h):
                act.wait_ge(query_lo, h * NG + NG)
                for n in range(4):
                    s, half = n // 2, n % 2
                    act.wait_ge(o_filled, h * 4 + n + 1)
                    act.activation(kept.queries[:, h, :].rearrange("p (b s d) -> p b s d", s=2, d=P)[:, 4 * half:4 * half + 4, s, :],
                                   o_bank[n % 2][:, :].rearrange("p (b d) -> p b d", b=4), ACT.Copy).then_inc(o_read, 1)

            def head(h, more):
                values(h)
                if more:
                    ctx_parts(h + 1)
                    read_keys(h + 1)
                    queries(h + 1)
                outputs(h)

            ctx_parts(0)
            queries(0)
            read_keys(0)
            head(0, True)
            with act.Fori(1, KD - 1) as h:
                head(h, True)
            head(KD - 1, False)

        @block.vector
        def _(dve):
            def ctx_parts(h):
                for g in range(NG):
                    dve.wait_ge(ctx_hi, h * NG + g + 1)
                    dve.tensor_tensor(ctxp[1][:, part(g)], ctx_raw[:, part(g)], whole(ctxp[0][:, part(g)]),
                                      ALU.subtract).then_inc(ctx_lo, 1)

            def split_keys(h):
                wait_count(dve, scored, h * 2)
                for g in range(NG):
                    dve.wait_ge(keys_read, h * NG + g + 1)
                    dve.tensor_copy(keyp[0][:, part(g)], keys[:, part(g)]).then_inc(key_hi, 1)
                for g in range(NG):
                    dve.wait_ge(key_hi, h * NG + g + 1)
                    dve.tensor_tensor(keyp[1][:, part(g)], keys[:, part(g)], whole(keyp[0][:, part(g)]),
                                      ALU.subtract).then_inc(key_lo, 1)

            def queries(h):
                for g in range(NG):
                    dve.wait_ge(query_hi, h * NG + g + 1)
                    dve.tensor_tensor(queryp[1][:, part(g)], kept.queries[:, h, part(g)], whole(queryp[0][:, part(g)]),
                                      ALU.subtract).then_inc(query_lo, 1)

            def values(h):
                for g in range(NG):
                    dve.wait_ge(value_hi, h * NG + g + 1)
                    for b in range(2):
                        done = dve.tensor_tensor(valuep[1][:, :, 2 * g + b, :],
                                                 value_bank[g % 2][:, b * S:(b + 1) * S].rearrange("p (t d) -> p t d", t=2),
                                                 whole(valuep[0][:, :, 2 * g + b, :]), ALU.subtract)
                    done.then_inc(value_lo, 1)

            def attention(h):
                for t, (a, b) in enumerate(((0, S), (S, MASKED))):
                    n = 2 * h + t
                    place = (slice(None), t, slice(H2 * t, S))
                    dve.wait_ge(scored, n + 1)
                    dve.tensor_tensor(scores[:, a:b], score_bank[t][:, 0:b - a], mask[:, h, a:b], ALU.mult).then_inc(masked, 1)
                    dve.wait_ge(masked, n + 1)
                    dve.scalar_tensor_tensor(att[:, a:b], scores[:, a:b], -1.0, scores[:, a:b], ALU.mult, ALU.max
                                             ).then_inc(att_ready, 1)
                    dve.wait_ge(att_ready, n + 1)
                    dve.tensor_scalar(attp[0][place], att[:, a:b], 1.0, None, ALU.max).then_inc(att_hi, 1)
                    dve.wait_ge(att_hi, n + 1)
                    dve.scalar_tensor_tensor(attp[1][place], att[:, a:b], 1.0, whole(attp[0][place]),
                                             ALU.max, ALU.subtract).then_inc(att_lo, 1)

            def head(h, more):
                values(h)
                if more:
                    ctx_parts(h + 1)
                wait_count(dve, o_filled, h * 4)
                attention(h)
                if more:
                    split_keys(h + 1)
                    queries(h + 1)

            dve.wait_ge(mask_loaded, 16)
            ctx_parts(0)
            queries(0)
            split_keys(0)
            head(0, True)
            with dve.Fori(1, KD - 1) as h:
                head(h, True)
            head(KD - 1, False)

        @block.tensor
        def _(pe):
            pe.wait_ge(ones_set, 1)

            def make_keys(h):
                pe.wait_ge(w_slot, h * 2 + 2)
                for g in range(NG):
                    pe.wait_ge(ctx_lo, h * NG + g + 1)
                    wait_count(pe, keys_read, h * NG + g - 1)
                    product(pe, key_bank[g % 2][:, :], [w[:, :] for w in w_head],
                            [c[:, part(g)] for c in ctxp]).then_inc(key_filled, 1)

            def head(h, more):
                for g in range(NG):
                    pe.wait_ge(keys_read, h * NG + g + 1)
                    wait_count(pe, value_lo, h * NG + g - 1)
                    for i in range(GT):
                        col = g * GW + i * P
                        done = pe.transpose(value_bank[g % 2][:, i * P:(i + 1) * P], keys[:, col:col + P], kept.ident[:, :])
                    done.then_inc(value_turned, 1)
                pe.wait_ge(key_lo, h * NG + NG)
                pe.wait_ge(query_lo, h * NG + NG)
                wait_count(pe, masked, h * 2)
                for t in range(2):
                    for b in range(B):
                        k, q = b * S + t * H2, b * S + t * H2
                        done = product(pe, score_bank[t][:, 0:S - t * H2], [w[:, k:k + P] for w in keyp],
                                       [x[:, q:(b + 1) * S] for x in queryp], first=(b == 0), last=(b == B - 1))
                    done.then_inc(scored, 1)
                if more:
                    make_keys(h + 1)
                pe.wait_ge(value_lo, h * NG + NG)
                pe.wait_ge(att_lo, h * 2 + 2)
                for n in range(4):
                    s, half = n // 2, n % 2
                    wait_count(pe, o_read, h * 4 + n - 1)
                    for t in range(2):
                        done = product(pe, o_bank[n % 2][:, :], [a[:, t, s * P:(s + 1) * P] for a in attp],
                                       [v[:, t, 4 * half:4 * half + 4, :] for v in valuep], first=(t == 0), last=(t == 1))
                    done.then_inc(o_filled, 1)

            make_keys(0)
            head(0, True)
            with pe.Fori(1, KD - 1) as h:
                head(h, True)
            head(KD - 1, False)


def output_stage(nc, kept, io):
    GN_EPS = 1e-3
    with ExitStack() as ctx:
        mem = Memory(nc, ctx)
        sb, sem = mem.sb, mem.sem
        w_out = mem.pair("w_out", [P, KD, D])
        split = Split(mem, "out_w", [(io["wo"][k * P:(k + 1) * P, :], w_out[0][:, k], w_out[1][:, k], D) for k in range(KD)])
        norm = Norm(mem, "out_norm", GN_EPS, kept.passed)
        gamma_beta = sb("gamma_beta", [P, 2, KD])
        yn = sb("yn", [P, GT, D])
        yt = sb("yt", [P, 2, GW])
        z = sb("z", [P, 2, GW])
        zp = [mem.pair(f"zp{i}", [P, KD, GW]) for i in range(2)]
        turn_bank = [mem.bank(f"turn4{c}") for c in range(KD)]
        row_bank = [mem.bank(f"row4{i}") for i in range(4)]
        small_loaded = sem("gamma_loaded")
        turned, y_read, z_ready, z_hi, z_lo = sem("turned4"), sem("y_read"), sem("z_ready"), sem("z_hi"), sem("z_lo")
        row_filled, row_added = sem("row4_filled"), sem("row4_added")
        block = ctx.enter_context(nc.Block())

        def out_row(g, i):
            return kept.queries[:, :, bass.ds(g * GW + i * P, P)]

        @block.gpsimd
        def _(pool):
            norm.pool_start(pool)
            norm.on_pool(pool, 0)
            split.on_pool(pool, range(len(split.parts)))
            norm.on_pool(pool, 1)
            with pool.Fori(2, NG) as g:
                norm.on_pool(pool, g)

        @block.sync
        def _(sp):
            split.load(sp)

        @block.scalar
        def _(act):
            act.dma_start(gamma_beta[:, :, :], io["gamma_beta"]).then_inc(small_loaded, 16)
            split.on_scalar(act, range(len(split.parts)))
            act.wait_ge(small_loaded, 16)

            def gated(g, slot):
                for c in range(KD):
                    n = g * KD + c
                    act.wait_ge(turned, n + 1)
                    wait_count(act, z_ready, n - 1)
                    act.activation(yt[:, c % 2], turn_bank[c][:, :], ACT.Identity, scale=gamma_beta[:, 0, c:c + 1],
                                   bias=gamma_beta[:, 1, c:c + 1]).then_inc(y_read, 1)
                    act.wait_ge(z_ready, n + 1)
                    if c == 0:
                        wait_count(act, row_filled, g * GT - GT)
                    act.activation(zp[slot][0][:, c], z[:, c % 2], ACT.Copy).then_inc(z_hi, 1)

            for g in range(NG):
                gated(g, g % 2)

        @block.vector
        def _(dve):
            def norms(g):
                for i in range(GT):
                    norm.stats_on_vector(dve, g, i, out_row(g, i))
                norm.meanvar_on_vector(dve, g)
                wait_count(dve, turned, g * KD)
                for i in range(GT):
                    norm.rows_on_vector(dve, i, out_row(g, i), yn[:, i, :].rearrange("p (h d) -> p h d", h=KD))

            def gated(g, slot):
                for c in range(KD):
                    n = g * KD + c
                    dve.wait_ge(y_read, n + 1)
                    dve.tensor_tensor(z[:, c % 2], yt[:, c % 2], kept.ogate[:, c, bass.ds(g * GW, GW)], ALU.mult
                                      ).then_inc(z_ready, 1)
                    dve.wait_ge(z_hi, n + 1)
                    dve.tensor_tensor(zp[slot][1][:, c], z[:, c % 2], whole(zp[slot][0][:, c]), ALU.subtract).then_inc(z_lo, 1)

            def rows(g):
                for i in range(GT):
                    row = kept.x[:, g * GT + i, :]
                    dve.wait_ge(row_filled, g * GT + i + 1)
                    dve.tensor_tensor(row, row, row_bank[i][:, :], ALU.add).then_inc(row_added, 1)

            def step(g, slot):
                norms(g + 1)
                gated(g, slot)
                rows(g - 1)

            norms(0)
            norms(1)
            gated(0, 0)
            step(1, 1)
            step(2, 0)
            gated(NG - 1, 1)
            rows(NG - 2)
            rows(NG - 1)

        @block.tensor
        def _(pe):
            def turns(g):
                pe.wait_ge(norm.normed, g * GT + GT)
                for c in range(KD):
                    wait_count(pe, y_read, (g - 1) * KD + c + 1)
                    for i in range(GT):
                        done = pe.transpose(turn_bank[c][:, i * P:(i + 1) * P], yn[:, i, c * P:(c + 1) * P], kept.ident[:, :])
                    done.then_inc(turned, 1)

            def rows(g):
                pe.wait_ge(split.lo_ready, KD)
                pe.wait_ge(z_lo, g * KD + KD)
                for i in range(GT):
                    wait_count(pe, row_added, g * GT - GT + i + 1)
                    for k in range(KD):
                        done = product(pe, row_bank[i][:, :], [x[:, k, i * P:(i + 1) * P] for x in zp[g % 2]],
                                       [w[:, k] for w in w_out], first=(k == 0), last=(k == KD - 1))
                    done.then_inc(row_filled, 1)

            turns(0)
            for g in range(NG):
                if g + 1 < NG:
                    turns(g + 1)
                rows(g)


def router_stage(nc, kept, io):
    NH = 2 * HID // P
    with ExitStack() as ctx:
        mem = Memory(nc, ctx)
        sb, sem = mem.sb, mem.sem
        w_route, w_up, w_down = mem.pair("w_route", [P, KD, P]), mem.pair("w_shup", [P, KD, D]), mem.pair("w_shdown", [P, NH, D])
        split = Split(mem, "shared_w",
                      [(io["w_router"].rearrange("(k p) e -> p k e", p=P), w_route[0][:, :, 0:E1], w_route[1][:, :, 0:E1], KD * E1)]
                      + [(io["wsh_up"][k * P:(k + 1) * P, :], w_up[0][:, k], w_up[1][:, k], D) for k in range(KD)]
                      + [(io["wsh_down"][j * P:(j + 1) * P, :], w_down[0][:, j], w_down[1][:, j], D) for j in range(NH)])
        norm = Norm(mem, "route_norm", LN_EPS, kept.passed)
        xn = sb("xn3", [P, GT, D])
        xnt = mem.pair("xn3t", [P, KD, T])
        hid = sb("hid5", [P, 2, GW])
        hidp = mem.pair("hid5p", [P, NH, GW])
        logit_t = sb("logit5_t", [E1, GW])
        logits = sb("logits5", [P, NT, E1])
        peak, total_exp = sb("peak", [P, NT]), sb("total_exp", [P, NT])
        probs = sb("probs5", [P, NT, E1])
        top8, index8 = sb("top8_5", [P, NT, 8]), sb("index8", [P, NT, 8], U32)
        expert_no, slot_no, lane_no = sb("expert_no", [P, E1]), sb("slot_no", [P, SLOTS]), sb("lane_no", [P, P])
        tile_ends, tile_no, row_no = sb("tile_ends", [P, NT + 1]), sb("tile_no", [P, NT]), sb("row_no", [P, 1])
        keep = sb("keep", [P, E1, NT])
        before_me, all_ones = sb("before_me", [P, P], BF16), sb("all_ones", [P, P], BF16)
        choice = sb("choice", [P, 2, NT])
        picked = sb("picked", [P, 2, NT, E1])
        member = sb("member", [P, NT, E1], BF16)
        counts = sb("counts", [P, E1, NT])
        base = sb("base", [P, NT, E1])
        wide = sb("wide", [P, SLOTS, E1])
        tiles, slot_end, slot_start = sb("tiles5", [P, E1]), sb("slot_end", [P, E1]), sb("slot_start", [P, E1])
        slot_of = sb("slot_of", [P, SLOTS])
        rank, first, skip, lane = (sb(n, [P, 2, NT]) for n in ("rank", "first_slot", "skip_slots", "lane"))
        lane_hot = split.raw[:, 0:4, :].rearrange("p n m -> p (n m)").bitcast(BF16).rearrange("p (c j l) -> p c j l", c=2, j=NT)
        slot_ids = sb("slot_ids", [P, 2, NT, 2, SLOTS], BF16)
        id_part = sb("id_part", [P, SLOTS])

        turn_bank = [mem.bank(f"turn5{i}") for i in range(2)]
        logit_bank, plan_bank = mem.bank("logit5"), mem.bank("plan5")
        up_bank = [mem.bank(f"up5{i}") for i in range(2)]
        row_bank = [mem.bank(f"row5{i}") for i in range(2)]
        set_pool, set_dve = sem("set5_pool"), sem("set5_dve")
        row_stored = [sem(f"row5_stored{i}") for i in range(GT)]
        turned, hi_ready, lo_ready = sem("turned5"), sem("xn3t_hi"), sem("xn3t_lo")
        logit_filled, logit_read = sem("logit_filled"), sem("logit_read")
        logit_turned, logits_ready = sem("logit_turned"), sem("logits_ready")
        up_filled, gelu_ready, hid_hi, hid_lo = sem("up5_filled"), sem("gelu_ready"), sem("hid5_hi"), sem("hid5_lo")
        row_filled, row_added = sem("row5_filled"), sem("row5_added")
        shifted, exped, plan = sem("shifted"), sem("exped"), sem("plan_steps")
        member_ready, counted, ids_hot, ids_filled = sem("member_ready"), sem("counted"), sem("ids_hot"), sem("ids_filled")
        block = ctx.enter_context(nc.Block())

        def by_chunk(ap):
            return ap.rearrange("p (c t) -> p c t", c=KD)

        def flat(ap):
            return ap.rearrange("p a b -> p (a b)")

        def staggered(ahead, logits_part, shared_part):
            for g in range(NG + 1):
                if g < NG:
                    ahead(g)
                if g > 0:
                    logits_part(g - 1)
                if 2 <= g < NG:
                    shared_part(g - 2)

        @block.sync
        def _(sp):
            rows = kept.xn_dram.rearrange("(n p) d -> p n d", p=P)
            with sp.Fori(0, NG) as g:
                for i in range(GT):
                    sp.wait_ge(norm.normed, g * GT + i + 1)
                    sp.dma_start(rows[:, bass.ds(g * GT + i, 1), :].rearrange("p n d -> p (n d)"), xn[:, i, :]
                                 ).then_inc(row_stored[i], 16)
            for i in range(GT):
                sp.wait_ge(row_stored[i], 16 * NG)

        @block.gpsimd
        def _(pool):
            norm.pool_start(pool)
            for tile, pattern, base_value, per_partition in (
                    (expert_no[:, :], [[1, E1]], 0, 0), (slot_no[:, :], [[1, SLOTS]], 0, 0),
                    (lane_no[:, :], [[1, P]], 0, 0), (tile_ends[:, :], [[P, NT + 1]], 0, 0),
                    (tile_no[:, :], [[1, NT]], 0, 0), (row_no[:, :], [[1, 1]], 0, 1)):
                pool.iota(tile, pattern, base=base_value, channel_multiplier=per_partition,
                          allow_small_or_imprecise_dtypes=True)
            pool.memset(keep[:, :, :], 1.0)
            pool.memset(all_ones[:, :], 1.0).then_inc(set_pool, 1)
            pool.wait_ge(set_pool, 1)
            pool.memset(keep[:, :, 0:1], 0.0)
            pool.affine_select(out=before_me[:, :], in_=kept.ones[:, :], pattern=[[1, P]], compare_op=ALU.is_gt,
                               fill=0.0, base=0, channel_multiplier=-1).then_inc(set_pool, 1)
            norm.on_pool(pool, 0)
            split.on_pool(pool, range(1))
            norm.on_pool(pool, 1)
            split.on_pool(pool, range(1, 1 + KD))
            norm.on_pool(pool, 2)
            split.on_pool(pool, range(1 + KD, len(split.parts)))
            norm.on_pool(pool, 3)

        @block.scalar
        def _(act):
            split.load(act)

            def ahead(g):
                for i in range(GT):
                    act.wait_ge(turned, g * GT + i + 1)
                    act.activation(xnt[0][:, :, bass.ds(g * GW + i * P, P)], by_chunk(turn_bank[i % 2][:, :]),
                                   ACT.Copy).then_inc(hi_ready, 1)

            def logits_part(g):
                act.wait_ge(logit_filled, g + 1)
                wait_count(act, logit_turned, g)
                act.activation(logit_t[:, :], logit_bank[0:E1, :], ACT.Copy).then_inc(logit_read, 1)
                act.wait_ge(logit_turned, g + 1)
                act.activation(flat(logits[:, bass.ds(g * GT, GT), :]), plan_bank[:, 0:GT * E1], ACT.Copy
                               ).then_inc(logits_ready, 1)

            def shared_part(g):
                for j in range(NH):
                    n = g * NH + j
                    act.wait_ge(up_filled, n + 1)
                    wait_count(act, hid_lo, n - 1)
                    act.activation(hid[:, j % 2], up_bank[j % 2][:, :], ACT.Gelu).then_inc(gelu_ready, 1)
                    act.wait_ge(gelu_ready, n + 1)
                    if j == 0:
                        wait_count(act, row_filled, g * GT)
                    act.activation(hidp[0][:, j], hid[:, j % 2], ACT.Copy).then_inc(hid_hi, 1)

            def ahead_and_weights(g):
                ahead(g)
                if g == 0:
                    split.on_scalar(act, range(len(split.parts)))

            staggered(ahead_and_weights, logits_part, shared_part)
            act.wait_ge(shifted, 1)
            act.activation(flat(probs[:, :, :]), flat(logits[:, :, :]), ACT.Exp).then_inc(exped, 1)
            shared_part(NG - 2)
            shared_part(NG - 1)

        @block.vector
        def _(dve):
            def norms(g):
                for i in range(GT):
                    norm.stats_on_vector(dve, g, i, kept.x[:, g * GT + i, :])
                norm.meanvar_on_vector(dve, g)
                for i in range(GT):
                    wait_count(dve, turned, g * GT + i - GT + 1)
                    wait_count(dve, row_stored[i], 16 * g)
                    norm.rows_on_vector(dve, i, kept.x[:, g * GT + i, :], xn[:, i, :])

            def ahead(g):
                for i in range(GT):
                    part = bass.ds(g * GW + i * P, P)
                    dve.wait_ge(hi_ready, g * GT + i + 1)
                    dve.tensor_tensor(xnt[1][:, :, part], by_chunk(turn_bank[i % 2][:, :]), whole(xnt[0][:, :, part]),
                                      ALU.subtract).then_inc(lo_ready, 1)
                if g + 1 < NG:
                    norms(g + 1)

            def split_hidden(g, chunks):
                for j in chunks:
                    dve.wait_ge(hid_hi, g * NH + j + 1)
                    dve.tensor_tensor(hidp[1][:, j], hid[:, j % 2], whole(hidp[0][:, j]), ALU.subtract).then_inc(hid_lo, 1)

            def add_rows(g, tiles):
                for i in tiles:
                    row = kept.x[:, g * GT + i, :]
                    dve.wait_ge(row_filled, g * GT + i + 1)
                    dve.tensor_tensor(row, row, row_bank[i % 2][:, :], ALU.add).then_inc(row_added, 1)

            def shared_part(g):
                split_hidden(g, range(NH))
                add_rows(g, range(GT))

            step = Ticks(plan)

            def on(ins):
                dve.wait_ge(plan, step.tick(ins))

            def along(ap, n, axis):
                shape = list(ap.shape)
                shape.insert(axis, n)
                return ap.unsqueeze(axis).to_broadcast(shape)

            def choose():
                dve.wait_ge(logits_ready, NG)
                on(dve.tensor_reduce(peak[:, :], logits[:, :, :], AX_X, ALU.max))
                dve.tensor_tensor(logits[:, :, :], logits[:, :, :], along(peak[:, :], E1, 2), ALU.subtract).then_inc(shifted, 1)
                dve.wait_ge(exped, 1)
                on(dve.tensor_reduce(total_exp[:, :], probs[:, :, :], AX_X, ALU.add))
                on(dve.reciprocal(total_exp[:, :], total_exp[:, :]))
                on(dve.tensor_tensor(probs[:, :, :], probs[:, :, :], along(total_exp[:, :], E1, 2), ALU.mult))
                for j in range(NT):
                    last = step.tick(dve.max(top8[:, j], probs[:, j]))
                for j in range(NT):
                    dve.wait_ge(plan, last - NT + 1 + j)
                    found = step.tick(dve.max_index(index8[:, j], top8[:, j], probs[:, j]))
                step.tick(dve.tensor_copy(kept.route_gate[:, :, :], top8[:, :, 0:2].rearrange("p j c -> p c j")))
                dve.wait_ge(plan, found)
                on(dve.tensor_copy(choice[:, :, :], index8[:, :, 0:2].rearrange("p j c -> p c j")))
                dve.wait_ge(set_pool, 2)
                for c in range(2):
                    last = step.tick(dve.tensor_tensor(picked[:, c], along(expert_no[:, :], NT, 1),
                                                       along(choice[:, c], E1, 2), ALU.is_equal))
                dve.wait_ge(plan, last)
                dve.tensor_tensor(member[:, :, :], picked[:, 0], picked[:, 1], ALU.add).then_inc(member_ready, 1)

            def plan_slots():
                before = plan_bank[:, 0:NT * E1].rearrange("p (j e) -> p j e", j=NT)
                total = plan_bank[:, NT * E1:2 * NT * E1].rearrange("p (j e) -> p j e", j=NT)
                dve.wait_ge(counted, 1)
                on(dve.tensor_copy(counts[:, :, :], total.rearrange("p j e -> p e j")))
                on(dve.tensor_tensor_scan(flat(counts[:, :, :]), flat(keep[:, :, :]), flat(counts[:, :, :]), 0.0,
                                          ALU.mult, ALU.add))
                on(dve.tensor_tensor(base[:, :, :], counts[:, :, :].rearrange("p e j -> p j e"), total, ALU.subtract))
                on(dve.tensor_tensor(base[:, :, :], base[:, :, :], before, ALU.add))
                on(dve.tensor_tensor(wide[:, 0:E1, :], along(counts[:, :, NT - 1], NT, 2), along(tile_ends[:, 0:NT], E1, 1),
                                     ALU.is_gt))
                on(dve.tensor_reduce(tiles[:, :], wide[:, 0:E1, :], AX_X, ALU.add))
                on(dve.tensor_tensor_scan(slot_end[:, :], all_ones[:, 0:E1], tiles[:, :], 0.0, ALU.mult, ALU.add))
                on(dve.tensor_tensor(slot_start[:, :], slot_end[:, :], tiles[:, :], ALU.subtract))
                on(dve.tensor_tensor(wide[:, :, :], along(slot_end[:, :], SLOTS, 1), along(slot_no[:, :], E1, 2), ALU.is_le))
                on(dve.tensor_reduce(slot_of[:, :], wide[:, :, :], AX_X, ALU.add))
                on(dve.tensor_scalar(kept.slot_expert[:, :], slot_of[:, :], float(E1 - 1), None, ALU.min))

            def place(c):
                part = wide[:, 16 * c:16 * c + NT, :]
                on(dve.tensor_tensor(part, picked[:, c], base[:, :, :], ALU.mult))
                on(dve.tensor_reduce(rank[:, c], part, AX_X, ALU.add))
                on(dve.tensor_tensor(part, picked[:, c], along(slot_start[:, :], NT, 1), ALU.mult))
                on(dve.tensor_reduce(first[:, c], part, AX_X, ALU.add))
                on(dve.tensor_tensor(part, along(rank[:, c], NT, 2), along(tile_ends[:, 1:NT + 1], NT, 1), ALU.is_ge))
                on(dve.tensor_reduce(skip[:, c], part, AX_X, ALU.add))
                on(dve.tensor_tensor(first[:, c], first[:, c], skip[:, c], ALU.add))
                on(dve.scalar_tensor_tensor(lane[:, c], skip[:, c], float(-P), rank[:, c], ALU.mult, ALU.add))
                on(dve.scalar_tensor_tensor(kept.route_row[:, c], first[:, c], float(P), lane[:, c], ALU.mult, ALU.add))

            def number_slots(c):
                step.tick(dve.tensor_tensor(lane_hot[:, c], along(lane_no[:, :], NT, 1), along(lane[:, c], P, 2),
                                            ALU.is_equal))
                slot_hot = slot_ids[:, c, :, 1, :]
                on(dve.tensor_tensor(slot_hot, along(slot_no[:, :], NT, 1), along(first[:, c], SLOTS, 2), ALU.is_equal))
                on(dve.tensor_scalar(slot_ids[:, c, :, 0, :], slot_hot, row_no[:, 0:1], None, ALU.mult))
                dve.tensor_tensor(slot_hot, slot_hot, along(tile_no[:, :], SLOTS, 2), ALU.mult).then_inc(ids_hot, 1)

            norms(0)
            for part in w_route:
                dve.memset(part[:, :, E1:P].bitcast(F32), 0.0).then_inc(set_dve, 1)
            staggered(ahead, lambda g: None, shared_part)
            choose()
            split_hidden(NG - 2, range(NH))
            plan_slots()
            add_rows(NG - 2, (0, 1))
            place(0)
            add_rows(NG - 2, (2, 3))
            place(1)
            split_hidden(NG - 1, (0, 1))
            dve.wait_ge(split.lo_ready, len(split.parts))
            number_slots(0)
            split_hidden(NG - 1, (2, 3))
            number_slots(1)
            add_rows(NG - 1, range(GT))
            dve.wait_ge(ids_filled, 1)
            on(dve.tensor_copy(id_part[:, :], plan_bank[:, 0:SLOTS]))
            on(dve.scalar_tensor_tensor(kept.slot_token[:, :], plan_bank[:, SLOTS:2 * SLOTS], float(P), id_part[:, :],
                                        ALU.mult, ALU.add))

        @block.tensor
        def _(pe):
            def ahead(g):
                for i in range(GT):
                    pe.wait_ge(norm.normed, g * GT + i + 1)
                    wait_count(pe, lo_ready, g * GT + i - 1)
                    for c in range(KD):
                        done = pe.transpose(turn_bank[i % 2][:, c * P:(c + 1) * P], xn[:, i, c * P:(c + 1) * P],
                                            kept.ident[:, :])
                    done.then_inc(turned, 1)

            def logits_part(g):
                pe.wait_ge(lo_ready, g * GT + GT)
                pe.wait_ge(split.lo_ready, 1)
                pe.wait_ge(set_dve, 2)
                wait_count(pe, logit_read, g)
                for k in range(KD):
                    done = product(pe, logit_bank[:, :], [w[:, k] for w in w_route],
                                   [x[:, k, bass.ds(g * GW, GW)] for x in xnt], first=(k == 0), last=(k == KD - 1))
                done.then_inc(logit_filled, 1)
                pe.wait_ge(logit_read, g + 1)
                wait_count(pe, logits_ready, g)
                for i in range(GT):
                    done = pe.transpose(plan_bank[:, i * E1:(i + 1) * E1], logit_t[:, i * P:(i + 1) * P],
                                        kept.ident[0:E1, 0:E1])
                done.then_inc(logit_turned, 1)

            def up_part(g):
                pe.wait_ge(split.lo_ready, len(split.parts))
                for j in range(NH):
                    n = g * NH + j
                    wait_count(pe, gelu_ready, n - 1)
                    for k in range(KD):
                        done = product(pe, up_bank[j % 2][:, :], [w[:, k, j * P:(j + 1) * P] for w in w_up],
                                       [x[:, k, bass.ds(g * GW, GW)] for x in xnt], first=(k == 0), last=(k == KD - 1))
                    done.then_inc(up_filled, 1)

            def down_part(g):
                pe.wait_ge(hid_lo, g * NH + NH)
                for i in range(GT):
                    wait_count(pe, row_added, g * GT + i - 1)
                    for j in range(NH):
                        done = product(pe, row_bank[i % 2][:, :], [h[:, j, i * P:(i + 1) * P] for h in hidp],
                                       [w[:, j] for w in w_down], first=(j == 0), last=(j == NH - 1))
                    done.then_inc(row_filled, 1)

            def shared_part(g):
                up_part(g)
                down_part(g)

            staggered(ahead, logits_part, shared_part)
            up_part(NG - 2)
            pe.wait_ge(member_ready, 1)
            pe.wait_ge(logits_ready, NG)
            pe.wait_ge(set_pool, 2)
            pe.matmul(plan_bank[:, 0:NT * E1], before_me[:, :], flat(member[:, :, :]), start=True, stop=True)
            pe.matmul(plan_bank[:, NT * E1:2 * NT * E1], all_ones[:, :], flat(member[:, :, :]), start=True, stop=True
                      ).then_inc(counted, 1)
            down_part(NG - 2)
            shared_part(NG - 1)
            pe.wait_ge(ids_hot, 2)
            for c in range(2):
                for j in range(NT):
                    done = pe.matmul(plan_bank[:, 0:2 * SLOTS], lane_hot[:, c, j], flat(slot_ids[:, c, j]),
                                     start=(c == 0 and j == 0), stop=(c == 1 and j == NT - 1))
            done.then_inc(ids_filled, 1)


def routed_stage(nc, kept, io):
    CU, CD = KD * HID, HJ * D
    AHEAD = 2
    SETS = 4
    with ExitStack() as ctx:
        mem = Memory(nc, ctx)
        sb, sem = mem.sb, mem.sem
        w_up, w_down = sb("w_rt_up", [P, E1, CU]), sb("w_rt_down", [P, E1, CD])
        rows = sb("slot_rows", [P, 2, D])
        index = [sb(f"slot_index{i}", [P, 1], I32) for i in range(2)]
        xt = [sb(f"slot_xt{i}", [P, KD, P]) for i in range(2)]
        mid = [sb(f"slot_mid{i}", [P, HID]) for i in range(2)]
        mid_t = [sb(f"slot_mid_t{i}", [P, HJ, P]) for i in range(2)]
        y = sb("slot_y", [P, 2, D])
        turn_bank = [mem.bank(f"turn6{i}") for i in range(2)]
        up_bank = [mem.bank(f"up6{i}") for i in range(2)]
        mid_bank = [mem.bank(f"mid6{i}") for i in range(2)]
        y_bank = [mem.bank(f"y6{i}") for i in range(2)]
        w_loaded, w_ready = [sem(f"rt_w_loaded{e}") for e in range(E1)], sem("rt_w_ready")
        fetched, indexed = [sem("fetched_even"), sem("fetched_odd")], sem("indexed")
        turned, xt_ready = sem("rows_turned"), sem("xt_ready")
        up_filled, mid_ready, mid_turned, mid_t_ready = sem("up6_filled"), sem("mid_ready"), sem("mid_turned"), sem("mid_t_ready")
        y_filled, y_ready = sem("y6_filled"), sem("y6_ready")
        y_stored = [sem("y_stored_even"), sem("y_stored_odd")]
        picks = sb("picks", [P, SETS, 2, D])
        pick_index = [[sb(f"pick_index{i}_{c}", [P, 1], I32) for c in range(2)] for i in range(SETS)]
        pick_indexed, picks_fetched = sem("pick_indexed"), [sem(f"picks_fetched{i}") for i in range(SETS)]
        half, added, out_stored = sem("first_added"), sem("both_added"), sem("out_stored")
        block = ctx.enter_context(nc.Block())

        def tiles(eng, one):
            for i in range(SETS):
                one(i, i, 0)
            with eng.Fori(1, NT // SETS) as r:
                for i in range(SETS):
                    one(r * SETS + i, i, r)

        def slots(eng, one):
            one(0, 0)
            one(1, 1)
            with eng.Fori(1, SLOTS // 2) as pair:
                s = 2 * pair
                one(s, 0)
                one(s + 1, 1)
            one(SLOTS - 1, (SLOTS - 1) % 2)

        @block.sync
        def _(sp):
            def load(e):
                sp.dma_start(w_up[:, e], io["wrt_up"][e]).then_inc(w_loaded[e], 16)
                sp.dma_start(w_down[:, e], io["wrt_down"][e]).then_inc(w_loaded[e], 16)

            for e in range(AHEAD):
                load(e)
            for e in range(E1):
                sp.wait_ge(w_loaded[e], 32)
                sp.sem_inc(w_ready, 1)
                if e + AHEAD < E1:
                    load(e + AHEAD)

            out = io["out"].rearrange("(n p) d -> p n d", p=P)

            def store(j, i, r):
                sp.wait_ge(added, j + 1)
                sp.dma_start(out[:, bass.ds(j, 1), :], kept.x[:, bass.ds(j, 1), :]).then_inc(out_stored, 16)

            tiles(sp, store)
            sp.wait_ge(out_stored, 16 * NT)

        @block.gpsimd
        def _(pool):
            def fetch(s, i):
                wait_count(pool, fetched[i], (s - i) * 8)
                pool.tensor_copy(index[i][:, :], kept.slot_token[:, bass.ds(s, 1)]).then_inc(indexed, 1)
                pool.wait_ge(indexed, s + 1)
                wait_alone(pool, turned, s - 1, kept.passed)
                pool.indirect_dma_start(rows[:, i, :], None, kept.xn_dram, bass.IndirectOffsetOnAxis(index[i][:, :], 0)
                                        ).then_inc(fetched[i], 16)

            def fetch_back(j, i, r):
                wait_count(pool, added, j - SETS + 1)
                for c in range(2):
                    pool.tensor_copy(pick_index[i][c][:, :], kept.route_row[:, c, bass.ds(j, 1)]).then_inc(pick_indexed, 1)
                wait_alone(pool, pick_indexed, 2 * j + 2, kept.passed)
                for c in range(2):
                    pool.indirect_dma_start(picks[:, i, c, :], None, kept.y_dram, bass.IndirectOffsetOnAxis(pick_index[i][c][:, :], 0)
                                            ).then_inc(picks_fetched[i], 16)

            slots(pool, fetch)
            pool.wait_ge(y_stored[0], 16 * ((SLOTS + 1) // 2))
            pool.wait_ge(y_stored[1], 16 * (SLOTS // 2))
            tiles(pool, fetch_back)

        @block.scalar
        def _(act):
            def hidden(s, i):
                act.wait_ge(up_filled, s + 1)
                wait_count(act, mid_turned, s - 1)
                act.activation(mid[i][:, :], up_bank[i][:, 0:HID], ACT.Gelu).then_inc(mid_ready, 1)
                act.wait_ge(mid_turned, s + 1)
                wait_count(act, y_filled, s - 1)
                act.activation(mid_t[i][:, :, :].rearrange("p j t -> p (j t)"), mid_bank[i][:, 0:HID], ACT.Copy
                               ).then_inc(mid_t_ready, 1)

            def store(s, i):
                act.wait_ge(y_ready, s + 1)
                act.dma_start(kept.y_dram[bass.ds(s * P, P), :], y[:, i, :]).then_inc(y_stored[i], 16)

            def hidden_and_store(s, i):
                hidden(s, i)
                store(s - 1, 1 - i)

            hidden(0, 0)
            hidden_and_store(1, 1)
            with act.Fori(1, SLOTS // 2) as pair:
                s = 2 * pair
                hidden_and_store(s, 0)
                hidden_and_store(s + 1, 1)
            hidden_and_store(SLOTS - 1, 0)
            store(SLOTS - 1, 0)

        @block.vector
        def _(dve):
            def turned_rows(s, i):
                dve.wait_ge(turned, s + 1)
                wait_count(dve, up_filled, s - 1)
                dve.tensor_copy(xt[i][:, :, :].rearrange("p k t -> p (k t)"), turn_bank[i][:, :]).then_inc(xt_ready, 1)

            def result(s, i):
                dve.wait_ge(y_filled, s + 1)
                stored = (s - i) * 8
                wait_count(dve, y_stored[i], stored)
                dve.tensor_copy(y[:, i, :], y_bank[i][:, :]).then_inc(y_ready, 1)

            turned_rows(0, 0)
            turned_rows(1, 1)
            turned_rows(2, 0)
            result(0, 0)
            turned_rows(3, 1)
            result(1, 1)
            with dve.Fori(1, SLOTS // 2 - 1) as pair:
                s = 2 * pair
                turned_rows(s + 2, 0)
                result(s, 0)
                turned_rows(s + 3, 1)
                result(s + 1, 1)
            turned_rows(SLOTS - 1, 0)
            for s in range(SLOTS - 3, SLOTS):
                result(s, s % 2)

            def add(j, i, r):
                row = kept.x[:, bass.ds(j, 1), :].rearrange("p o d -> p (o d)")
                dve.wait_ge(picks_fetched[i], r * 32 + 32)
                dve.scalar_tensor_tensor(row, picks[:, i, 0, :], kept.route_gate[:, 0, bass.ds(j, 1)], row,
                                         ALU.mult, ALU.add).then_inc(half, 1)
                dve.wait_ge(half, j + 1)
                dve.scalar_tensor_tensor(row, picks[:, i, 1, :], kept.route_gate[:, 1, bass.ds(j, 1)], row,
                                         ALU.mult, ALU.add).then_inc(added, 1)

            tiles(dve, add)

        @block.tensor
        def _(pe):
            def turn(s, i):
                pe.wait_ge(fetched[i], (s - i) * 8 + 16)
                wait_count(pe, xt_ready, s - 1)
                for c in range(KD):
                    done = pe.transpose(turn_bank[i][:, c * P:(c + 1) * P], rows[:, i, c * P:(c + 1) * P], kept.ident[:, :])
                done.then_inc(turned, 1)

            def turn_mid(s, i):
                pe.wait_ge(mid_ready, s + 1)
                wait_count(pe, mid_t_ready, s - 1)
                for j in range(HJ):
                    done = pe.transpose(mid_bank[i][:, j * P:(j + 1) * P], mid[i][:, j * P:(j + 1) * P], kept.ident[:, :])
                done.then_inc(mid_turned, 1)

            def up(s, i, e):
                pe.wait_ge(xt_ready, s + 1)
                wait_count(pe, mid_ready, s - 1)
                for k in range(KD):
                    done = pe.matmul(up_bank[i][:, 0:HID], xt[i][:, k], w_up[:, bass.ds(e, 1), k * HID:(k + 1) * HID]
                                     .rearrange("p o m -> p (o m)"), start=(k == 0), stop=(k == KD - 1))
                done.then_inc(up_filled, 1)

            def down(s, i, e):
                pe.wait_ge(mid_t_ready, s + 1)
                wait_count(pe, y_ready, s - 1)
                for j in range(HJ):
                    done = pe.matmul(y_bank[i][:, :], mid_t[i][:, j], w_down[:, bass.ds(e, 1), j * D:(j + 1) * D]
                                     .rearrange("p o m -> p (o m)"), start=(j == 0), stop=(j == HJ - 1))
                done.then_inc(y_filled, 1)

            def expert(s):
                return pe.value_load(kept.slot_expert[0:1, bass.ds(s, 1)], min_val=0, max_val=E1 - 1)

            def step(s, i, turn_next=True, behind=True):
                e = expert(s)
                pe.wait_ge(w_ready, e + 1)
                if turn_next:
                    turn(s + 1, 1 - i)
                if behind:
                    turn_mid(s - 1, 1 - i)
                up(s, i, e)
                if behind:
                    down(s - 1, 1 - i, expert(s - 1))

            turn(0, 0)
            step(0, 0, behind=False)
            step(1, 1)
            step(2, 0)
            step(3, 1)
            with pe.Fori(2, SLOTS // 2) as pair:
                s = 2 * pair
                step(s, 0)
                step(s + 1, 1)
            step(SLOTS - 1, 0, turn_next=False)
            turn_mid(SLOTS - 1, 0)
            down(SLOTS - 1, 0, expert(SLOTS - 1))


class Kept:
    pass


def build(nc, io):
    kept = Kept()
    with ExitStack() as ctx:
        mem = Memory(nc, ctx)
        kept.gate_dram = nc.dram_tensor("gate_scratch", [E0, T], F32).ap()
        kept.passed = mem.sem("passed")
        kept.x = mem.sb("x_rows", [P, NT, D])
        kept.ident = mem.sb("ident", [P, P])
        kept.ones = mem.sb("ones", [P, P])
        with ExitStack() as latent_ctx:
            kept.latent = Memory(nc, latent_ctx).sb("latent", [P, T])
            kept.finished = mix_stage(nc, kept, io)
            kept.finished = latent_moe_stage(nc, kept, io)
            with ExitStack() as att_ctx:
                att = Memory(nc, att_ctx)
                kept.queries = att.sb("queries", [P, KD, T])
                kept.ogate = att.sb("ogate", [P, KD, T])
                kept.head_raw, kept.ctx_raw = att.sb("head_raw", [P, D]), att.sb("ctx_raw", [P, T])
                kept.head_loaded, kept.ctx_loaded = att.sem("head_loaded"), att.sem("first_ctx_loaded")
                query_stage(nc, kept, io)
                attention_stage(nc, kept, io)
                output_stage(nc, kept, io)
        moe_stages(nc, kept, io, mem)


def moe_stages(nc, kept, io, mem):
    kept.xn_dram = nc.dram_tensor("xn_scratch", [T, D], F32).ap()
    kept.y_dram = nc.dram_tensor("y_scratch", [SLOTS * P, D], F32).ap()
    kept.slot_token = mem.sb("slot_token", [P, SLOTS], I32)
    kept.slot_expert = mem.sb("slot_expert", [P, SLOTS], I32)
    kept.route_row = mem.sb("route_row", [P, 2, NT], I32)
    kept.route_gate = mem.sb("route_gate", [P, 2, NT])
    router_stage(nc, kept, io)
    routed_stage(nc, kept, io)


def decay_mask():
    import numpy as np

    gam = 1.0 - 2.0 ** (-5.0 - np.arange(KD, dtype=np.float64))
    expo = np.arange(S, dtype=np.float64)[None, :] - np.arange(S, dtype=np.float64)[:, None]
    table = np.where(expo[None] <= 0, gam[:, None, None] ** np.minimum(expo, 0.0)[None], 0.0)
    table = table / np.sqrt(table.sum(axis=-1))[:, None, :] / np.sqrt(float(P))
    turned = table.transpose(2, 0, 1)
    return np.ascontiguousarray(np.concatenate([turned[0:P], turned[P:S, :, P:S]], axis=2).astype(np.float32))


def layouts(a):
    import numpy as np

    def rows(x):
        return np.ascontiguousarray(x)

    return {
        "x": rows(a["x"].reshape(T, D)),
        "ctx_t": rows(a["ctx_2048"].reshape(T, D).T),
        "decay_first": rows(np.stack([a["L0_xattn_time_decay"].reshape(KD, P).T,
                                      a["L0_xattn_time_first"].reshape(KD, P).T], axis=1)),
        "bias": rows(a["L0_ffn_biases"].reshape(1, E0)),
        "w_front": rows(np.concatenate([a["L0_ffn_Wdown"].T, a["L0_ffn_swg"].T, a["L0_ffn_sw1"].T,
                                        a["L0_ffn_Wg"].T], axis=1)),
        "sw2_t": rows(a["L0_ffn_sw2"].T),
        "wup_t": rows(a["L0_ffn_Wup"].T),
        "heads": rows(a["L1_xattn_Wh"]),
        "wg": rows(a["L1_xattn_wg_w"]),
        "wo": rows(a["L1_xattn_wo_w"]),
        "gamma_beta": rows(np.stack([a["L1_xattn_gn_gamma"].reshape(KD, P).T,
                                     a["L1_xattn_gn_beta"].reshape(KD, P).T], axis=1)),
        "mask": decay_mask(),
        "w_router": rows(a["L1_ffn_W_router"]),
        "wsh_up": rows(a["L1_ffn_Wsh_up"].transpose(1, 0, 2).reshape(D, 2 * HID)),
        "wsh_down": rows(a["L1_ffn_Wsh_down"].reshape(2 * HID, D)),
        "wrt_up": rows(a["L1_ffn_Wrt_up"].reshape(E1, KD, P, HID).transpose(0, 2, 1, 3).reshape(E1, P, KD * HID)),
        "wrt_down": rows(a["L1_ffn_Wrt_down"].reshape(E1, HJ, P, D).transpose(0, 2, 1, 3).reshape(E1, P, HJ * D)),
        "experts": rows(np.concatenate([a["L0_ffn_rw1"].transpose(0, 2, 1), a["L0_ffn_rwg"].transpose(0, 2, 1),
                                        a["L0_ffn_rw2"].transpose(0, 2, 1).reshape(E0, HJ, P, LAT)
                                        .transpose(0, 2, 1, 3).reshape(E0, P, HJ * LAT)], axis=2)),
    }


def kernel(**inputs):
    import concourse.bacc as bacc
    from concourse.bass_utils import run_bass_kernel_spmd

    nc = bacc.Bacc("TRN2", target_bir_lowering=False, num_devices=1)
    arrays, io = {}, {}
    for name, a in layouts(inputs).items():
        arrays["in_" + name] = a
        io[name] = nc.dram_tensor("in_" + name, a.shape, mybir.dt.from_np(a.dtype), kind="ExternalInput").ap()
    io["out"] = nc.dram_tensor("out_rows", [T, D], F32, kind="ExternalOutput").ap()
    build(nc, io)
    result = run_bass_kernel_spmd(nc, [arrays], core_ids=[0])
    return result.results[0]["out_rows"].reshape(B, S, D)
```
